# Optimizing a Trainium2 kernel written in Bass

```python
import numpy as np
import jax
import jax.numpy as jnp

def _softmax(x, axis=-1):
    return jax.nn.softmax(x, axis=axis)

def _gelu(x):
    return jax.nn.gelu(x, approximate=True)

def _silu(x):
    return jax.nn.silu(x)

def _sigmoid(x):
    return jax.nn.sigmoid(x)

def _layernorm(x, axis=-1, eps=1e-05):
    m = jnp.mean(x, axis=axis, keepdims=True)
    v = jnp.var(x, axis=axis, keepdims=True)
    return (x - m) / jnp.sqrt(v + eps)

def _scatter_add(tgt, idx, src, axis=0):
    return tgt.at[idx].add(src)

def _segment_sum(src, seg, n):
    return jax.ops.segment_sum(src, seg, n)
kernel_name = 'mk_macaron_d2_jaxref_r8_523bbe'

def setup_inputs(seed: int=0):
    np.random.seed(seed)
    _w = jnp.asarray

    def _L0_attn_setup():
        import jax, jax.numpy as jnp
        import numpy as np
        DIM = 256
        N_HEAD = 16
        HEAD_DIM = DIM // N_HEAD
        key = jax.random.key(seed)
        k1, k2, k3 = jax.random.split(key, 3)
        B, N = (8, 512)
        x = jax.random.normal(k1, (B, N, DIM), dtype=jnp.float32)
        w_qkv = jax.random.normal(k2, (3 * DIM, DIM), dtype=jnp.float32) * DIM ** (-0.5)
        w_proj = jax.random.normal(k3, (DIM, DIM), dtype=jnp.float32) * DIM ** (-0.5)
        return {'x': x, 'w_qkv': w_qkv, 'w_proj': w_proj}
    _L0_attn_in = _L0_attn_setup()

    def _L0_ffn_setup():
        import jax, jax.numpy as jnp
        import numpy as np
        B, S, D, H = (8, 512, 256, 640)

        def ternarize_weight(w):
            abs_mean = jnp.maximum(jnp.mean(jnp.abs(w)), 1e-05)
            thr = 0.7 * abs_mean
            one = jnp.ones((), dtype=w.dtype)
            q = jnp.where(w > thr, one, jnp.where(w < -thr, -one, jnp.zeros((), dtype=w.dtype)))
            return w + jax.lax.stop_gradient(q * abs_mean - w)
        key = jax.random.key(seed)
        k1, k2, k3 = jax.random.split(key, 3)
        x = jax.random.normal(k1, (B, S, D), dtype=jnp.float32)
        w_fc = jax.random.normal(k2, (H, D), dtype=jnp.float32) / np.sqrt(D).astype(np.float32)
        w_proj = jax.random.normal(k3, (D, H), dtype=jnp.float32) / np.sqrt(H).astype(np.float32)
        return {'x': x, 'w_fc': w_fc, 'w_proj': w_proj}
    _L0_ffn_in = _L0_ffn_setup()

    def _L1_attn_setup():
        import math
        import jax, jax.numpy as jnp
        import numpy as np
        B, T, D = (2, 256, 256)
        NH, NKV = (32, 8)
        HD = D // NH
        key = jax.random.key(seed)
        kx, kq, kk, kv, ko = jax.random.split(key, 5)
        s = 1.0 / math.sqrt(D)
        return {'x': jax.random.normal(kx, (B, T, D), dtype=jnp.float32), 'wq': jax.random.normal(kq, (D, NH * HD), dtype=jnp.float32) * s, 'wk': jax.random.normal(kk, (D, NKV * HD), dtype=jnp.float32) * s, 'wv': jax.random.normal(kv, (D, NKV * HD), dtype=jnp.float32) * s, 'wo': jax.random.normal(ko, (NH * HD, D), dtype=jnp.float32) * s}
    _L1_attn_in = _L1_attn_setup()

    def _L1_ffn_setup():
        import jax, jax.numpy as jnp
        import numpy as np
        EPS = 1e-08

        def _bit_quant(w):
            scale = jnp.maximum(jnp.mean(jnp.abs(w)), EPS)
            w_ternary = jnp.clip(jnp.round(w / scale), -1.0, 1.0)
            return w + jax.lax.stop_gradient(w_ternary - w)
        key = jax.random.key(seed)
        k = jax.random.split(key, 5)
        emb, dff = (256, 1024)
        B, S = (4, 256)
        x = jax.random.normal(k[0], (B, S, emb), dtype=jnp.float32)
        w1 = jax.random.normal(k[1], (dff, emb), dtype=jnp.float32) * 0.02
        b1 = jax.random.normal(k[2], (dff,), dtype=jnp.float32) * 0.02
        w2 = jax.random.normal(k[3], (emb, dff), dtype=jnp.float32) * 0.02
        b2 = jax.random.normal(k[4], (emb,), dtype=jnp.float32) * 0.02
        return {'x': x, 'w1': w1, 'b1': b1, 'w2': w2, 'b2': b2}
    _L1_ffn_in = _L1_ffn_setup()
    _d = {'L0_attn_x': _L0_attn_in['x'], 'L0_attn_w_qkv': _L0_attn_in['w_qkv'], 'L0_attn_w_proj': _L0_attn_in['w_proj'], 'L0_ffn_w_fc': _L0_ffn_in['w_fc'], 'L0_ffn_w_proj': _L0_ffn_in['w_proj'], 'L1_attn_wq': _L1_attn_in['wq'], 'L1_attn_wk': _L1_attn_in['wk'], 'L1_attn_wv': _L1_attn_in['wv'], 'L1_attn_wo': _L1_attn_in['wo'], 'L1_ffn_w1': _L1_ffn_in['w1'], 'L1_ffn_b1': _L1_ffn_in['b1'], 'L1_ffn_w2': _L1_ffn_in['w2'], 'L1_ffn_b2': _L1_ffn_in['b2']}
    _x0 = _d['L0_attn_x']
    _d['L0_attn_x'] = jax.random.normal(jax.random.fold_in(jax.random.key(seed), 1), (2, 1024, 256), dtype=_x0.dtype)
    del _x0
    return _d

def reference(L0_attn_x, L0_attn_w_qkv, L0_attn_w_proj, L0_ffn_w_fc, L0_ffn_w_proj, L1_attn_wq, L1_attn_wk, L1_attn_wv, L1_attn_wo, L1_ffn_w1, L1_ffn_b1, L1_ffn_w2, L1_ffn_b2):

    def _L0_attn_ref(x, w_qkv, w_proj):
        import jax, jax.numpy as jnp
        import numpy as np
        DIM = 256
        N_HEAD = 16
        HEAD_DIM = DIM // N_HEAD
        B, N, D = x.shape
        H, hd = (N_HEAD, HEAD_DIM)
        qkv = (x @ w_qkv.T).reshape(B, N, 3, H, hd)
        q, k, v = (qkv[:, :, 0], qkv[:, :, 1], qkv[:, :, 2])
        scale = hd ** (-0.5)
        att = jnp.einsum('bnid,bnjd->bnij', q, k) * scale
        att = jax.nn.softmax(att, axis=-1)
        out = jnp.einsum('bnij,bnjd->bnid', att, v)
        out = out.transpose(0, 2, 1, 3).reshape(B, N, D)
        return out @ w_proj.T

    def _L0_ffn_ref(x, w_fc, w_proj):
        import jax, jax.numpy as jnp
        import numpy as np
        B, S, D, H = (8, 512, 256, 640)

        def ternarize_weight(w):
            abs_mean = jnp.maximum(jnp.mean(jnp.abs(w)), 1e-05)
            thr = 0.7 * abs_mean
            one = jnp.ones((), dtype=w.dtype)
            q = jnp.where(w > thr, one, jnp.where(w < -thr, -one, jnp.zeros((), dtype=w.dtype)))
            return w + jax.lax.stop_gradient(q * abs_mean - w)
        h = jnp.einsum('bsd,hd->bsh', x, ternarize_weight(w_fc))
        h = jnp.square(jax.nn.relu(h))
        return jnp.einsum('bsh,dh->bsd', h, ternarize_weight(w_proj))

    def _L1_attn_ref(x, wq, wk, wv, wo):
        import math
        import jax, jax.numpy as jnp
        import numpy as np
        B, T, D = (2, 256, 256)
        NH, NKV = (32, 8)
        HD = D // NH
        bsz, seqlen, _ = x.shape
        q = (x @ wq).reshape(bsz, seqlen, NH, HD).transpose(0, 2, 1, 3)
        k = (x @ wk).reshape(bsz, seqlen, NKV, HD).transpose(0, 2, 1, 3)
        v = (x @ wv).reshape(bsz, seqlen, NKV, HD).transpose(0, 2, 1, 3)
        rep = NH // NKV
        k = jnp.repeat(k, rep, axis=1)
        v = jnp.repeat(v, rep, axis=1)
        att = jnp.einsum('bhqd,bhkd->bhqk', q.astype(jnp.float32), k.astype(jnp.float32)) / math.sqrt(HD)
        mask = jnp.triu(jnp.ones((seqlen, seqlen), dtype=bool), k=1)
        att = jnp.where(mask[None, None, :, :], -jnp.inf, att)
        att = jax.nn.softmax(att, axis=-1)
        y = jnp.einsum('bhqk,bhkd->bhqd', att, v.astype(jnp.float32)).astype(q.dtype)
        y = y.transpose(0, 2, 1, 3).reshape(bsz, seqlen, NH * HD)
        return y @ wo

    def _L1_ffn_ref(x, w1, b1, w2, b2):
        import jax, jax.numpy as jnp
        import numpy as np
        EPS = 1e-08

        def _bit_quant(w):
            scale = jnp.maximum(jnp.mean(jnp.abs(w)), EPS)
            w_ternary = jnp.clip(jnp.round(w / scale), -1.0, 1.0)
            return w + jax.lax.stop_gradient(w_ternary - w)
        w1q = _bit_quant(w1)
        w2q = _bit_quant(w2)
        h = jnp.einsum('bsd,fd->bsf', x, w1q) + b1
        h = jax.nn.gelu(h, approximate=False)
        return jnp.einsum('bsf,df->bsd', h, w2q) + b2
    x = L0_attn_x
    x = x + 0.5 * _L0_ffn_ref(_layernorm(x, axis=-1), L0_ffn_w_fc, L0_ffn_w_proj)
    x = x + _L0_attn_ref(_layernorm(x, axis=-1), L0_attn_w_qkv, L0_attn_w_proj)
    x = x + 0.5 * _L0_ffn_ref(_layernorm(x, axis=-1), L0_ffn_w_fc, L0_ffn_w_proj)
    x = x + 0.5 * _L1_ffn_ref(_layernorm(x, axis=-1), L1_ffn_w1, L1_ffn_b1, L1_ffn_w2, L1_ffn_b2)
    x = x + _L1_attn_ref(_layernorm(x, axis=-1), L1_attn_wq, L1_attn_wk, L1_attn_wv, L1_attn_wo)
    x = x + 0.5 * _L1_ffn_ref(_layernorm(x, axis=-1), L1_ffn_w1, L1_ffn_b1, L1_ffn_w2, L1_ffn_b2)
    return x

_drawn_inputs = setup_inputs


def setup_inputs(seed=0):
    import zlib

    import numpy as np

    out = dict(_drawn_inputs(seed))
    spreads = {}
    factors = {'L1_attn_wq': 8.0,
     'L1_attn_wk': 8.0,
     'L1_attn_wv': 8.0,
     'L1_attn_wo': 8.0,
     'L1_ffn_b1': 8.0,
     'L1_ffn_b2': 200.0}
    for name, (base, spread) in spreads.items():
        noise = np.random.default_rng([zlib.crc32(name.encode()), seed]).standard_normal(out[name].shape)
        drawn = base * np.exp(spread * noise) if base else spread * noise
        out[name] = jnp.asarray(drawn.astype(out[name].dtype))
    for name, factor in factors.items():
        out[name] = (out[name] * factor).astype(out[name].dtype)
    return out
```

```python
from contextlib import ExitStack

import concourse.bass as bass
from concourse import mybir

F32 = mybir.dt.float32
F16 = mybir.dt.float16
BF16 = mybir.dt.bfloat16
ALU = mybir.AluOpType
ACT = mybir.ActivationFunctionType
AX_X = mybir.AxisListType.X

P = 128
D = 256
DC = D // P
TOK = 2048
NT = TOK // P
SEQ = 1024
ST_ = SEQ // P
BATCH = TOK // SEQ
GT = 4
GROUPS = NT // GT
GTOK = GT * P
BANK = 512
HPG = 4
WSCALE = 64.0
RSCALE = 0.25
NEG = -1.0e30
EPS = 1e-5

HID = (640, 1024)
BIG = 60000.0

HD0, HEADS0, NEAR = 16, 16, 8
BLOCKS = P // NEAR
MIXES = NT // 2
CHUNK = 8


class Att:

    def __init__(self, heads, kv_heads, causal):
        self.heads, self.kv, self.causal = heads, kv_heads, causal
        self.hd = D // heads
        self.row = 64 if self.hd == 16 else 32
        self.step = self.row if causal else 2 * self.row
        self.qkw = HPG * self.row
        self.tiles = self.qkw // P
        self.groups = heads // HPG
        self.iters = BATCH * self.groups
        self.vh = HPG if kv_heads == heads else 1
        self.scale = float(self.hd) ** -0.5
        self.kvw = kv_heads * self.hd
        self.cols = D + 2 * self.kvw
        self.sets = [(h, k) for h in range(2) for k in range(GT * (h + 1) if causal else ST_)]
        self.maxes = []
        for qt in range(ST_):
            n = min(HPG, 2 * BANK // self.width(qt))
            self.maxes += [(qt, list(range(h, h + n))) for h in range(0, HPG, n)]
        self.lead = 2 + len(self.maxes) + 1
        self.uses = self.lead + 1
        assert self.uses % 2 == 0

    def at(self, g, t):
        if self.causal:
            return g * (GT * 1024) + t * 1024
        return g * (GT * 1024) + (t // 2 * 2048 + t % 2 * self.row)

    def v_at(self, g, t):
        if self.causal:
            return g * (GT * self.kvw) + t * self.kvw
        return g * (GT * 2 * D) + (t // 2 * 4 * D + t % 2 * 2 * self.hd)

    def keys(self, qt):
        return P * (qt + 1) if self.causal else SEQ

    def width(self, qt):
        w = self.keys(qt)
        return w if BANK % w == 0 else -(-w // BANK) * BANK

    def first(self, s):
        h, k = self.sets[s]
        return max(0, (k - GT * h) * P) if self.causal else 0

    def diagonal(self, s):
        h, k = self.sets[s]
        return self.causal and k >= GT * h

    def quota(self, s):
        n, last = len(self.maxes), len(self.sets) - 1
        return max(0, min(n, -(-n * (s - 1) // (last - 2))))

    def half_ends(self, s):
        return s + 1 == len(self.sets) or self.sets[s + 1][0] != self.sets[s][0]


ATTS = (Att(HEADS0, HEADS0, False), Att(32, 8, True))


def before(j, n, ring):
    if j >= ring:
        return ring
    last = max(k for k in range(n) if k % ring == j % ring)
    return j + n - last


class Phase:

    def __init__(self, kind, layer, at):
        self.kind, self.layer, self.at = kind, layer, at
        self.att = ATTS[layer]
        self.nb = HID[layer] // P
        n, a = {}, self.att
        if kind in ("ffn", "qkv"):
            n.update(stats_done=GROUPS, var_ready=GROUPS, eps_done=GROUPS, rstd_ready=GROUPS, xn_ready=GROUPS,
                     xt_ready=DC * GROUPS, xh_ready=DC * GROUPS, xl_ready=DC * GROUPS)
        if kind == "ffn":
            for name in ("h_ready", "t_ready", "uh_ready", "ul_ready", "down_done"):
                n[name] = self.nb * GROUPS
            n["resid"] = GROUPS
            n["u_done" if layer == 0 else "bias_added"] = self.nb * GROUPS if layer == 0 else GROUPS
        if kind == "qkv":
            n.update(qkv_ready=NT, hi_ready=NT, qkv_free=NT, dup_done=NT)
            if a.vh == 1:
                n["k_dup"] = NT
        if kind == "mix":
            w = MIXES
            n.update(a_full=4 * w, q_turned=w, k_turned=w, k_turned_2=w, v_turned=w, v_ready=w, b_full=5 * w, maxed=4 * w,
                     m_ready=w, st_ready=4 * w, p_ready=4 * w, pv_done=4 * w, o_out=2 * w, ot_full=2 * w,
                     rd_done=2 * w, on_ready=2 * w, on_turned=2 * w, oh_ready=2 * w, ol_ready=2 * w)
        if kind == "out":
            n.update(y_ready=GROUPS, resid=GROUPS)
        if kind == "att":
            i, s = a.iters, len(a.sets)
            n.update(slot_full=a.lead + (i - 1) * a.uses + 1, maxed=len(a.maxes) * i, copied=3 * i,
                     mh_done=i, m_written=i, st_ready=HPG * s * i, p_ready=HPG * s * i, pv_done=s * i,
                     o_out=2 * i, v_ready=i, rd_done=i, on_ready=i, ah_done=i, ao_ready=i)
        if kind == "proj":
            n.update(at_ready=2 * GROUPS, ah_copied=GROUPS, al_copied=GROUPS, y_ready=GROUPS, resid=GROUPS)
        self.n = n
        self.after = {**at, **{k: at.get(k, 0) + v for k, v in n.items()}}

    def __getitem__(self, name):
        return self.at.get(name, 0)


CREDIT = {"down_done": 8, "t_ready": 8, "qkv_free": 2, "pv_done": 2, "p_ready": 4}


def plan():
    phases, at = [], dict(CREDIT)
    for kind, layer in [("ffn", 0), ("qkv", 0), ("mix", 0), ("out", 0), ("ffn", 0),
                        ("ffn", 1), ("qkv", 1), ("att", 1), ("proj", 1), ("ffn", 1)]:
        phases.append(Phase(kind, layer, at))
        at = phases[-1].after
    return phases


def macaron_kernel(nc, x, apart, fc0, down0, fc1, down1, b1, b2, qkv0, wo0, qkv1, wo1, out):
    phases = plan()

    with ExitStack() as ctx:
        def sb(name, cols, dt):
            return ctx.enter_context(nc.sbuf_tensor(name, [P, cols], dt))

        def ps(name, cols):
            return ctx.enter_context(nc.psum_tensor(name, [P, cols], F32))

        def sem(name):
            return ctx.enter_context(nc.semaphore(name))

        def view(t, at, *dims):
            return bass.AP(t, at, [[t.shape[1], P], *[list(d) for d in dims]])

        def view16(t, at, *dims):
            full = t[:, :].bitcast(F16)
            return bass.AP(full.tensor, at, [[t.shape[1] * 2, P], *[list(d) for d in dims]])

        X = sb("X", NT * D, F32)
        QA = sb("QA", NT * 1024, F16)
        KA = sb("KA", NT * 1024, F16)
        VS = sb("VS", NT * D + P // 4, F32)
        VG = [sb(f"VG{k}", ST_ * HPG * 32, F32) for k in range(2)]
        QT1 = sb("QT1", 2 * SEQ, F16)
        QT2 = [sb(f"QT2{k}", 2 * SEQ, F16) for k in range(2)]
        KT = [sb(f"KT{k}", HPG * SEQ, F16) for k in range(2)]
        AH = sb("AH", NT * D, F16)
        AL = sb("AL", NT * D, F16)
        OT = sb("OT", 2 * BANK, F32)
        ON = sb("ON", ST_ * HPG * 16, F32)
        RD = sb("RD", ST_ * HPG, F32)
        NM = sb("NM", ST_ * HPG, F32)
        work = sb("work", 5120, F32)
        PR = [work[:, k * HPG * BANK:(k + 1) * HPG * BANK] for k in range(2)]
        XN = work[:, 0:GT * D]
        XH = work[:, 1024:1536].bitcast(F16)
        XL = work[:, 1536:2048].bitcast(F16)
        T = [work[:, 2048 + k * BANK:2048 + (k + 1) * BANK] for k in range(2)]
        U = [work[:, 3072 + k * BANK:3072 + (k + 1) * BANK] for k in range(2)]
        UH = [work[:, 4096 + k * 256:4096 + (k + 1) * 256].bitcast(F16) for k in range(2)]
        UL = [work[:, 4608 + k * 256:4608 + (k + 1) * 256].bitcast(F16) for k in range(2)]
        up = [sb(f"up_w{k}", DC * HID[k], F16) for k in range(2)]
        down = [sb(f"down_w{k}", HID[k] // P * D, F16) for k in range(2)]
        wqkv = [[sb(f"qkv_w{k}{p}", DC * ATTS[k].cols, F16) for p in "hl"] for k in range(2)]
        wo = [[sb(f"wo_w{k}{p}", DC * D, F16) for p in "hl"] for k in range(2)]
        b1s = sb("b1s", HID[1] // P, F32)
        b2h = sb("b2h", D, F32)
        ident = sb("ident", P, F32)
        ident16 = sb("ident16", P, F16)
        identb = sb("identb", P, BF16)
        maskb = sb("maskb", P, BF16)
        maskt = sb("maskt", P, BF16)
        ones = sb("ones", P, F32)
        sums = sb("sums", 4, F32)
        means = sb("means", 4, F32)
        lim = sb("lim", 8, F32)
        sc = sb("sc", 2, F32)
        bn = sb("bn", GT * 6, F32)
        mv = sb("mv", GT * 2, F32)
        var = sb("var", GT, F32)
        rstd = sb("rstd", GT, F32)
        mhalf = sb("mhalf", GT, F32)
        eps = sb("eps", GT, F32)
        aparts = sb("aparts", 2 * NEAR, F32)
        MT = [sb(f"MT{k}", P, BF16) for k in range(2)]
        two = sb("two", HD0, F16)

        A = ps("A", 2 * BANK)
        B = ps("B", 2 * BANK)
        C = ps("C", 4 * BANK)
        slots = [A, B]

        s = {k: sem(k) for k in sorted({k for ph in phases for k in ph.n})}
        gate, x_in, w_in, const_ready, const_step, sums_ready, tot_ready = (sem(k) for k in (
            "gate", "x_in", "w_in", "const_ready", "const_step", "sums_ready", "tot_ready"))
        setup_step, high_done, w_ready, pad_zeroed, pad_ready, v_pad, k_zeroed, out_done = (sem(k) for k in (
            "setup_step", "high_done", "w_ready", "pad_zeroed", "pad_ready", "v_pad", "k_zeroed", "out_done"))

        off, quant = 0, []
        for w, dst in ((fc0, up[0]), (down0, down[0]), (fc1, up[1]), (down1, down[1])):
            n = w.shape[0] // P * w.shape[1]
            quant.append((w, QA[:, :].bitcast(F32)[:, off:off + n], dst))
            off += n
        off, split = 0, []
        for w, dst in ((qkv0, wqkv[0]), (wo0, wo[0]), (qkv1, wqkv[1]), (wo1, wo[1])):
            n = DC * w.shape[1]
            split.append((w, KA[:, :].bitcast(F32)[:, off:off + n], dst))
            off += n

        block = ctx.enter_context(nc.Block())

        @block.sync
        def _(sp):
            def tiles(dram, g):
                return dram.rearrange("(t p) d -> p t d", p=P)[:, g * GT:(g + 1) * GT, :]

            for w, dst, _ in quant + split:
                sp.dma_start(dst.rearrange("p (c n) -> p c n", c=w.shape[0] // P),
                             w.rearrange("(c p) n -> p c n", p=P)).then_inc(w_in, 16)
            sp.dma_start(b1s[:, :], b1).then_inc(w_in, 16)
            sp.dma_start(aparts[:, :], apart).then_inc(w_in, 16)
            sp.dma_start(b2h[:, :], b2.broadcast_to([P, D])).then_inc(w_in, 16)
            for g in range(GROUPS):
                sp.dma_start(view(X, g * GT * D, (D, GT), (1, D)), tiles(x, g)).then_inc(x_in, 16)
            for g in range(GROUPS):
                sp.wait_ge(s["resid"], phases[-1]["resid"] + g + 1)
                sp.dma_start(tiles(out, g), view(X, g * GT * D, (D, GT), (1, D))).then_inc(out_done, 16)
            sp.wait_ge(out_done, 16 * GROUPS)

        @block.tensor
        def _(pe):
            def transposes(k, g):
                pe.wait_ge(s["xn_ready"], k["xn_ready"] + g + 1)
                for c in range(DC):
                    for t in range(GT):
                        mm = pe.transpose(A[:, c * BANK + t * P:c * BANK + (t + 1) * P],
                                          XN[:, t * D + c * P:t * D + (c + 1) * P], ident[:, :])
                    mm.then_inc(s["xt_ready"], 1)

            def ffn(k):
                W, V, nb, hid = up[k.layer], down[k.layer], k.nb, HID[k.layer]

                def hidden(g, j):
                    pe.wait_ge(s["t_ready"], k["t_ready"] + g * nb + j - before(j, nb, 4) + 1)
                    for c in range(DC):
                        if j == 0:
                            pe.wait_ge(s["xl_ready"], k["xl_ready"] + g * DC + c + 1)
                        for n, part in enumerate((XH, XL)):
                            mm = pe.matmul(C[:, j % 4 * BANK:(j % 4 + 1) * BANK],
                                           W[:, c * hid + j * P:c * hid + (j + 1) * P],
                                           part[:, c * GTOK:(c + 1) * GTOK],
                                           start=(c == 0 and n == 0), stop=(c == DC - 1 and n == 1))
                    mm.then_inc(s["h_ready"], 1)

                def to_model(g, j):
                    if j == 0:
                        pe.wait_ge(s["resid"], k["resid"] + g)
                    pe.wait_ge(s["ul_ready"], k["ul_ready"] + g * nb + j + 1)
                    for t in range(GT):
                        for n, part in enumerate((UH[j % 2], UL[j % 2])):
                            mm = pe.matmul(B[:, t * D:(t + 1) * D], part[:, t * P:(t + 1) * P],
                                           V[:, j * D:(j + 1) * D],
                                           start=(j == 0 and n == 0 and t % 2 == 0),
                                           stop=(j == nb - 1 and n == 1), skip_group_check=True)
                    mm.then_inc(s["down_done"], 1)

                def group(g, last):
                    hidden(g, 0)
                    for j in range(nb):
                        if j + 1 < nb:
                            hidden(g, j + 1)
                            if j + 2 == nb and not last:
                                transposes(k, g + 1)
                        to_model(g, j)

                transposes(k, 0)
                with pe.Fori(0, GROUPS - 1) as g:
                    group(g, False)
                group(GROUPS - 1, True)

            def qkv(k):
                a = k.att
                Wh, Wl = wqkv[k.layer]

                def group(g, last):
                    for t in range(GT):
                        pe.wait_ge(s["qkv_free"], k["qkv_free"] + g * GT + t - 1)
                        if t == 0:
                            pe.wait_ge(s["xl_ready"], k["xl_ready"] + g * DC + DC)
                        for lo in range(0, a.cols, BANK):
                            w, o = min(BANK, a.cols - lo), t % 2 * 2 * BANK + lo
                            for c in range(DC):
                                for n, (p, q) in enumerate(((XH, Wh), (XH, Wl), (XL, Wh))):
                                    mm = pe.matmul(C[:, o:o + w], p[:, c * GTOK + t * P:c * GTOK + (t + 1) * P],
                                                   q[:, c * a.cols + lo:c * a.cols + lo + w],
                                                   start=(c == 0 and n == 0), stop=(c == DC - 1 and n == 2))
                        mm.then_inc(s["qkv_ready"], 1)
                    if not last:
                        transposes(k, g + 1)

                transposes(k, 0)
                with pe.Fori(0, GROUPS - 1) as g:
                    group(g, False)
                group(GROUPS - 1, True)

            def att(k):
                a = k.att
                nset, nmax = len(a.sets), len(a.maxes)

                def slot(n, i):
                    return slots[(n if i is None else a.lead + n) % 2]

                def slots_free(i):
                    pe.wait_ge(s["copied"], k["copied"] + i * 3 + 3)
                    pe.wait_ge(s["on_ready"], k["on_ready"] + i)

                def turn(src, i, dst):
                    b = i // a.groups
                    at = b * (ST_ * 1024) + (i % a.groups) * a.qkw
                    at = at if isinstance(at, int) else pe.snap(at)
                    for p in range(a.tiles):
                        for t in range(ST_):
                            mm = pe.transpose(dst[:, :].bitcast(F16)[:, p * SEQ + t * P:p * SEQ + (t + 1) * P],
                                              view(src, at + (t * 1024 + p * P), (1, P)), ident16[:, :])
                    mm.then_inc(s["slot_full"], 1)

                def maximum(i, par, m, dst):
                    qt, heads = a.maxes[m]
                    if m == 0:
                        pe.wait_ge(s["copied"], k["copied"] + i * 3 + 2)
                    elif m > 1:
                        pe.wait_ge(s["maxed"], k["maxed"] + i * nmax + m - 1)
                    keys, begun = a.keys(qt), []
                    for w in range(len(heads)):
                        o = w * a.width(qt) + keys - P
                        pe.matmul(dst[:, o:o + P], identb[:, :], maskb[:, :], start=o // BANK not in begun,
                                  stop=False, skip_group_check=True)
                        begun.append(o // BANK)
                    for w, h in enumerate(heads):
                        for lo in range(0, keys, BANK):
                            o, c = w * a.width(qt) + lo, min(BANK, keys - lo)
                            mm = pe.matmul(dst[:, o:o + c], QT1[:, qt * P:(qt + 1) * P],
                                           KT[par][:, h * SEQ + lo:h * SEQ + lo + c], start=o // BANK not in begun,
                                           stop=True, skip_group_check=True)
                            begun.append(o // BANK)
                    mm.then_inc(s["slot_full"], 1)

                def score(i, par, x, h):
                    st = x * HPG + h
                    pe.wait_ge(s["p_ready"], k["p_ready"] + i * (HPG * nset) + st - before(st, HPG * nset, 3) + 1)
                    if st == 0:
                        pe.wait_ge(s["copied"], k["copied"] + i * 3 + 3)
                    qh, kt = a.sets[x]
                    lo, b = a.first(x), st % 3
                    diagonal = a.diagonal(x)
                    if diagonal:
                        pe.matmul(C[:, b * BANK + lo:b * BANK + lo + P], identb[:, :], maskt[:, :],
                                  start=True, stop=False, skip_group_check=True)
                    pe.matmul(C[:, b * BANK + lo:(b + 1) * BANK], KT[par][:, h * SEQ + kt * P:h * SEQ + (kt + 1) * P],
                              QT2[par][:, qh * BANK + lo:(qh + 1) * BANK],
                              start=not diagonal, stop=True, skip_group_check=True).then_inc(s["st_ready"], 1)

                def values(i, par, x):
                    qh, kt = a.sets[x]
                    lo = a.first(x)
                    if x == 0:
                        pe.wait_ge(s["v_ready"], k["v_ready"] + i + 1)
                    if kt == 0:
                        pe.wait_ge(s["o_out"], k["o_out"] + i * 2 + qh)
                    pe.wait_ge(s["p_ready"], k["p_ready"] + i * (HPG * nset) + HPG * (x + 1))
                    for h in range(HPG):
                        v = (kt * a.vh + h % a.vh) * 32
                        mm = pe.matmul(C[32 * h:32 * h + 32, 3 * BANK + lo:4 * BANK], VG[par][:, v:v + 32],
                                       PR[x % 2][:, h * BANK + lo:(h + 1) * BANK],
                                       start=(kt == 0), stop=a.half_ends(x), skip_group_check=True,
                                       tile_position=(0, 32 * h))
                    mm.then_inc(s["pv_done"], 1)

                def half(i, par, more):
                    slots_free(i)
                    m = 0
                    for x in range(nset):
                        for h in range(HPG):
                            score(i, par, x, h)
                            if more and x == 0 and h == 1:
                                turn(QA, i + 1, slot(0, i))
                                turn(KA, i + 1, slot(1, i))
                            goal = a.quota(x) if h == HPG - 1 else (m + a.quota(x)) // 2 if h == 1 else m
                            while more and m < goal:
                                maximum(i + 1, 1 - par, m, slot(2 + m, i))
                                m += 1
                        if x:
                            values(i, par, x - 1)
                    values(i, par, nset - 1)
                    if more:
                        pe.wait_ge(s["m_written"], k["m_written"] + i + 2)
                    pe.wait_ge(s["o_out"], k["o_out"] + i * 2 + 2)
                    dst = slot(a.uses - 2 if more else 0, i)
                    for t in range(ST_):
                        mm = pe.transpose(dst[:, t * P:(t + 1) * P], OT[:, t * P:(t + 1) * P], ident[:, :])
                    mm.then_inc(s["slot_full"], 1)
                    if more:
                        turn(QA, i + 1, slot(a.uses - 1, i))

                pe.wait_ge(s["qkv_free"], k["qkv_free"])
                pe.wait_ge(s["dup_done"], k["dup_done"])
                turn(QA, 0, slot(0, None))
                turn(KA, 0, slot(1, None))
                for m in range(nmax):
                    maximum(0, 0, m, slot(2 + m, None))
                pe.wait_ge(s["m_written"], k["m_written"] + 1)
                turn(QA, 0, slot(a.lead - 1, None))
                with pe.Fori(0, a.iters // 2 - 1) as r:
                    i = pe.snap(r * 2)
                    half(i, 0, True)
                    half(i + 1, 1, True)
                half(a.iters - 2, 0, True)
                half(a.iters - 1, 1, False)

            def mix(k):
                def turn(seen, src, w, step):
                    at = w * (step * HEADS0)
                    for h in range(HEADS0):
                        mm = pe.transpose(A[:, :].bitcast(F16)[:, h * P:(h + 1) * P],
                                          seen(src, at + h * step, (1, P)), ident16[:, :])
                    mm.then_inc(s["a_full"], 1)

                def k_out(w):
                    pe.wait_ge(s["k_turned"], k["k_turned"] + w + 1)
                    pe.wait_ge(s["k_turned_2"], k["k_turned_2"] + w + 1)

                def turn_q(w):
                    turn(view, QA, w, P)

                def turn_k(w):
                    pe.wait_ge(s["q_turned"], k["q_turned"] + w + 1)
                    turn(view, KA, w, P)

                def turn_v(w):
                    k_out(w)
                    turn(view16, VS, w, P // 2)

                def blocks_v(w):
                    pe.wait_ge(s["v_turned"], k["v_turned"] + w + 1)
                    for u in range(2):
                        for r in range(BLOCKS):
                            mm = pe.matmul(A[:, u * BANK + r * HD0:u * BANK + (r + 1) * HD0],
                                           QT1[32 * u:32 * u + 32, r * P:(r + 1) * P], two[32 * u:32 * u + 32, :],
                                           start=(r == 0), stop=True, skip_group_check=True)
                    mm.then_inc(s["a_full"], 1)

                def maximum(w, par, c):
                    if c == 0:
                        k_out(w)
                        pe.wait_ge(s["m_ready"], k["m_ready"] + w)
                    else:
                        pe.wait_ge(s["maxed"], k["maxed"] + w * 4 + c)
                    u = c // 2
                    for n in range(CHUNK):
                        r = c % 2 * CHUNK + n
                        mm = pe.matmul(B[:, n * P:(n + 1) * P], QT2[par][:, r * P:(r + 1) * P],
                                       KT[par][:, (u * BLOCKS + r) * P:(u * BLOCKS + r + 1) * P],
                                       start=(n % 4 == 0), stop=True, skip_group_check=True)
                    mm.then_inc(s["b_full"], 1)

                def turn_m(w):
                    pe.wait_ge(s["maxed"], k["maxed"] + w * 4 + 4)
                    pe.transpose(B[0:2 * BLOCKS, 0:P], NM[:, :], ident[:, :]).then_inc(s["b_full"], 1)

                def score(w, par, c):
                    if c == 0:
                        pe.wait_ge(s["m_ready"], k["m_ready"] + w + 1)
                    pe.wait_ge(s["p_ready"], k["p_ready"] + w * 4 + c)
                    u = c // 2
                    for n in range(CHUNK):
                        r = u * BLOCKS + c % 2 * CHUNK + n
                        pe.matmul(C[:, n * P:(n + 1) * P], view(identb, r, (0, P)), MT[par][:, :], start=(n % 4 == 0), stop=False, skip_group_check=True)
                    for n in range(CHUNK):
                        r = c % 2 * CHUNK + n
                        mm = pe.matmul(C[:, n * P:(n + 1) * P],
                                       KT[par][:, (u * BLOCKS + r) * P:(u * BLOCKS + r + 1) * P],
                                       QT2[par][:, r * P:(r + 1) * P],
                                       start=False, stop=True, skip_group_check=True)
                    mm.then_inc(s["st_ready"], 1)

                def values(w, par, c):
                    if c == 0:
                        pe.wait_ge(s["v_ready"], k["v_ready"] + w + 1)
                    if c % 2 == 0:
                        pe.wait_ge(s["o_out"], k["o_out"] + w * 2 + c // 2)
                    pe.wait_ge(s["p_ready"], k["p_ready"] + w * 4 + c + 1)
                    for n in range(CHUNK):
                        q, o = n % 4, 2 * BANK + (c % 2 * 2 + n // 4) * P
                        v = (c * CHUNK + n) * 32
                        mm = pe.matmul(C[32 * q:32 * q + 32, o:o + P], VG[par][:, v:v + 32],
                                       PR[c % 2][:, n * P:(n + 1) * P], start=(c % 2 == 0 and n < 4), stop=True,
                                       skip_group_check=True, tile_position=(0, 32 * q))
                    mm.then_inc(s["pv_done"], 1)

                def turn_sums(w, u):
                    pe.wait_ge(s["o_out"], k["o_out"] + w * 2 + u + 1)
                    pe.wait_ge(s["ol_ready"], k["ol_ready"] + w * 2 + u)
                    for n in range(4):
                        mm = pe.transpose(C[:, 3 * BANK + n * P:3 * BANK + (n + 1) * P],
                                          OT[:, u * BANK + n * P:u * BANK + (n + 1) * P], ident[:, :])
                    mm.then_inc(s["ot_full"], 1)

                def turn_out(w, u):
                    pe.wait_ge(s["on_ready"], k["on_ready"] + w * 2 + u + 1)
                    for c in range(DC):
                        mm = pe.transpose(C[:, 3 * BANK + c * P:3 * BANK + (c + 1) * P],
                                          ON[:, u * D + c * P:u * D + (c + 1) * P], ident[:, :])
                    mm.then_inc(s["on_turned"], 1)

                def half(w, par, more):
                    n = w + 1
                    score(w, par, 0)
                    if more:
                        turn_q(n)
                        turn_k(n)
                    values(w, par, 0)
                    score(w, par, 1)
                    if more:
                        turn_v(n)
                        blocks_v(n)
                    values(w, par, 1)
                    score(w, par, 2)
                    if more:
                        maximum(n, 1 - par, 0)
                        maximum(n, 1 - par, 1)
                    turn_sums(w, 0)
                    values(w, par, 2)
                    score(w, par, 3)
                    if more:
                        maximum(n, 1 - par, 2)
                    turn_out(w, 0)
                    values(w, par, 3)
                    if more:
                        maximum(n, 1 - par, 3)
                    turn_sums(w, 1)
                    if more:
                        turn_m(n)
                    turn_out(w, 1)

                pe.wait_ge(s["qkv_free"], k["qkv_free"])
                pe.wait_ge(s["dup_done"], k["dup_done"])
                turn_q(0)
                turn_k(0)
                turn_v(0)
                blocks_v(0)
                for c in range(4):
                    maximum(0, 0, c)
                turn_m(0)
                with pe.Fori(0, MIXES // 2 - 1) as r:
                    w = pe.snap(r * 2)
                    half(w, 0, True)
                    half(w + 1, 1, True)
                half(MIXES - 2, 0, True)
                half(MIXES - 1, 1, False)

            def outward(k):
                Wh, Wl = wo[k.layer]
                pe.wait_ge(s["ol_ready"], k["ol_ready"])
                pe.wait_ge(s["oh_ready"], k["oh_ready"])
                with pe.Fori(0, GROUPS) as g:
                    pe.wait_ge(s["resid"], k["resid"] + g)
                    for t in range(GT):
                        for c in range(DC):
                            for n, (p, q) in enumerate(((AH, Wh), (AH, Wl), (AL, Wh))):
                                mm = pe.matmul(B[:, t * D:(t + 1) * D], view(p, g * GTOK + (c * TOK + t * P), (1, P)),
                                               q[:, c * D:(c + 1) * D], start=(c == 0 and n == 0 and t % 2 == 0),
                                               stop=(c == DC - 1 and n == 2), skip_group_check=True)
                    mm.then_inc(s["y_ready"], 1)

            def proj(k):
                Wh, Wl = wo[k.layer]
                pe.wait_ge(s["ao_ready"], k["ao_ready"])
                with pe.Fori(0, GROUPS) as g:
                    for part, src in enumerate((AH, AL)):
                        for c in range(DC):
                            for t in range(GT):
                                o = part * 2 * BANK + c * GTOK + t * P
                                mm = pe.transpose(A[:, :].bitcast(F16)[:, o:o + P],
                                                  view(src, g * (GT * D) + (t * D + c * P), (1, P)), ident16[:, :])
                        mm.then_inc(s["at_ready"], 1)
                    pe.wait_ge(s["ah_copied"], k["ah_copied"] + g + 1)
                    pe.wait_ge(s["al_copied"], k["al_copied"] + g + 1)
                    pe.wait_ge(s["resid"], k["resid"] + g)
                    for t in range(GT):
                        for c in range(DC):
                            for n, (p, q) in enumerate(((XH, Wh), (XH, Wl), (XL, Wh))):
                                mm = pe.matmul(B[:, t * D:(t + 1) * D], p[:, c * GTOK + t * P:c * GTOK + (t + 1) * P],
                                               q[:, c * D:(c + 1) * D], start=(c == 0 and n == 0 and t % 2 == 0),
                                               stop=(c == DC - 1 and n == 2), skip_group_check=True)
                    mm.then_inc(s["y_ready"], 1)

            pe.wait_ge(const_ready, 8)
            pe.wait_ge(sums_ready, 1)
            pe.matmul(C[:, 0:4], ones[:, :], sums[:, :], start=True, stop=True).then_inc(tot_ready, 1)
            pe.wait_ge(w_ready, 1)
            for k in phases:
                {"ffn": ffn, "qkv": qkv, "mix": mix, "out": outward, "att": att, "proj": proj}[k.kind](k)

        @block.scalar
        def _(act):
            def split_high(k, g):
                for c in range(DC):
                    act.wait_ge(s["xt_ready"], k["xt_ready"] + g * DC + c + 1)
                    nc.scalar.activation(XH[:, c * GTOK:(c + 1) * GTOK], A[:, c * BANK:(c + 1) * BANK],
                                         ACT.Copy).then_inc(s["xh_ready"], 1)

            def ffn(k):
                def group(g, last):
                    for j in range(k.nb):
                        n = g * k.nb + j
                        act.wait_ge(s["h_ready"], k["h_ready"] + n + 1)
                        act.wait_ge(s["down_done"], k["down_done"] + n - before(j, k.nb, 2) + 1)
                        src = C[:, j % 4 * BANK:(j % 4 + 1) * BANK]
                        if k.layer == 0:
                            nc.scalar.activation(T[j % 2], src, ACT.Relu, scale=RSCALE).then_inc(s["t_ready"], 1)
                        else:
                            nc.scalar.activation(T[j % 2], src, ACT.Gelu, bias=b1s[:, j:j + 1]).then_inc(s["t_ready"], 1)
                        act.wait_ge(s["t_ready"], k["t_ready"] + n + 1)
                        nc.scalar.activation(UH[j % 2], T[j % 2], ACT.Square if k.layer == 0 else ACT.Copy)\
                            .then_inc(s["uh_ready"], 1)
                    if not last:
                        split_high(k, g + 1)

                nc.scalar.preload_act_table(ACT.Exp if k.layer == 0 else ACT.Gelu)
                split_high(k, 0)
                with act.Fori(0, GROUPS - 1) as g:
                    group(g, False)
                group(GROUPS - 1, True)

            def qkv(k):
                a = k.att

                def group(g, last):
                    for t in range(GT):
                        act.wait_ge(s["qkv_ready"], k["qkv_ready"] + g * GT + t + 1)
                        o = t % 2 * 2 * BANK
                        at, row = a.at(g, t), a.step * (HPG // a.vh)
                        nc.scalar.activation(view(QA, at, (a.step, a.heads), (1, a.hd)),
                                             view(C, o, (a.hd, a.heads), (1, a.hd)), ACT.Copy, scale=1 / WSCALE)
                        nc.scalar.activation(view(KA, at, (row, a.kv), (1, a.hd)),
                                             view(C, o + D, (a.hd, a.kv), (1, a.hd)), ACT.Copy, scale=1 / WSCALE)
                        if k.layer == 0:
                            dst = view16(VS, a.v_at(g, t), (4 * a.hd, a.kv), (1, a.hd))
                        else:
                            dst = view(VS, a.v_at(g, t), (a.hd, a.kv), (1, a.hd))
                        nc.scalar.activation(dst, view(C, o + D + a.kvw, (a.hd, a.kv), (1, a.hd)), ACT.Copy,
                                             scale=1 / WSCALE).then_inc(s["hi_ready"], 1)
                    if not last:
                        split_high(k, g + 1)

                split_high(k, 0)
                act.wait_ge(pad_ready, 2 + k.layer)
                with act.Fori(0, GROUPS - 1) as g:
                    group(g, False)
                group(GROUPS - 1, True)

            def att(k):
                a = k.att
                nset = len(a.sets)

                def copy_out(n, i, dst):
                    u = n if i is None else a.lead + n
                    act.wait_ge(s["slot_full"], k["slot_full"] + (0 if i is None else i * a.uses) + u + 1)
                    nc.scalar.activation(dst[:, 0:SEQ], slots[u % 2][:, :].bitcast(F16)[:, 0:SEQ],
                                         ACT.Copy).then_inc(s["copied"], 1)

                def copy_k(n, i, par):
                    u = n if i is None else a.lead + n
                    act.wait_ge(s["slot_full"], k["slot_full"] + (0 if i is None else i * a.uses) + u + 1)
                    for h in range(HPG):
                        r = slice(h * a.row, (h + 1) * a.row)
                        op = nc.scalar.activation(KT[par][r, h * SEQ:(h + 1) * SEQ],
                                                  slots[u % 2][r, :].bitcast(F16)[:, 0:SEQ], ACT.Copy)
                    op.then_inc(s["copied"], 1)

                def drain(i, x):
                    qh = a.sets[x][0]
                    act.wait_ge(s["pv_done"], k["pv_done"] + i * nset + x + 1)
                    if qh == 0:
                        act.wait_ge(s["slot_full"], k["slot_full"] + a.lead + i * a.uses)
                    nc.scalar.activation(OT[:, qh * BANK:(qh + 1) * BANK], C[:, 3 * BANK:4 * BANK],
                                         ACT.Copy).then_inc(s["o_out"], 1)

                def half(i, par, more):
                    if more:
                        copy_out(0, i, QT1)
                        copy_k(1, i, 1 - par)
                    for x in range(nset):
                        lo = a.first(x)
                        act.wait_ge(s["pv_done"], k["pv_done"] + i * nset + x - 1)
                        for h in range(HPG):
                            st = x * HPG + h
                            b = st % 3
                            act.wait_ge(s["st_ready"], k["st_ready"] + i * (HPG * nset) + st + 1)
                            nc.scalar.activation(PR[x % 2][:, h * BANK + lo:(h + 1) * BANK],
                                                 C[:, b * BANK + lo:(b + 1) * BANK], ACT.Exp,
                                                 scale=a.scale).then_inc(s["p_ready"], 1)
                        if x and a.half_ends(x - 1):
                            drain(i, x - 1)
                    drain(i, nset - 1)
                    if more:
                        copy_out(a.uses - 1, i, QT2[1 - par])

                nc.scalar.preload_act_table(ACT.Exp)
                copy_out(0, None, QT1)
                copy_k(1, None, 0)
                copy_out(a.lead - 1, None, QT2[0])
                with act.Fori(0, a.iters // 2 - 1) as r:
                    i = act.snap(r * 2)
                    half(i, 0, True)
                    half(i + 1, 1, True)
                half(a.iters - 2, 0, True)
                half(a.iters - 1, 1, False)

            def mix(k):
                def turned(w, use, name, dst, rows):
                    act.wait_ge(s["a_full"], k["a_full"] + w * 4 + use + 1)
                    nc.scalar.activation(dst.rearrange("p (r h n) -> p r h n", r=BLOCKS, h=HEADS0),
                                         A[rows, :].bitcast(F16).rearrange("p (h n r) -> p r h n", r=BLOCKS, h=HEADS0),
                                         ACT.Copy).then_inc(s[name], 1)

                def turned_q(w, par):
                    turned(w, 0, "q_turned", QT2[par][:, :], slice(0, P))

                def turned_k(w, par):
                    act.wait_ge(s["k_turned"], k["k_turned"] + w + 1)
                    turned(w, 1, "k_turned_2", KT[par][64:P, BLOCKS * P:], slice(64, P))

                def turned_v(w):
                    turned(w, 2, "v_turned", QT1[0:64, :], slice(0, 64))

                def exps(w, c):
                    act.wait_ge(s["pv_done"], k["pv_done"] + w * 4 + c - 1)
                    act.wait_ge(s["st_ready"], k["st_ready"] + w * 4 + c + 1)
                    nc.scalar.activation(PR[c % 2][:, 0:CHUNK * P], C[:, 0:CHUNK * P], ACT.Exp,
                                         scale=k.att.scale).then_inc(s["p_ready"], 1)

                def sums_out(w, u):
                    act.wait_ge(s["pv_done"], k["pv_done"] + w * 4 + 2 * u + 2)
                    act.wait_ge(s["ot_full"], k["ot_full"] + w * 2 + u - 1 + 1)
                    nc.scalar.activation(OT[:, u * BANK:(u + 1) * BANK], C[:, 2 * BANK:3 * BANK],
                                         ACT.Copy).then_inc(s["o_out"], 1)

                def high(w, u):
                    act.wait_ge(s["on_turned"], k["on_turned"] + w * 2 + u + 1)
                    t = w * 2 + u
                    at = (t // ST_) * SEQ + (t % ST_) * NEAR
                    for c in range(DC):
                        op = nc.scalar.activation(view(AH, at + c * TOK, (SEQ // HEADS0, HEADS0), (1, NEAR)),
                                                  view(C, 3 * BANK + c * P, (NEAR, HEADS0), (1, NEAR)), ACT.Copy)
                    op.then_inc(s["oh_ready"], 1)

                def half(w, par, more):
                    exps(w, 0)
                    if more:
                        turned_q(w + 1, 1 - par)
                        turned_k(w + 1, 1 - par)
                    exps(w, 1)
                    if more:
                        turned_v(w + 1)
                    sums_out(w, 0)
                    exps(w, 2)
                    exps(w, 3)
                    high(w, 0)
                    sums_out(w, 1)
                    high(w, 1)

                nc.scalar.preload_act_table(ACT.Exp)
                turned_q(0, 0)
                turned_k(0, 0)
                turned_v(0)
                with act.Fori(0, MIXES // 2 - 1) as r:
                    w = act.snap(r * 2)
                    half(w, 0, True)
                    half(w + 1, 1, True)
                half(MIXES - 2, 0, True)
                half(MIXES - 1, 1, False)

            def outward(k):
                pass

            def proj(k):
                with act.Fori(0, GROUPS) as g:
                    act.wait_ge(s["at_ready"], k["at_ready"] + g * 2 + 1)
                    nc.scalar.activation(XH, A[:, 0:BANK].bitcast(F16), ACT.Copy).then_inc(s["ah_copied"], 1)

            act.sem_inc(s["t_ready"], CREDIT["t_ready"])
            act.sem_inc(s["p_ready"], CREDIT["p_ready"])
            act.wait_ge(w_in, 16 * 11)
            for n, (_, src, dst) in enumerate(split):
                nc.scalar.activation(dst[0][:, :], src, ACT.Copy, scale=WSCALE).then_inc(high_done, 1)
            for k in phases:
                {"ffn": ffn, "qkv": qkv, "mix": mix, "out": outward, "att": att, "proj": proj}[k.kind](k)

        @block.vector
        def _(dve):
            def statistics(k, g):
                for t in range(GT):
                    st = nc.vector.bn_stats(bn[:, t * 6:(t + 1) * 6], view(X, g * (GT * D) + t * D, (1, D)))
                st.then_inc(s["stats_done"], 1)
                dve.wait_ge(s["stats_done"], k["stats_done"] + g + 1)
                dve.sem_inc(gate, 1)
                for t in range(GT):
                    ag = nc.vector.bn_aggr(mv[:, t * 2:(t + 1) * 2], bn[:, t * 6:(t + 1) * 6])
                ag.then_inc(s["var_ready"], 1)

            def normalise(k, g):
                dve.wait_ge(s["rstd_ready"], k["rstd_ready"] + g + 1)
                for t in range(GT):
                    op = nc.vector.tensor_scalar(XN[:, t * D:(t + 1) * D], view(X, g * (GT * D) + t * D, (1, D)),
                                                 mv[:, t * 2:t * 2 + 1], rstd[:, t:t + 1], ALU.subtract, ALU.mult)
                op.then_inc(s["xn_ready"], 1)

            def split_low(k, g):
                for c in range(DC):
                    dve.wait_ge(s["xh_ready"], k["xh_ready"] + g * DC + c + 1)
                    nc.vector.tensor_tensor(XL[:, c * GTOK:(c + 1) * GTOK], A[:, c * BANK:(c + 1) * BANK],
                                            XH[:, c * GTOK:(c + 1) * GTOK], ALU.subtract).then_inc(s["xl_ready"], 1)

            def add_to_x(g, scale):
                for n in range(2):
                    xs = view(X, g * (GT * D) + n * BANK, (1, BANK))
                    op = nc.vector.scalar_tensor_tensor(out=xs, in0=B[:, n * BANK:(n + 1) * BANK], scalar=scale,
                                                        in1=xs, op0=ALU.mult, op1=ALU.add)
                op.then_inc(s["resid"], 1)

            def ffn(k):
                def group(g, last):
                    for j in range(k.nb):
                        n = g * k.nb + j
                        dve.wait_ge(s["t_ready"], k["t_ready"] + n + 1)
                        if k.layer == 0:
                            nc.vector.tensor_tensor(U[j % 2], T[j % 2], T[j % 2], ALU.mult).then_inc(s["u_done"], 1)
                            dve.wait_ge(s["u_done"], k["u_done"] + n + 1)
                        dve.wait_ge(s["uh_ready"], k["uh_ready"] + n + 1)
                        nc.vector.tensor_tensor(UL[j % 2], (U if k.layer == 0 else T)[j % 2], UH[j % 2],
                                                ALU.subtract).then_inc(s["ul_ready"], 1)
                        if j == 1 and not last:
                            statistics(k, g + 1)
                        if j == 3 and not last:
                            normalise(k, g + 1)
                    if not last:
                        split_low(k, g + 1)
                    dve.wait_ge(s["down_done"], k["down_done"] + (g + 1) * k.nb)
                    if k.layer == 1:
                        dve.wait_ge(s["bias_added"], k["bias_added"] + g + 1)
                    add_to_x(g, sc[:, 1:2] if k.layer == 0 else 0.5)

                dve.wait_ge(s["resid"], k["resid"])
                statistics(k, 0)
                normalise(k, 0)
                split_low(k, 0)
                with dve.Fori(0, GROUPS - 1) as g:
                    group(g, False)
                group(GROUPS - 1, True)

            def qkv(k):
                a = k.att

                def low(dst, o, at, row, heads, part):
                    return nc.vector.scalar_tensor_tensor(
                        out=view(dst, at + part * a.hd, (row, heads), (1, a.hd)),
                        in0=view(C, o, (a.hd, heads), (1, a.hd)), scalar=1 / WSCALE,
                        in1=view(dst, at, (row, heads), (1, a.hd)), op0=ALU.mult, op1=ALU.subtract)

                def group(g, last):
                    for t in range(GT):
                        dve.wait_ge(s["hi_ready"], k["hi_ready"] + g * GT + t + 1)
                        o, at = t % 2 * 2 * BANK, a.at(g, t)
                        low(QA, o, at, a.step, a.heads, 1)
                        op = low(KA, o + D, at, a.step * (HPG // a.vh), a.kv, 2)
                        if k.layer == 0:
                            v_at = a.v_at(g, t)
                            op = nc.vector.scalar_tensor_tensor(
                                out=view16(VS, v_at + a.hd, (4 * a.hd, a.kv), (1, a.hd)),
                                in0=view(C, o + 2 * D, (a.hd, a.kv), (1, a.hd)), scalar=1 / WSCALE,
                                in1=view16(VS, v_at, (4 * a.hd, a.kv), (1, a.hd)), op0=ALU.mult, op1=ALU.subtract)
                        op.then_inc(s["qkv_free"], 1)
                        if t == 0 and not last:
                            statistics(k, g + 1)
                        if t == 2 and not last:
                            normalise(k, g + 1)
                    if not last:
                        split_low(k, g + 1)

                dve.wait_ge(s["resid"], k["resid"])
                statistics(k, 0)
                normalise(k, 0)
                split_low(k, 0)
                with dve.Fori(0, GROUPS - 1) as g:
                    group(g, False)
                group(GROUPS - 1, True)

            def att(k):
                a = k.att
                nmax = len(a.maxes)

                def place(i, of_batch, of_group):
                    b = i // a.groups
                    at = b * of_batch + (i % a.groups) * of_group
                    return at if isinstance(at, int) else dve.snap(at)

                def maximum(i, m, full, dst):
                    qt, heads = a.maxes[m]
                    dve.wait_ge(s["slot_full"], full)
                    src = view(dst, 0, (a.width(qt), len(heads)), (1, a.keys(qt)))
                    c = qt * HPG + heads[0]
                    nc.vector.tensor_reduce(NM[:, c:c + len(heads)], src, AX_X, ALU.max,
                                            negate=True).then_inc(s["maxed"], 1)

                def maxima(i, n0, full):
                    dve.wait_ge(s["m_written"], k["m_written"] + i)
                    for m in range(nmax):
                        maximum(i, m, full + m, slots[(n0 + m) % 2])
                    at = place(i, ST_ * 1024, a.qkw)
                    dve.wait_ge(s["maxed"], k["maxed"] + (i + 1) * nmax)
                    nm = view(NM, 0, (HPG, ST_), (1, HPG))
                    mh = view(QA, at + 3 * a.hd, (1024, ST_), (a.row, HPG))
                    nc.vector.tensor_copy(mh, nm).then_inc(s["mh_done"], 1)
                    dve.wait_ge(s["mh_done"], k["mh_done"] + i + 1)
                    nc.vector.tensor_tensor(view(QA, at + (3 * a.hd + 1), (1024, ST_), (a.row, HPG)), nm, mh,
                                            ALU.subtract).then_inc(s["m_written"], 1)

                def divide(i, n):
                    u = a.lead + n
                    dve.wait_ge(s["slot_full"], k["slot_full"] + i * a.uses + u + 1)
                    dve.wait_ge(s["ao_ready"], k["ao_ready"] + i)
                    src = slots[u % 2]
                    nc.vector.reciprocal(view(RD, 0, (HPG, ST_), (1, HPG)),
                                         view(src, a.hd, (P, ST_), (32, HPG))).then_inc(s["rd_done"], 1)
                    dve.wait_ge(s["rd_done"], k["rd_done"] + i + 1)
                    nc.vector.tensor_tensor(view(ON, 0, (HPG * a.hd, ST_), (a.hd, HPG), (1, a.hd)),
                                            view(src, 0, (P, ST_), (32, HPG), (1, a.hd)),
                                            view(RD, 0, (HPG, ST_), (1, HPG), (0, a.hd)),
                                            ALU.mult).then_inc(s["on_ready"], 1)

                def half(i, more):
                    if more:
                        maxima(i + 1, a.lead + 2, k["slot_full"] + i * a.uses + a.lead + 3)
                    divide(i, a.uses - 2 if more else 0)

                maxima(0, 2, k["slot_full"] + 3)
                with dve.Fori(0, a.iters // 2 - 1) as r:
                    i = dve.snap(r * 2)
                    half(i, True)
                    half(i + 1, True)
                half(a.iters - 2, True)
                half(a.iters - 1, False)

            def mix(k):
                def turned_k(w, par):
                    dve.wait_ge(s["a_full"], k["a_full"] + w * 4 + 2)
                    nc.vector.tensor_copy(KT[par][0:64, 0:BLOCKS * P].rearrange("p (r h n) -> p r h n", r=BLOCKS, h=HEADS0),
                                          A[0:64, :].bitcast(F16).rearrange("p (h n r) -> p r h n", r=BLOCKS, h=HEADS0))\
                        .then_inc(s["k_turned"], 1)

                def blocks_v(w, par):
                    dve.wait_ge(s["a_full"], k["a_full"] + w * 4 + 4)
                    nc.vector.tensor_copy(view(VG[par], 0, (32 * BLOCKS, 2), (32, BLOCKS), (1, HD0)),
                                          view(A, 0, (BANK, 2), (HD0, BLOCKS), (1, HD0))).then_inc(s["v_ready"], 1)

                def maximum(w, c):
                    dve.wait_ge(s["b_full"], k["b_full"] + w * 5 + c + 1)
                    nc.vector.tensor_reduce(NM[:, c * CHUNK:(c + 1) * CHUNK], view(B, 0, (P, CHUNK), (1, P)), AX_X,
                                            ALU.max, negate=True).then_inc(s["maxed"], 1)

                def turned_m(w, par):
                    dve.wait_ge(s["b_full"], k["b_full"] + w * 5 + 5)
                    nc.vector.tensor_copy(MT[par][0:2 * BLOCKS, :], B[0:2 * BLOCKS, 0:P]).then_inc(s["m_ready"], 1)

                def divide(w, u):
                    dve.wait_ge(s["ot_full"], k["ot_full"] + w * 2 + u + 1)
                    nc.vector.reciprocal(RD[:, u * BLOCKS:(u + 1) * BLOCKS], view(C, 3 * BANK + HD0, (32, BLOCKS)))\
                        .then_inc(s["rd_done"], 1)
                    dve.wait_ge(s["rd_done"], k["rd_done"] + w * 2 + u + 1)
                    nc.vector.tensor_tensor(view(ON, u * D, (HD0, BLOCKS), (1, HD0)),
                                            view(C, 3 * BANK, (32, BLOCKS), (1, HD0)),
                                            view(RD, u * BLOCKS, (1, BLOCKS), (0, HD0)),
                                            ALU.mult).then_inc(s["on_ready"], 1)

                def low(w, u):
                    dve.wait_ge(s["oh_ready"], k["oh_ready"] + w * 2 + u + 1)
                    t = w * 2 + u
                    at = (t // ST_) * SEQ + (t % ST_) * NEAR
                    for c in range(DC):
                        op = nc.vector.tensor_tensor(view(AL, at + c * TOK, (SEQ // HEADS0, HEADS0), (1, NEAR)),
                                                     view(C, 3 * BANK + c * P, (NEAR, HEADS0), (1, NEAR)),
                                                     view(AH, at + c * TOK, (SEQ // HEADS0, HEADS0), (1, NEAR)),
                                                     ALU.subtract)
                    op.then_inc(s["ol_ready"], 1)

                def half(w, par, more):
                    n = w + 1
                    if more:
                        turned_k(n, 1 - par)
                        blocks_v(n, 1 - par)
                        maximum(n, 0)
                        maximum(n, 1)
                    divide(w, 0)
                    if more:
                        maximum(n, 2)
                    low(w, 0)
                    if more:
                        maximum(n, 3)
                    divide(w, 1)
                    if more:
                        turned_m(n, 1 - par)
                    low(w, 1)

                dve.wait_ge(v_pad, 4)
                turned_k(0, 0)
                blocks_v(0, 0)
                for c in range(4):
                    maximum(0, c)
                turned_m(0, 0)
                with dve.Fori(0, MIXES // 2 - 1) as r:
                    w = dve.snap(r * 2)
                    half(w, 0, True)
                    half(w + 1, 1, True)
                half(MIXES - 2, 0, True)
                half(MIXES - 1, 1, False)

            def outward(k):
                with dve.Fori(0, GROUPS) as g:
                    dve.wait_ge(s["y_ready"], k["y_ready"] + g + 1)
                    add_to_x(g, 1 / WSCALE)

            def proj(k):
                with dve.Fori(0, GROUPS) as g:
                    dve.wait_ge(s["at_ready"], k["at_ready"] + g * 2 + 2)
                    nc.vector.tensor_copy(XL, A[:, BANK:2 * BANK].bitcast(F16)).then_inc(s["al_copied"], 1)
                    dve.wait_ge(s["y_ready"], k["y_ready"] + g + 1)
                    add_to_x(g, 1 / WSCALE)

            steps = [0]

            def step(op):
                steps[0] += 1
                op.then_inc(setup_step, 1)
                dve.wait_ge(setup_step, steps[0])

            dve.sem_inc(s["qkv_free"], CREDIT["qkv_free"])
            dve.wait_ge(w_in, 16 * 11)
            for n, (_, src, _) in enumerate(quant):
                op = nc.vector.tensor_reduce(sums[:, n:n + 1], src, AX_X, ALU.add, apply_absolute_value=True)
            op.then_inc(sums_ready, 1)
            dve.wait_ge(tot_ready, 1)
            for k, (floor, cut) in enumerate(((1e-5, 0.7), (1e-8, 0.5))):
                c = slice(2 * k, 2 * k + 2)
                size = float(D * HID[k])
                step(nc.vector.tensor_scalar(means[:, c], C[:, c], 1 / size, floor, ALU.mult, ALU.max))
                nc.vector.tensor_scalar(lim[:, c], means[:, c], cut, None, ALU.mult)
                step(nc.vector.tensor_scalar(lim[:, 4 + 2 * k:6 + 2 * k], means[:, c], -cut, None, ALU.mult))
            step(nc.vector.tensor_tensor(sc[:, 0:1], means[:, 0:1], means[:, 0:1], ALU.mult))
            step(nc.vector.tensor_scalar(sc[:, 1:2], sc[:, 0:1], means[:, 1:2], 0.5 / RSCALE ** 2, ALU.mult, ALU.mult))
            for n, (w, src, dst) in enumerate(quant):
                below = work[:, 0:dst.shape[1]]
                step(nc.vector.tensor_scalar(below, src, lim[:, 4 + n:5 + n], None, ALU.is_lt))
                step(nc.vector.scalar_tensor_tensor(out=dst[:, :], in0=src, scalar=lim[:, n:n + 1], in1=below,
                                                    op0=ALU.is_gt, op1=ALU.subtract))
            for n, (_, src, dst) in enumerate(split):
                dve.wait_ge(high_done, n + 1)
                nc.vector.scalar_tensor_tensor(out=dst[1][:, :], in0=src, scalar=WSCALE, in1=dst[0][:, :],
                                               op0=ALU.mult, op1=ALU.subtract)
            nc.vector.tensor_scalar(b2h[:, :], b2h[:, :], 0.5, None, ALU.mult).then_inc(w_ready, 1)
            dve.wait_ge(x_in, 16 * GROUPS)
            for k in phases:
                {"ffn": ffn, "qkv": qkv, "mix": mix, "out": outward, "att": att, "proj": proj}[k.kind](k)

        @block.gpsimd
        def _(pool):
            def rsqrt(k, g):
                pool.wait_ge(s["var_ready"], k["var_ready"] + g + 1)
                nc.gpsimd.tensor_tensor(var[:, :], view(mv, 1, (2, GT)), eps[:, :], ALU.add).then_inc(s["eps_done"], 1)
                pool.wait_ge(s["eps_done"], k["eps_done"] + g + 1)
                nc.gpsimd.tensor_tensor(rstd[:, :], var[:, :], mhalf[:, :], ALU.pow).then_inc(s["rstd_ready"], 1)

            def ffn(k):
                def group(g, last):
                    if k.layer == 1:
                        pool.wait_ge(s["xn_ready"], k["xn_ready"] + g + 1)
                        xs = view(X, g * (GT * D), (D, GT), (1, D))
                        nc.gpsimd.tensor_tensor(xs, xs, view(b2h, 0, (0, GT), (1, D)), ALU.add)\
                            .then_inc(s["bias_added"], 1)
                    if not last:
                        rsqrt(k, g + 1)

                rsqrt(k, 0)
                with pool.Fori(0, GROUPS - 1) as g:
                    group(g, False)
                group(GROUPS - 1, True)

            def qkv(k):
                a = k.att
                row = a.step * (HPG // a.vh)

                def group(g, last):
                    if not last:
                        rsqrt(k, g + 1)
                    for t in range(GT):
                        pool.wait_ge(s["qkv_free"], k["qkv_free"] + g * GT + t + 1)
                        at = a.at(g, t)
                        nc.gpsimd.tensor_copy(view(QA, at + 2 * a.hd, (a.step, a.heads), (1, a.hd)),
                                              view(QA, at, (a.step, a.heads), (1, a.hd)))
                        op = nc.gpsimd.tensor_copy(view(KA, at + a.hd, (row, a.kv), (1, a.hd)),
                                                   view(KA, at, (row, a.kv), (1, a.hd)))
                        if a.vh == 1:
                            op.then_inc(s["k_dup"], 1)
                            pool.wait_ge(s["k_dup"], k["k_dup"] + g * GT + t + 1)
                            op = nc.gpsimd.tensor_copy(view(KA, at + a.row, (row, a.kv), (a.row, HPG - 1), (1, 3 * a.hd)),
                                                       view(KA, at, (row, a.kv), (0, HPG - 1), (1, 3 * a.hd)))
                        op.then_inc(s["dup_done"], 1)

                rsqrt(k, 0)
                with pool.Fori(0, GROUPS - 1) as g:
                    group(g, False)
                group(GROUPS - 1, True)

            def att(k):
                a = k.att
                nset = len(a.sets)

                def place(i, of_batch, of_group):
                    b = i // a.groups
                    at = b * of_batch + (i % a.groups) * of_group
                    return at if isinstance(at, int) else pool.snap(at)

                def group_v(i, par):
                    if not (isinstance(i, int) and i == 0):
                        pool.wait_ge(s["pv_done"], k["pv_done"] + (i - 1) * nset)
                    at = place(i, ST_ * a.kvw, a.vh * a.hd)
                    nc.gpsimd.tensor_copy(view(VG[par], 0, (a.vh * 32, ST_), (32, a.vh), (1, a.hd)),
                                          view(VS, at, (a.kvw, ST_), (a.hd, a.vh), (1, a.hd))).then_inc(s["v_ready"], 1)

                def half(i, par, more):
                    if more:
                        group_v(i + 1, 1 - par)
                    pool.wait_ge(s["on_ready"], k["on_ready"] + i + 1)
                    at = place(i, ST_ * D, HPG * a.hd)
                    w = HPG * a.hd
                    nc.gpsimd.tensor_copy(view(AH, at, (D, ST_), (1, w)), view(ON, 0, (w, ST_), (1, w)))\
                        .then_inc(s["ah_done"], 1)
                    pool.wait_ge(s["ah_done"], k["ah_done"] + i + 1)
                    nc.gpsimd.tensor_tensor(view(AL, at, (D, ST_), (1, w)), view(ON, 0, (w, ST_), (1, w)),
                                            view(AH, at, (D, ST_), (1, w)), ALU.subtract).then_inc(s["ao_ready"], 1)

                pool.wait_ge(s["hi_ready"], k["hi_ready"])
                ones_of_v(1)
                group_v(0, 0)
                with pool.Fori(0, a.iters // 2 - 1) as r:
                    i = pool.snap(r * 2)
                    half(i, 0, True)
                    half(i + 1, 1, True)
                half(a.iters - 2, 0, True)
                half(a.iters - 1, 1, False)

            def mix(k):
                ones_of_v(0)

            def outward(k):
                pads(1)

            def ones_of_v(layer):
                a = ATTS[layer]
                for n in range(2):
                    nc.gpsimd.memset(VG[n][:, :], 0.0).then_inc(v_pad, 1)
                pool.wait_ge(v_pad, 4 * layer + 2)
                for n in range(2):
                    nc.gpsimd.memset(view(VG[n], a.hd, (32, ST_ * a.vh)), 1.0).then_inc(v_pad, 1)
                pool.wait_ge(v_pad, 4 * layer + 4)

            def pads(layer):
                a = ATTS[layer]
                if layer == 1:
                    pool.wait_ge(s["ol_ready"], phases[3]["ol_ready"])
                nc.gpsimd.memset(QA[:, :].bitcast(F32), 0.0).then_inc(pad_zeroed, 1)
                nc.gpsimd.memset(KA[:, :].bitcast(F32), 0.0).then_inc(pad_zeroed, 1)
                for t in KT:
                    nc.gpsimd.memset(t[:, :].bitcast(F32), 0.0).then_inc(k_zeroed, 1)
                if layer == 0:
                    for t in MT:
                        nc.gpsimd.memset(t[:, :], 0.0).then_inc(k_zeroed, 1)
                pool.wait_ge(k_zeroed, 4 if layer == 0 else 6)
                pool.wait_ge(pad_zeroed, 2 * layer + 2)
                if layer == 1:
                    nc.gpsimd.memset(view(KA, 3 * a.hd, (a.row, NT * 1024 // a.row), (1, 2)), 1.0)\
                        .then_inc(pad_ready, 1)
                else:
                    for n, t in enumerate((QA, KA)):
                        op = nc.gpsimd.tensor_copy(view(t, 3 * a.hd, (a.row, NT * a.heads), (1, NEAR)),
                                                   view(aparts, n * NEAR, (0, NT * a.heads), (1, NEAR)))
                    op.then_inc(pad_ready, 1)

            def proj(k):
                pass

            pool.sem_inc(s["down_done"], CREDIT["down_done"])
            pool.sem_inc(s["pv_done"], CREDIT["pv_done"])
            for n, t in enumerate((ident, ident16, identb, maskb, maskt)):
                nc.gpsimd.memset(t[:, :], 0.0).then_inc(const_step, 1)
            pool.wait_ge(const_step, 5)
            for t in (ident, ident16, identb):
                nc.gpsimd.affine_select(out=t[:, :], in_=t[:, :], compare_op=ALU.not_equal, fill=1.0, base=0,
                                        pattern=[[-1, P]], channel_multiplier=1).then_inc(const_ready, 1)
            for t, sign in ((maskb, 1), (maskt, -1)):
                nc.gpsimd.affine_select(out=t[:, :], in_=t[:, :], compare_op=ALU.is_ge, fill=NEG, base=0,
                                        pattern=[[-sign, P]], channel_multiplier=sign).then_inc(const_ready, 1)
            nc.gpsimd.memset(ones[:, :], 1.0).then_inc(const_ready, 1)
            nc.gpsimd.memset(two[:, :], 0.0).then_inc(const_step, 1)
            for n in range(4):
                pool.wait_ge(const_step, 6 + n)
                nc.gpsimd.affine_select(out=two[:, :], in_=two[:, :], compare_op=ALU.not_equal, fill=1.0,
                                        base=-n * HD0, pattern=[[-1, HD0]], channel_multiplier=1)\
                    .then_inc(const_step, 1)
            pool.wait_ge(const_step, 10)
            nc.gpsimd.memset(mhalf[:, :], -0.5).then_inc(const_ready, 1)
            nc.gpsimd.memset(eps[:, :], EPS).then_inc(const_ready, 1)
            pool.wait_ge(const_ready, 8)
            pool.wait_ge(w_ready, 1)
            nc.gpsimd.memset(VS[:, NT * D:], 0.0).then_inc(pad_ready, 1)
            pads(0)
            for k in phases:
                {"ffn": ffn, "qkv": qkv, "mix": mix, "out": outward, "att": att, "proj": proj}[k.kind](k)


def kernel(L0_attn_x, L0_attn_w_qkv, L0_attn_w_proj, L0_ffn_w_fc, L0_ffn_w_proj, L1_attn_wq, L1_attn_wk,
           L1_attn_wv, L1_attn_wo, L1_ffn_w1, L1_ffn_b1, L1_ffn_w2, L1_ffn_b2):
    import numpy as np
    import concourse.bacc as bacc
    from concourse.bass_utils import run_bass_kernel_spmd

    shape = L0_attn_x.shape
    near = BIG * (np.arange(P)[:, None] // BLOCKS == np.arange(NEAR)[None, :])
    arrays = {
        "x": np.asarray(L0_attn_x).reshape(TOK, D),
        "fc0": np.asarray(L0_ffn_w_fc).T, "down0": np.asarray(L0_ffn_w_proj).T,
        "fc1": np.asarray(L1_ffn_w1).T, "down1": np.asarray(L1_ffn_w2).T,
        "apart": np.concatenate([near, near - BIG], axis=1).astype(np.float32),
        "b1": np.asarray(L1_ffn_b1).reshape(-1, P).T, "b2": np.asarray(L1_ffn_b2).reshape(1, D),
        "qkv0": np.asarray(L0_attn_w_qkv).T, "wo0": np.asarray(L0_attn_w_proj).T,
        "qkv1": np.concatenate([np.asarray(w) for w in (L1_attn_wq, L1_attn_wk, L1_attn_wv)], axis=1),
        "wo1": np.asarray(L1_attn_wo),
    }
    arrays = {name: np.ascontiguousarray(a) for name, a in arrays.items()}
    nc = bacc.Bacc("TRN2", target_bir_lowering=False, num_devices=1)
    args = [nc.dram_tensor(name, a.shape, F32, kind="ExternalInput").ap() for name, a in arrays.items()]
    out = nc.dram_tensor("out", [TOK, D], F32, kind="ExternalOutput").ap()
    names = list(arrays)
    order = dict(zip(names, args))
    macaron_kernel(nc, out=out, **order)
    r = run_bass_kernel_spmd(nc, [arrays], core_ids=[0])
    return r.results[0]["out"].reshape(shape)
```

```python
from contextlib import ExitStack

import concourse.bass as bass
from concourse import mybir

F32 = mybir.dt.float32
F16 = mybir.dt.float16
BF16 = mybir.dt.bfloat16
ALU = mybir.AluOpType
ACT = mybir.ActivationFunctionType
AX_X = mybir.AxisListType.X

P = 128
D = 256
DC = D // P
TOK = 2048
NT = TOK // P
SEQ = 1024
ST_ = SEQ // P
BATCH = TOK // SEQ
GT = 4
GROUPS = NT // GT
GTOK = GT * P
BANK = 512
HPG = 4
WSCALE = 64.0
RSCALE = 0.25
NEG = -1.0e30
EPS = 1e-5

HID = (640, 1024)
BIG = 60000.0

HD0, HEADS0, NEAR = 16, 16, 8
BLOCKS = P // NEAR
MIXES = NT // 2
CHUNK = 4
HALF = HEADS0 // 2
CHUNKS = 2 * BLOCKS // CHUNK


class Att:

    def __init__(self, heads, kv_heads, causal):
        self.heads, self.kv, self.causal = heads, kv_heads, causal
        self.hd = D // heads
        self.row = 64 if self.hd == 16 else 32
        self.step = self.row if causal else 2 * self.row
        self.qkw = HPG * self.row
        self.tiles = self.qkw // P
        self.groups = heads // HPG
        self.iters = BATCH * self.groups
        self.vh = HPG if kv_heads == heads else 1
        self.scale = float(self.hd) ** -0.5
        self.kvw = kv_heads * self.hd
        self.cols = D + 2 * self.kvw
        self.sets = [(h, k) for h in range(2) for k in range(GT * (h + 1) if causal else ST_)]
        self.maxes = []
        for qt in range(ST_):
            n = min(HPG, 2 * BANK // self.width(qt))
            self.maxes += [(qt, list(range(h, h + n))) for h in range(0, HPG, n)]
        n = len(self.maxes)
        self.lead = n + 5
        self.m_use, self.q_use, self.k_use, self.o_use = n, n + 1, n + 2, n + 3
        self.uses = n + 4
        assert self.uses % 2 == 0

    def out_use(self, ahead):
        return [0, self.q_use, self.o_use][ahead]

    def full(self, i, n):
        if i is None:
            return n + 1
        if isinstance(i, int) and i == self.iters - 1:
            return self.full(i - 1, self.out_use(1)) + n + 1
        return self.lead + i * self.uses + n + 1

    def at(self, g, t):
        if self.causal:
            return g * (GT * 1024) + t * 1024
        return g * (GT * 1024) + (t // 2 * 2048 + t % 2 * self.row)

    def v_at(self, g, t):
        if self.causal:
            return g * (GT * self.kvw) + t * self.kvw
        return g * (GT * 2 * D) + (t // 2 * 4 * D + t % 2 * 2 * self.hd)

    def keys(self, qt):
        return P * (qt + 1) if self.causal else SEQ

    def width(self, qt):
        w = self.keys(qt)
        return w if BANK % w == 0 else -(-w // BANK) * BANK

    def first(self, s):
        h, k = self.sets[s]
        return max(0, (k - GT * h) * P) if self.causal else 0

    def diagonal(self, s):
        h, k = self.sets[s]
        return self.causal and k >= GT * h

    def work(self, s, h):
        cols = [HPG * (BANK - self.first(x)) for x in range(len(self.sets))]
        return sum(cols[:s]) + cols[s] * (h + 1) // HPG

    def quota(self, s, h):
        cols, part = 0, self.work(s, h) / self.work(len(self.sets) - 4, HPG - 1)
        done = [sum(self.keys(q) * len(hs) for q, hs in self.maxes[:n + 1]) for n in range(len(self.maxes))]
        return sum(d <= part * done[-1] for d in done)

    def half_ends(self, s):
        return s + 1 == len(self.sets) or self.sets[s + 1][0] != self.sets[s][0]


ATTS = (Att(HEADS0, HEADS0, False), Att(32, 8, True))


def before(j, used):
    steps = [n for n, b in enumerate(used * 2) if b == used[j] and n < j + len(used)]
    return j + len(used) - steps[-1]


class Phase:

    def __init__(self, kind, layer, at):
        self.kind, self.layer, self.at = kind, layer, at
        self.next, self.primed = None, False
        self.att = ATTS[layer]
        self.nb = HID[layer] // P
        self.banks = [j % 4 if j % 4 or j + 1 < self.nb else 1 for j in range(self.nb)]
        self.rings = [j % 3 for j in range(self.nb)]
        n, a = {}, self.att
        if kind in ("ffn", "qkv"):
            n.update(stats_done=GROUPS, var_ready=GROUPS, eps_done=GROUPS, rstd_ready=GROUPS, xn_ready=GROUPS,
                     xt_ready=DC * GROUPS, xh_ready=DC * GROUPS, xl_ready=DC * GROUPS)
        if kind == "ffn":
            for name in ("h_ready", "t_ready", "uh_ready", "ul_ready", "down_done"):
                n[name] = self.nb * GROUPS
            n["resid"] = GROUPS
            n["u_done" if layer == 0 else "bias_added"] = self.nb * GROUPS if layer == 0 else GROUPS
        if kind == "qkv":
            n.update(qkv_ready=NT, hi_ready=NT, qkv_free=NT, dup_done=NT)
        if kind == "mix":
            w = MIXES
            n.update(a_full=8 * w, a0_read=4 * w, a1_read=4 * w, b_full=(CHUNKS + 1) * w, maxed=CHUNKS * w,
                     m_ready=w, st_ready=CHUNKS * w, p_ready=CHUNKS * w, pv_done=CHUNKS * w, o_out=2 * w, ot_full=2 * w,
                     rd_done=2 * w, on_ready=2 * w, on_turned=2 * w, oh_ready=2 * w, ol_ready=2 * w)
        if kind == "out":
            n.update(y_ready=GROUPS, resid=GROUPS)
        if kind == "att":
            i, s = a.iters, len(a.sets)
            n.update(slot_full=a.full(i - 1, 0), maxed=len(a.maxes) * i, q_copied=i, k_copied=i, qm_copied=i,
                     mh_done=i, m_written=i, st_ready=HPG * s * i, p_ready=HPG * s * i, pv_done=s * i,
                     o_out=2 * i, v_ready=i, rd_done=i, on_ready=i, ah_done=i, ao_ready=i)
        if kind == "proj":
            n.update(at_ready=2 * GROUPS, ah_copied=GROUPS, al_copied=GROUPS, y_ready=GROUPS, resid=GROUPS)
        self.n = n
        self.after = {**at, **{k: at.get(k, 1) + v for k, v in n.items()}}

    def __getitem__(self, name):
        return self.at.get(name, 1)


CREDIT = {"down_done": 8, "t_ready": 8, "qkv_free": 2, "pv_done": 8, "p_ready": 4}


def plan():
    phases, at = [], dict(CREDIT)
    for kind, layer in [("ffn", 0), ("qkv", 0), ("mix", 0), ("out", 0), ("ffn", 0),
                        ("ffn", 1), ("qkv", 1), ("att", 1), ("proj", 1), ("ffn", 1)]:
        phases.append(Phase(kind, layer, at))
        at = phases[-1].after
    for k, n in zip(phases, phases[1:]):
        if k.kind in ("ffn", "out") and n.kind in ("ffn", "qkv"):
            k.next, n.primed = n, True
    return phases


def macaron_kernel(nc, x, apart, fc0, down0, fc1, down1, b1, b2, qkv0, wo0, qkv1, wo1, out):
    phases = plan()

    with ExitStack() as ctx:
        def sb(name, cols, dt):
            return ctx.enter_context(nc.sbuf_tensor(name, [P, cols], dt))

        def ps(name, cols):
            return ctx.enter_context(nc.psum_tensor(name, [P, cols], F32))

        def sem(name):
            return ctx.enter_context(nc.semaphore(name))

        def view(t, at, *dims):
            return bass.AP(t, at, [[t.shape[1], P], *[list(d) for d in dims]])

        def view16(t, at, *dims):
            full = t[:, :].bitcast(F16)
            return bass.AP(full.tensor, at, [[t.shape[1] * 2, P], *[list(d) for d in dims]])

        X = sb("X", NT * D, F32)
        QA = sb("QA", NT * 1024, F16)
        KA = sb("KA", NT * 1024, F16)
        VS = sb("VS", NT * D + P // 4, F32)
        VG = [sb(f"VG{k}", ST_ * HPG * 32, F32) for k in range(2)]
        QT1 = sb("QT1", 2 * SEQ, F16)
        QT2 = [sb(f"QT2{k}", 2 * SEQ, F16) for k in range(2)]
        KT = [sb(f"KT{k}", HPG * SEQ, F16) for k in range(2)]
        AH = sb("AH", NT * D, F16)
        AL = sb("AL", NT * D, F16)
        OT = sb("OT", 2 * BANK, F32)
        ON = sb("ON", ST_ * HPG * 16, F32)
        RD = sb("RD", ST_ * HPG, F32)
        NM = sb("NM", ST_ * HPG, F32)
        work = sb("work", 5120, F32)
        PR = [work[:, k * HPG * BANK:(k + 1) * HPG * BANK] for k in range(2)]
        XN = work[:, 0:GT * D]
        XH = work[:, 1024:1536].bitcast(F16)
        XL = work[:, 1536:2048].bitcast(F16)
        T = [work[:, 2048 + k * BANK:2048 + (k + 1) * BANK] for k in range(2)] + [OT[:, 0:BANK]]
        U = [work[:, 3072 + k * BANK:3072 + (k + 1) * BANK] for k in range(2)] + [OT[:, BANK:2 * BANK]]
        UH = [t.bitcast(F16) for t in (work[:, 4096:4352], work[:, 4352:4608], ON[:, 0:256])]
        UL = [t.bitcast(F16) for t in (work[:, 4608:4864], work[:, 4864:5120], ON[:, 256:512])]
        up = [sb(f"up_w{k}", DC * HID[k], F16) for k in range(2)]
        down = [sb(f"down_w{k}", HID[k] // P * D, F16) for k in range(2)]
        wqkv = [[sb(f"qkv_w{k}{p}", DC * ATTS[k].cols, F16) for p in "hl"] for k in range(2)]
        wo = [[sb(f"wo_w{k}{p}", DC * D, F16) for p in "hl"] for k in range(2)]
        b1s = sb("b1s", HID[1] // P, F32)
        b2h = sb("b2h", D, F32)
        ident = sb("ident", P, F32)
        ident16 = sb("ident16", P, F16)
        identb = sb("identb", P, BF16)
        maskb = sb("maskb", P, BF16)
        maskt = sb("maskt", P, BF16)
        ones = sb("ones", P, F32)
        sums = sb("sums", 4, F32)
        means = sb("means", 4, F32)
        lim = sb("lim", 8, F32)
        sc = sb("sc", 2, F32)
        bn = sb("bn", GT * 6, F32)
        mv = sb("mv", GT * 2, F32)
        var = sb("var", GT, F32)
        rstd = sb("rstd", GT, F32)
        mhalf = sb("mhalf", GT, F32)
        eps = sb("eps", GT, F32)
        aparts = sb("aparts", 2 * NEAR, F32)
        MT = [sb(f"MT{k}", P, BF16) for k in range(2)]
        two = sb("two", HD0, F16)

        A = ps("A", 2 * BANK)
        B = ps("B", 2 * BANK)
        C = ps("C", 4 * BANK)
        slots = [A, B]

        def by_block(t, b):
            return t.rearrange("p (r h n) -> p r h n", r=BLOCKS, h=HEADS0)[:, :, b * HALF:(b + 1) * HALF, :]

        def by_head(t, rows, b):
            return t[rows, b * BANK:(b + 1) * BANK].bitcast(F16).rearrange("p (h n r) -> p r h n", r=BLOCKS, h=HALF)

        def slot(i, n):
            return slots[(n if i is None else ATTS[1].lead + n) % 2]

        s = {k: sem(k) for k in sorted({k for ph in phases for k in ph.n})}
        gate, x_in, ffn_w_in, w_in, ternary_step, ternary_1, const_ready, const_step, sums_ready, tot_ready = (sem(k) for k in (
            "gate", "x_in", "ffn_w_in", "w_in", "ternary_step", "ternary_1", "const_ready", "const_step", "sums_ready", "tot_ready"))
        setup_step, high_done, w_ready, pad_zeroed, pad_ready, v_pad, k_zeroed, out_done = (sem(k) for k in (
            "setup_step", "high_done", "w_ready", "pad_zeroed", "pad_ready", "v_pad", "k_zeroed", "out_done"))

        landing = {id(fc0): VS[:, 0:1280], id(down0): VS[:, 1280:2560], id(qkv0): VS[:, 2560:4096],
                   id(fc1): AH[:, :].bitcast(F32), id(down1): AL[:, :].bitcast(F32), id(wo0): ON[:, :],
                   id(qkv1): OT[:, 0:DC * ATTS[1].cols], id(wo1): QT1[:, :].bitcast(F32)[:, 0:DC * D]}
        quant = [(w, landing[id(w)], dst) for w, dst in ((fc0, up[0]), (down0, down[0]), (fc1, up[1]), (down1, down[1]))]
        split = [(w, landing[id(w)], dst) for w, dst in ((qkv0, wqkv[0]), (wo0, wo[0]), (qkv1, wqkv[1]), (wo1, wo[1]))]

        block = ctx.enter_context(nc.Block())

        @block.sync
        def _(sp):
            def tiles(dram, g):
                return dram.rearrange("(t p) d -> p t d", p=P)[:, g * GT:(g + 1) * GT, :]

            def load(w, dst, done):
                sp.dma_start(dst.rearrange("p (c n) -> p c n", c=w.shape[0] // P),
                             w.rearrange("(c p) n -> p c n", p=P)).then_inc(done, 16)

            for w, dst, _ in quant:
                load(w, dst, ffn_w_in)
            for g in range(GROUPS):
                sp.dma_start(view(X, g * GT * D, (D, GT), (1, D)), tiles(x, g)).then_inc(x_in, 16)
            for w, dst, _ in split:
                load(w, dst, w_in)
            sp.dma_start(aparts[:, :], apart).then_inc(w_in, 16)
            sp.dma_start(b1s[:, :], b1).then_inc(w_in, 16)
            sp.dma_start(b2h[:, :], b2.broadcast_to([P, D])).then_inc(w_in, 16)
            for g in range(GROUPS):
                sp.wait_ge(s["resid"], phases[-1]["resid"] + g + 1)
                sp.dma_start(tiles(out, g), view(X, g * GT * D, (D, GT), (1, D))).then_inc(out_done, 16)
            sp.wait_ge(out_done, 16 * GROUPS)

        @block.tensor
        def _(pe):
            def transposes(k, g):
                pe.wait_ge(s["xn_ready"], k["xn_ready"] + g + 1)
                for c in range(DC):
                    for t in range(GT):
                        mm = pe.transpose(A[:, c * BANK + t * P:c * BANK + (t + 1) * P],
                                          XN[:, t * D + c * P:t * D + (c + 1) * P], ident[:, :])
                    mm.then_inc(s["xt_ready"], 1)

            def ffn(k):
                W, V, nb, hid = up[k.layer], down[k.layer], k.nb, HID[k.layer]

                def hidden(g, j):
                    b = k.banks[j]
                    pe.wait_ge(s["t_ready"], k["t_ready"] + g * nb + j - before(j, k.banks) + 1)
                    for c in range(DC):
                        if j == 0:
                            pe.wait_ge(s["xl_ready"], k["xl_ready"] + g * DC + c + 1)
                        for n, part in enumerate((XH, XL)):
                            mm = pe.matmul(C[:, b * BANK:(b + 1) * BANK],
                                           W[:, c * hid + j * P:c * hid + (j + 1) * P],
                                           part[:, c * GTOK:(c + 1) * GTOK],
                                           start=(c == 0 and n == 0), stop=(c == DC - 1 and n == 1))
                    mm.then_inc(s["h_ready"], 1)

                def to_model(g, j):
                    if j == 0:
                        pe.wait_ge(s["resid"], k["resid"] + g)
                    pe.wait_ge(s["ul_ready"], k["ul_ready"] + g * nb + j + 1)
                    for t in range(GT):
                        for n, part in enumerate((UH[k.rings[j]], UL[k.rings[j]])):
                            mm = pe.matmul(B[:, t * D:(t + 1) * D], part[:, t * P:(t + 1) * P],
                                           V[:, j * D:(j + 1) * D],
                                           start=(j == 0 and n == 0 and t % 2 == 0),
                                           stop=(j == nb - 1 and n == 1), skip_group_check=True)
                    mm.then_inc(s["down_done"], 1)

                def group(g, last):
                    for j in range(nb):
                        if j + 2 < nb:
                            hidden(g, j + 2)
                        elif not last:
                            hidden(g + 1, j + 2 - nb)
                        if j + 3 == nb and not last:
                            transposes(k, g + 1)
                        elif j + 3 == nb and k.next:
                            transposes(k.next, 0)
                        to_model(g, j)

                if not k.primed:
                    transposes(k, 0)
                hidden(0, 0)
                hidden(0, 1)
                with pe.Fori(0, GROUPS - 1) as g:
                    group(g, False)
                group(GROUPS - 1, True)

            def qkv(k):
                a = k.att
                Wh, Wl = wqkv[k.layer]

                def group(g, last):
                    for t in range(GT):
                        pe.wait_ge(s["qkv_free"], k["qkv_free"] + g * GT + t - 1)
                        if t == 0:
                            pe.wait_ge(s["xl_ready"], k["xl_ready"] + g * DC + DC)
                        for lo in range(0, a.cols, BANK):
                            w, o = min(BANK, a.cols - lo), t % 2 * 2 * BANK + lo
                            for c in range(DC):
                                for n, (p, q) in enumerate(((XH, Wh), (XH, Wl), (XL, Wh))):
                                    mm = pe.matmul(C[:, o:o + w], p[:, c * GTOK + t * P:c * GTOK + (t + 1) * P],
                                                   q[:, c * a.cols + lo:c * a.cols + lo + w],
                                                   start=(c == 0 and n == 0), stop=(c == DC - 1 and n == 2))
                        mm.then_inc(s["qkv_ready"], 1)
                    if not last:
                        transposes(k, g + 1)

                if not k.primed:
                    transposes(k, 0)
                with pe.Fori(0, GROUPS - 1) as g:
                    group(g, False)
                group(GROUPS - 1, True)

            def att(k):
                a = k.att
                nset, nmax = len(a.sets), len(a.maxes)

                def turn(src, i, dst):
                    b = i // a.groups
                    at = b * (ST_ * 1024) + (i % a.groups) * a.qkw
                    at = at if isinstance(at, int) else pe.snap(at)
                    for p in range(a.tiles):
                        for t in range(ST_):
                            mm = pe.transpose(dst[:, :].bitcast(F16)[:, p * SEQ + t * P:p * SEQ + (t + 1) * P],
                                              view(src, at + (t * 1024 + p * P), (1, P)), ident16[:, :])
                    mm.then_inc(s["slot_full"], 1)

                def maximum(i, par, m, dst):
                    qt, heads = a.maxes[m]
                    if m == 0:
                        pe.wait_ge(s["q_copied"], k["q_copied"] + i + 1)
                        pe.wait_ge(s["k_copied"], k["k_copied"] + i + 1)
                    elif m == 1:
                        pe.wait_ge(s["on_ready"], k["on_ready"] + i - 1)
                    else:
                        pe.wait_ge(s["maxed"], k["maxed"] + i * nmax + m - 1)
                    keys, begun = a.keys(qt), []
                    for w in range(len(heads)):
                        o = w * a.width(qt) + keys - P
                        pe.matmul(dst[:, o:o + P], identb[:, :], maskb[:, :], start=o // BANK not in begun,
                                  stop=False, skip_group_check=True)
                        begun.append(o // BANK)
                    for w, h in enumerate(heads):
                        for lo in range(0, keys, BANK):
                            o, c = w * a.width(qt) + lo, min(BANK, keys - lo)
                            mm = pe.matmul(dst[:, o:o + c], QT1[:, qt * P:(qt + 1) * P],
                                           KT[par][:, h * SEQ + lo:h * SEQ + lo + c], start=o // BANK not in begun,
                                           stop=True, skip_group_check=True)
                            begun.append(o // BANK)
                    mm.then_inc(s["slot_full"], 1)

                def score(i, par, x, h):
                    st = x * HPG + h
                    pe.wait_ge(s["p_ready"], k["p_ready"] + i * (HPG * nset) + st - before(st, [n % 3 for n in range(HPG * nset)]) + 1)
                    if st == 0:
                        pe.wait_ge(s["qm_copied"], k["qm_copied"] + i + 1)
                    qh, kt = a.sets[x]
                    lo, b = a.first(x), st % 3
                    diagonal = a.diagonal(x)
                    if diagonal:
                        pe.matmul(C[:, b * BANK + lo:b * BANK + lo + P], identb[:, :], maskt[:, :],
                                  start=True, stop=False, skip_group_check=True)
                    pe.matmul(C[:, b * BANK + lo:(b + 1) * BANK], KT[par][:, h * SEQ + kt * P:h * SEQ + (kt + 1) * P],
                              QT2[par][:, qh * BANK + lo:(qh + 1) * BANK],
                              start=not diagonal, stop=True, skip_group_check=True).then_inc(s["st_ready"], 1)

                def values(i, par, x):
                    qh, kt = a.sets[x]
                    lo = a.first(x)
                    if x == 0:
                        pe.wait_ge(s["v_ready"], k["v_ready"] + i + 1)
                    if kt == 0:
                        pe.wait_ge(s["o_out"], k["o_out"] + i * 2 + qh)
                    pe.wait_ge(s["p_ready"], k["p_ready"] + i * (HPG * nset) + HPG * (x + 1))
                    for h in range(HPG):
                        v = (kt * a.vh + h % a.vh) * 32
                        mm = pe.matmul(C[32 * h:32 * h + 32, 3 * BANK + lo:4 * BANK], VG[par][:, v:v + 32],
                                       PR[x % 2][:, h * BANK + lo:(h + 1) * BANK],
                                       start=(kt == 0), stop=a.half_ends(x), skip_group_check=True,
                                       tile_position=(0, 32 * h))
                    mm.then_inc(s["pv_done"], 1)

                def turned_qm(i, dst):
                    pe.wait_ge(s["m_written"], k["m_written"] + i + 1)
                    pe.sem_inc(gate, 1)
                    turn(QA, i, dst)

                def turned_k(i, dst):
                    pe.wait_ge(s["qm_copied"], k["qm_copied"] + i)
                    pe.sem_inc(gate, 1)
                    turn(KA, i, dst)

                def half(i, par, ahead):
                    m = 0
                    for x in range(nset):
                        for h in range(HPG):
                            if x or h > 2:
                                score(i, par, x, h)
                            if x == nset - 2 and h == HPG - 1 and ahead:
                                turned_qm(i + 1, slot(i, a.m_use))
                            if x == nset - 1 and h == 1 and ahead > 1:
                                turn(QA, i + 2, slot(i, a.q_use))
                            while ahead and m < a.quota(x, h):
                                maximum(i + 1, 1 - par, m, slot(i, m))
                                m += 1
                        if x:
                            values(i, par, x - 1)
                    if ahead > 1:
                        turned_k(i + 2, slot(i, a.k_use))
                    values(i, par, nset - 1)
                    if ahead:
                        for h in range(3):
                            score(i + 1, 1 - par, 0, h)
                    if ahead > 1:
                        pe.wait_ge(s["q_copied"], k["q_copied"] + i + 3)
                    elif not ahead:
                        pe.wait_ge(s["qm_copied"], k["qm_copied"] + a.iters)
                    pe.wait_ge(s["o_out"], k["o_out"] + i * 2 + 2)
                    dst = slot(i, a.out_use(ahead))
                    for t in range(ST_):
                        mm = pe.transpose(dst[:, t * P:(t + 1) * P], OT[:, t * P:(t + 1) * P], ident[:, :])
                    mm.then_inc(s["slot_full"], 1)

                pe.wait_ge(s["qkv_free"], k["qkv_free"])
                pe.wait_ge(s["dup_done"], k["dup_done"])
                turn(QA, 0, slot(None, 0))
                turn(KA, 0, slot(None, 1))
                for m in range(nmax):
                    maximum(0, 0, m, slot(None, 2 + m))
                turned_qm(0, slot(None, nmax + 2))
                turn(QA, 1, slot(None, nmax + 3))
                turned_k(1, slot(None, nmax + 4))
                for h in range(3):
                    score(0, 0, 0, h)
                with pe.Fori(0, a.iters // 2 - 1) as r:
                    i = pe.snap(r * 2)
                    half(i, 0, 2)
                    half(i + 1, 1, 2)
                half(a.iters - 2, 0, 1)
                half(a.iters - 1, 1, 0)

            def mix(k):
                def bank_free(w, use, b):
                    pe.wait_ge(s[f"a{b}_read"], k[f"a{b}_read"] + w * 4 + use)

                def turn(seen, src, w, use, step):
                    at = w * (step * HEADS0)
                    for b in range(2):
                        bank_free(w, use, b)
                        pe.sem_inc(gate, 1)
                        for h in range(b * HALF, (b + 1) * HALF):
                            mm = pe.transpose(A[:, :].bitcast(F16)[:, h * P:(h + 1) * P],
                                              seen(src, at + h * step, (1, P)), ident16[:, :])
                        mm.then_inc(s["a_full"], 1)

                def turn_q(w):
                    turn(view, QA, w, 0, P)

                def turn_k(w):
                    turn(view, KA, w, 1, P)

                def turn_v(w):
                    turn(view16, VS, w, 2, P // 2)

                def blocks_v(w):
                    for u in range(2):
                        bank_free(w, 3, u)
                    for u in range(2):
                        for r in range(BLOCKS):
                            mm = pe.matmul(A[:, u * BANK + r * HD0:u * BANK + (r + 1) * HD0],
                                           QT1[32 * u:32 * u + 32, r * P:(r + 1) * P], two[32 * u:32 * u + 32, :],
                                           start=(r == 0), stop=True, skip_group_check=True)
                        mm.then_inc(s["a_full"], 1)

                def maximum(w, par, c):
                    if c == 0:
                        for b in range(2):
                            bank_free(w, 2, b)
                        pe.wait_ge(s["m_ready"], k["m_ready"] + w)
                    if c > 1:
                        pe.wait_ge(s["maxed"], k["maxed"] + w * CHUNKS + c - 1)
                    for n in range(CHUNK):
                        x = c * CHUNK + n
                        o, r = (c % 2 * CHUNK + n) * P, x % BLOCKS * P
                        mm = pe.matmul(B[:, o:o + P], QT2[par][:, r:r + P], KT[par][:, x * P:(x + 1) * P],
                                       start=(n == 0), stop=True, skip_group_check=True)
                    mm.then_inc(s["b_full"], 1)

                def turn_m(w):
                    pe.wait_ge(s["maxed"], k["maxed"] + (w + 1) * CHUNKS)
                    pe.transpose(B[0:2 * BLOCKS, 0:P], NM[:, :], ident[:, :]).then_inc(s["b_full"], 1)

                def score(w, par, c):
                    if c == 0:
                        pe.wait_ge(s["m_ready"], k["m_ready"] + w + 1)
                    pe.wait_ge(s["p_ready"], k["p_ready"] + w * CHUNKS + c - 1)
                    for n in range(CHUNK):
                        o = (c % 2 * CHUNK + n) * P
                        pe.matmul(C[:, o:o + P], view(identb, c * CHUNK + n, (0, P)), MT[par][:, :],
                                  start=(n == 0), stop=False, skip_group_check=True)
                    for n in range(CHUNK):
                        x = c * CHUNK + n
                        o, r = (c % 2 * CHUNK + n) * P, x % BLOCKS * P
                        mm = pe.matmul(C[:, o:o + P], KT[par][:, x * P:(x + 1) * P], QT2[par][:, r:r + P],
                                       start=False, stop=True, skip_group_check=True)
                    mm.then_inc(s["st_ready"], 1)

                def values(w, par, c):
                    if c == 0:
                        for b in range(2):
                            bank_free(w, 4, b)
                    if c % CHUNK == 0:
                        pe.wait_ge(s["o_out"], k["o_out"] + w * 2 + c // CHUNK)
                    pe.wait_ge(s["p_ready"], k["p_ready"] + w * CHUNKS + c + 1)
                    for n in range(CHUNK):
                        o, v = 2 * BANK + c % CHUNK * P, (c * CHUNK + n) * 32
                        mm = pe.matmul(C[32 * n:32 * n + 32, o:o + P], VG[par][:, v:v + 32],
                                       PR[c // CHUNK][:, (c % CHUNK * CHUNK + n) * P:(c % CHUNK * CHUNK + n + 1) * P],
                                       start=(c % CHUNK == 0), stop=True, skip_group_check=True,
                                       tile_position=(0, 32 * n))
                    mm.then_inc(s["pv_done"], 1)

                def turn_sums(w, u):
                    pe.wait_ge(s["o_out"], k["o_out"] + w * 2 + u + 1)
                    pe.wait_ge(s["ol_ready"], k["ol_ready"] + w * 2 + u)
                    for n in range(4):
                        mm = pe.transpose(C[:, 3 * BANK + n * P:3 * BANK + (n + 1) * P],
                                          OT[:, u * BANK + n * P:u * BANK + (n + 1) * P], ident[:, :])
                    mm.then_inc(s["ot_full"], 1)

                def turn_out(w, u):
                    pe.wait_ge(s["on_ready"], k["on_ready"] + w * 2 + u + 1)
                    for c in range(DC):
                        mm = pe.transpose(C[:, 3 * BANK + c * P:3 * BANK + (c + 1) * P],
                                          ON[:, u * D + c * P:u * D + (c + 1) * P], ident[:, :])
                    mm.then_inc(s["on_turned"], 1)

                def half(w, par, more):
                    n, other = w + 1, 1 - par
                    score(w, par, 0)
                    score(w, par, 1)
                    if more:
                        turn_q(n)
                    values(w, par, 0)
                    score(w, par, 2)
                    if more:
                        turn_k(n)
                    values(w, par, 1)
                    score(w, par, 3)
                    values(w, par, 2)
                    score(w, par, 4)
                    if more:
                        turn_v(n)
                    values(w, par, 3)
                    score(w, par, 5)
                    if more:
                        maximum(n, other, 0)
                        maximum(n, other, 1)
                    values(w, par, 4)
                    score(w, par, 6)
                    if more:
                        blocks_v(n)
                        maximum(n, other, 2)
                    values(w, par, 5)
                    score(w, par, 7)
                    turn_sums(w, 0)
                    if more:
                        maximum(n, other, 3)
                    values(w, par, 6)
                    if more:
                        maximum(n, other, 4)
                    turn_out(w, 0)
                    values(w, par, 7)
                    if more:
                        for c in range(5, CHUNKS):
                            maximum(n, other, c)
                        turn_m(n)
                    turn_sums(w, 1)
                    turn_out(w, 1)

                pe.wait_ge(s["qkv_free"], k["qkv_free"])
                pe.wait_ge(s["dup_done"], k["dup_done"])
                turn_q(0)
                turn_k(0)
                turn_v(0)
                blocks_v(0)
                for c in range(CHUNKS):
                    maximum(0, 0, c)
                turn_m(0)
                with pe.Fori(0, MIXES // 2 - 1) as r:
                    w = pe.snap(r * 2)
                    half(w, 0, True)
                    half(w + 1, 1, True)
                half(MIXES - 2, 0, True)
                half(MIXES - 1, 1, False)

            def outward(k):
                Wh, Wl = wo[k.layer]
                pe.wait_ge(s["ol_ready"], k["ol_ready"])
                pe.wait_ge(s["oh_ready"], k["oh_ready"])

                def group(g):
                    pe.wait_ge(s["resid"], k["resid"] + g)
                    for t in range(GT):
                        for c in range(DC):
                            for n, (p, q) in enumerate(((AH, Wh), (AH, Wl), (AL, Wh))):
                                mm = pe.matmul(B[:, t * D:(t + 1) * D], view(p, g * GTOK + (c * TOK + t * P), (1, P)),
                                               q[:, c * D:(c + 1) * D], start=(c == 0 and n == 0 and t % 2 == 0),
                                               stop=(c == DC - 1 and n == 2), skip_group_check=True)
                    mm.then_inc(s["y_ready"], 1)

                with pe.Fori(0, GROUPS - 1) as g:
                    group(g)
                group(GROUPS - 1)
                transposes(k.next, 0)

            def proj(k):
                Wh, Wl = wo[k.layer]
                pe.wait_ge(s["ao_ready"], k["ao_ready"])
                with pe.Fori(0, GROUPS) as g:
                    for part, src in enumerate((AH, AL)):
                        for c in range(DC):
                            for t in range(GT):
                                o = part * 2 * BANK + c * GTOK + t * P
                                mm = pe.transpose(A[:, :].bitcast(F16)[:, o:o + P],
                                                  view(src, g * (GT * D) + (t * D + c * P), (1, P)), ident16[:, :])
                        mm.then_inc(s["at_ready"], 1)
                    pe.wait_ge(s["ah_copied"], k["ah_copied"] + g + 1)
                    pe.wait_ge(s["al_copied"], k["al_copied"] + g + 1)
                    pe.wait_ge(s["resid"], k["resid"] + g)
                    for t in range(GT):
                        for c in range(DC):
                            for n, (p, q) in enumerate(((XH, Wh), (XH, Wl), (XL, Wh))):
                                mm = pe.matmul(B[:, t * D:(t + 1) * D], p[:, c * GTOK + t * P:c * GTOK + (t + 1) * P],
                                               q[:, c * D:(c + 1) * D], start=(c == 0 and n == 0 and t % 2 == 0),
                                               stop=(c == DC - 1 and n == 2), skip_group_check=True)
                    mm.then_inc(s["y_ready"], 1)

            pe.wait_ge(const_ready, 8)
            pe.wait_ge(sums_ready, 1)
            pe.matmul(C[:, 0:4], ones[:, :], sums[:, :], start=True, stop=True).then_inc(tot_ready, 1)
            pe.wait_ge(w_ready, 1)
            for k in phases:
                if k.layer == 1:
                    pe.wait_ge(ternary_1, 2)
                {"ffn": ffn, "qkv": qkv, "mix": mix, "out": outward, "att": att, "proj": proj}[k.kind](k)

        @block.scalar
        def _(act):
            def split_high(k, g):
                for c in range(DC):
                    act.wait_ge(s["xt_ready"], k["xt_ready"] + g * DC + c + 1)
                    nc.scalar.activation(XH[:, c * GTOK:(c + 1) * GTOK], A[:, c * BANK:(c + 1) * BANK],
                                         ACT.Copy).then_inc(s["xh_ready"], 1)

            def ffn(k):
                def group(g, last):
                    for j in range(k.nb):
                        n, b, t = g * k.nb + j, k.banks[j], k.rings[j]
                        act.wait_ge(s["h_ready"], k["h_ready"] + n + 1)
                        act.wait_ge(s["down_done"], k["down_done"] + n - before(j, k.rings) + 1)
                        src = C[:, b * BANK:(b + 1) * BANK]
                        if k.layer == 0:
                            nc.scalar.activation(T[t], src, ACT.Relu, scale=RSCALE).then_inc(s["t_ready"], 1)
                            act.wait_ge(s["t_ready"], k["t_ready"] + n + 1)
                            nc.scalar.activation(U[t], T[t], ACT.Square).then_inc(s["u_done"], 1)
                            act.wait_ge(s["u_done"], k["u_done"] + n + 1)
                        else:
                            nc.scalar.activation(T[t], src, ACT.Gelu, bias=b1s[:, j:j + 1]).then_inc(s["t_ready"], 1)
                            act.wait_ge(s["t_ready"], k["t_ready"] + n + 1)
                        nc.scalar.activation(UH[t], (U if k.layer == 0 else T)[t], ACT.Copy).then_inc(s["uh_ready"], 1)
                        if j + 2 == k.nb and not last:
                            split_high(k, g + 1)
                        elif j + 2 == k.nb and k.next:
                            split_high(k.next, 0)

                nc.scalar.preload_act_table(ACT.Exp if k.layer == 0 else ACT.Gelu)
                if not k.primed:
                    split_high(k, 0)
                with act.Fori(0, GROUPS - 1) as g:
                    group(g, False)
                group(GROUPS - 1, True)

            def qkv(k):
                a = k.att

                def group(g, last):
                    for t in range(GT):
                        act.wait_ge(s["qkv_ready"], k["qkv_ready"] + g * GT + t + 1)
                        o = t % 2 * 2 * BANK
                        at, row = a.at(g, t), a.step * (HPG // a.vh)
                        nc.scalar.activation(view(QA, at, (a.step, a.heads), (1, a.hd)),
                                             view(C, o, (a.hd, a.heads), (1, a.hd)), ACT.Copy, scale=1 / WSCALE)
                        nc.scalar.activation(view(KA, at, (row, a.kv), (1, a.hd)),
                                             view(C, o + D, (a.hd, a.kv), (1, a.hd)), ACT.Copy, scale=1 / WSCALE)
                        if k.layer == 0:
                            dst = view16(VS, a.v_at(g, t), (4 * a.hd, a.kv), (1, a.hd))
                        else:
                            dst = view(VS, a.v_at(g, t), (a.hd, a.kv), (1, a.hd))
                        nc.scalar.activation(dst, view(C, o + D + a.kvw, (a.hd, a.kv), (1, a.hd)), ACT.Copy,
                                             scale=1 / WSCALE).then_inc(s["hi_ready"], 1)
                    if not last:
                        split_high(k, g + 1)
                    elif k.next:
                        split_high(k.next, 0)

                if not k.primed:
                    split_high(k, 0)
                act.wait_ge(pad_ready, 2 + k.layer)
                with act.Fori(0, GROUPS - 1) as g:
                    group(g, False)
                group(GROUPS - 1, True)

            def att(k):
                a = k.att
                nset = len(a.sets)

                def await_slot(i, n):
                    act.wait_ge(s["slot_full"], k["slot_full"] + a.full(i, n))

                def copy_qm(i, n, dst):
                    await_slot(i, n)
                    nc.scalar.activation(dst[:, 0:SEQ], slot(i, n)[:, :].bitcast(F16)[:, 0:SEQ],
                                         ACT.Copy).then_inc(s["qm_copied"], 1)

                def drain(i, x):
                    qh = a.sets[x][0]
                    act.wait_ge(s["pv_done"], k["pv_done"] + i * nset + x + 1)
                    if qh == 0:
                        act.wait_ge(s["slot_full"], k["slot_full"] + a.full(i, -1))
                    nc.scalar.activation(OT[:, qh * BANK:(qh + 1) * BANK], C[:, 3 * BANK:4 * BANK],
                                         ACT.Copy).then_inc(s["o_out"], 1)

                def half(i, par, ahead):
                    for x in range(nset):
                        lo = a.first(x)
                        act.wait_ge(s["pv_done"], k["pv_done"] + i * nset + x - 1)
                        for h in range(HPG):
                            st = x * HPG + h
                            b = st % 3
                            act.wait_ge(s["st_ready"], k["st_ready"] + i * (HPG * nset) + st + 1)
                            nc.scalar.activation(PR[x % 2][:, h * BANK + lo:(h + 1) * BANK],
                                                 C[:, b * BANK + lo:(b + 1) * BANK], ACT.Exp,
                                                 scale=a.scale).then_inc(s["p_ready"], 1)
                        if x and a.half_ends(x - 1):
                            drain(i, x - 1)
                        if x == nset - 2 and ahead:
                            copy_qm(i, a.m_use, QT2[1 - par])
                    drain(i, nset - 1)

                nc.scalar.preload_act_table(ACT.Exp)
                copy_qm(None, a.lead - 3, QT2[0])
                with act.Fori(0, a.iters // 2 - 1) as r:
                    i = act.snap(r * 2)
                    half(i, 0, 2)
                    half(i + 1, 1, 2)
                half(a.iters - 2, 0, 1)
                half(a.iters - 1, 1, 0)

            def mix(k):
                def turned(w, use, dst, rows):
                    return nc.scalar.activation(by_block(dst, 0), by_head(A, rows, 0), ACT.Copy)

                def a_filled(w, use):
                    act.wait_ge(s["a_full"], k["a_full"] + w * 8 + 2 * use + 1)

                def turned_q(w, par):
                    a_filled(w, 0)
                    turned(w, 0, QT2[par][:, :], slice(0, P)).then_inc(s["a0_read"], 1)

                def turned_k(w, par):
                    a_filled(w, 1)
                    for u in range(2):
                        rows = slice(64 * u, 64 * u + 64)
                        op = turned(w, 1, KT[par][rows, u * BLOCKS * P:(u + 1) * BLOCKS * P], rows)
                    op.then_inc(s["a0_read"], 1)

                def turned_v(w):
                    a_filled(w, 2)
                    turned(w, 2, QT1[0:64, :], slice(0, 64)).then_inc(s["a0_read"], 1)

                def blocks_v(w, par):
                    a_filled(w, 3)
                    nc.scalar.activation(view(VG[par], 0, (32, BLOCKS), (1, HD0)),
                                         view(A, 0, (HD0, BLOCKS), (1, HD0)), ACT.Copy).then_inc(s["a0_read"], 1)

                def exps(w, c):
                    act.wait_ge(s["pv_done"], k["pv_done"] + w * CHUNKS + c - CHUNKS + 1)
                    act.wait_ge(s["st_ready"], k["st_ready"] + w * CHUNKS + c + 1)
                    o = c % CHUNK * BANK
                    nc.scalar.activation(PR[c // CHUNK][:, o:o + BANK], C[:, c % 2 * BANK:(c % 2 + 1) * BANK],
                                         ACT.Exp, scale=k.att.scale).then_inc(s["p_ready"], 1)

                def sums_out(w, u):
                    act.wait_ge(s["pv_done"], k["pv_done"] + w * CHUNKS + (u + 1) * CHUNK)
                    act.wait_ge(s["ot_full"], k["ot_full"] + w * 2 + u - 1 + 1)
                    nc.scalar.activation(OT[:, u * BANK:(u + 1) * BANK], C[:, 2 * BANK:3 * BANK],
                                         ACT.Copy).then_inc(s["o_out"], 1)

                def high(w, u):
                    act.wait_ge(s["on_turned"], k["on_turned"] + w * 2 + u + 1)
                    t = w * 2 + u
                    at = (t // ST_) * SEQ + (t % ST_) * NEAR
                    for c in range(DC):
                        op = nc.scalar.activation(view(AH, at + c * TOK, (SEQ // HEADS0, HEADS0), (1, NEAR)),
                                                  view(C, 3 * BANK + c * P, (NEAR, HEADS0), (1, NEAR)), ACT.Copy)
                    op.then_inc(s["oh_ready"], 1)

                def half(w, par, more):
                    n, other = w + 1, 1 - par
                    exps(w, 0)
                    exps(w, 1)
                    if more:
                        turned_q(n, other)
                    exps(w, 2)
                    if more:
                        turned_k(n, other)
                    exps(w, 3)
                    exps(w, 4)
                    if more:
                        turned_v(n)
                    sums_out(w, 0)
                    exps(w, 5)
                    exps(w, 6)
                    if more:
                        blocks_v(n, other)
                    exps(w, 7)
                    high(w, 0)
                    sums_out(w, 1)
                    high(w, 1)

                nc.scalar.preload_act_table(ACT.Exp)
                turned_q(0, 0)
                turned_k(0, 0)
                turned_v(0)
                blocks_v(0, 0)
                with act.Fori(0, MIXES // 2 - 1) as r:
                    w = act.snap(r * 2)
                    half(w, 0, True)
                    half(w + 1, 1, True)
                half(MIXES - 2, 0, True)
                half(MIXES - 1, 1, False)

            def outward(k):
                split_high(k.next, 0)

            def proj(k):
                with act.Fori(0, GROUPS) as g:
                    act.wait_ge(s["at_ready"], k["at_ready"] + g * 2 + 1)
                    nc.scalar.activation(XH, A[:, 0:BANK].bitcast(F16), ACT.Copy).then_inc(s["ah_copied"], 1)

            act.wait_ge(w_in, 16 * 7)
            for n, (_, src, dst) in enumerate(split):
                nc.scalar.activation(dst[0][:, :], src, ACT.Copy, scale=WSCALE).then_inc(high_done, 1)
            for k in phases:
                {"ffn": ffn, "qkv": qkv, "mix": mix, "out": outward, "att": att, "proj": proj}[k.kind](k)

        @block.vector
        def _(dve):
            def statistics(k, g):
                for t in range(GT):
                    st = nc.vector.bn_stats(bn[:, t * 6:(t + 1) * 6], view(X, g * (GT * D) + t * D, (1, D)))
                st.then_inc(s["stats_done"], 1)
                dve.wait_ge(s["stats_done"], k["stats_done"] + g + 1)
                dve.sem_inc(gate, 1)
                for t in range(GT):
                    ag = nc.vector.bn_aggr(mv[:, t * 2:(t + 1) * 2], bn[:, t * 6:(t + 1) * 6])
                ag.then_inc(s["var_ready"], 1)

            def normalise(k, g):
                dve.wait_ge(s["rstd_ready"], k["rstd_ready"] + g + 1)
                for t in range(GT):
                    op = nc.vector.tensor_scalar(XN[:, t * D:(t + 1) * D], view(X, g * (GT * D) + t * D, (1, D)),
                                                 mv[:, t * 2:t * 2 + 1], rstd[:, t:t + 1], ALU.subtract, ALU.mult)
                op.then_inc(s["xn_ready"], 1)

            def split_low(k, g):
                for c in range(DC):
                    dve.wait_ge(s["xh_ready"], k["xh_ready"] + g * DC + c + 1)
                    nc.vector.tensor_tensor(XL[:, c * GTOK:(c + 1) * GTOK], A[:, c * BANK:(c + 1) * BANK],
                                            XH[:, c * GTOK:(c + 1) * GTOK], ALU.subtract).then_inc(s["xl_ready"], 1)

            def first_group(k):
                if not k.primed:
                    statistics(k, 0)
                    normalise(k, 0)
                    split_low(k, 0)

            def add_to_x(g, scale):
                for n in range(2):
                    xs = view(X, g * (GT * D) + n * BANK, (1, BANK))
                    op = nc.vector.scalar_tensor_tensor(out=xs, in0=B[:, n * BANK:(n + 1) * BANK], scalar=scale,
                                                        in1=xs, op0=ALU.mult, op1=ALU.add)
                op.then_inc(s["resid"], 1)

            def ffn(k):
                def group(g, left):
                    follow = [(k, g + n) if n <= left else (k.next, 0) if n == left + 1 and k.next else None
                              for n in (1, 2)]
                    for j in range(k.nb):
                        n, t = g * k.nb + j, k.rings[j]
                        dve.wait_ge(s["uh_ready"], k["uh_ready"] + n + 1)
                        nc.vector.tensor_tensor(UL[t], (U if k.layer == 0 else T)[t], UH[t], ALU.subtract)\
                            .then_inc(s["ul_ready"], 1)
                        if j == 1 and follow[0]:
                            normalise(*follow[0])
                        if j + 2 == k.nb and follow[0]:
                            split_low(*follow[0])
                        if j + 2 == k.nb and follow[1]:
                            if left == 1:
                                dve.wait_ge(s["resid"], k["resid"] + 1)
                            statistics(*follow[1])
                    dve.wait_ge(s["down_done"], k["down_done"] + (g + 1) * k.nb)
                    if k.layer == 1:
                        dve.wait_ge(s["bias_added"], k["bias_added"] + g + 1)
                    add_to_x(g, sc[:, 1:2] if k.layer == 0 else 0.5)

                dve.wait_ge(s["resid"], k["resid"])
                first_group(k)
                statistics(k, 1)
                with dve.Fori(0, GROUPS - 2) as g:
                    group(g, 2)
                group(GROUPS - 2, 1)
                group(GROUPS - 1, 0)

            def qkv(k):
                a = k.att

                def low(dst, o, at, row, heads, part):
                    return nc.vector.scalar_tensor_tensor(
                        out=view(dst, at + part * a.hd, (row, heads), (1, a.hd)),
                        in0=view(C, o, (a.hd, heads), (1, a.hd)), scalar=1 / WSCALE,
                        in1=view(dst, at, (row, heads), (1, a.hd)), op0=ALU.mult, op1=ALU.subtract)

                def group(g, last):
                    for t in range(GT):
                        dve.wait_ge(s["hi_ready"], k["hi_ready"] + g * GT + t + 1)
                        o, at = t % 2 * 2 * BANK, a.at(g, t)
                        low(QA, o, at, a.step, a.heads, 1)
                        op = low(KA, o + D, at, a.step * (HPG // a.vh), a.kv, 2)
                        if k.layer == 0:
                            v_at = a.v_at(g, t)
                            op = nc.vector.scalar_tensor_tensor(
                                out=view16(VS, v_at + a.hd, (4 * a.hd, a.kv), (1, a.hd)),
                                in0=view(C, o + 2 * D, (a.hd, a.kv), (1, a.hd)), scalar=1 / WSCALE,
                                in1=view16(VS, v_at, (4 * a.hd, a.kv), (1, a.hd)), op0=ALU.mult, op1=ALU.subtract)
                        op.then_inc(s["qkv_free"], 1)
                        if t == 0 and not last:
                            statistics(k, g + 1)
                        if t == 2 and not last:
                            normalise(k, g + 1)
                    if not last:
                        split_low(k, g + 1)

                dve.wait_ge(s["resid"], k["resid"])
                first_group(k)
                with dve.Fori(0, GROUPS - 1) as g:
                    group(g, False)
                group(GROUPS - 1, True)

            def att(k):
                a = k.att
                nmax = len(a.maxes)

                def place(i, of_batch, of_group):
                    b = i // a.groups
                    at = b * of_batch + (i % a.groups) * of_group
                    return at if isinstance(at, int) else dve.snap(at)

                def maximum(i, m, full, dst):
                    qt, heads = a.maxes[m]
                    dve.wait_ge(s["slot_full"], full)
                    src = view(dst, 0, (a.width(qt), len(heads)), (1, a.keys(qt)))
                    c = qt * HPG + heads[0]
                    nc.vector.tensor_reduce(NM[:, c:c + len(heads)], src, AX_X, ALU.max,
                                            negate=True).then_inc(s["maxed"], 1)

                def copy_q(i, n):
                    dve.wait_ge(s["slot_full"], k["slot_full"] + a.full(i, n))
                    nc.vector.tensor_copy(QT1[:, 0:SEQ], slot(i, n)[:, :].bitcast(F16)[:, 0:SEQ])\
                        .then_inc(s["q_copied"], 1)

                def copy_k(i, n, par):
                    dve.wait_ge(s["slot_full"], k["slot_full"] + a.full(i, n))
                    for h in range(HPG):
                        op = nc.vector.tensor_copy(KT[par][h * a.row:(h + 1) * a.row, h * SEQ:(h + 1) * SEQ],
                                                   slot(i, n)[0:a.row, :].bitcast(F16)[:, 0:SEQ])
                    op.then_inc(s["k_copied"], 1)

                def maxima(i, at, n0):
                    dve.wait_ge(s["m_written"], k["m_written"] + i)
                    for m in range(nmax):
                        maximum(i, m, k["slot_full"] + a.full(at, n0 + m), slot(at, n0 + m))
                    at = place(i, ST_ * 1024, a.qkw)
                    dve.wait_ge(s["maxed"], k["maxed"] + (i + 1) * nmax)
                    nm = view(NM, 0, (HPG, ST_), (1, HPG))
                    mh = view(QA, at + 3 * a.hd, (1024, ST_), (a.row, HPG))
                    nc.vector.tensor_copy(mh, nm).then_inc(s["mh_done"], 1)
                    dve.wait_ge(s["mh_done"], k["mh_done"] + i + 1)
                    nc.vector.tensor_tensor(view(QA, at + (3 * a.hd + 1), (1024, ST_), (a.row, HPG)), nm, mh,
                                            ALU.subtract).then_inc(s["m_written"], 1)

                def divide(i, n):
                    dve.wait_ge(s["slot_full"], k["slot_full"] + a.full(i, n))
                    dve.wait_ge(s["ao_ready"], k["ao_ready"] + i)
                    src = slot(i, n)
                    nc.vector.reciprocal(view(RD, 0, (HPG, ST_), (1, HPG)),
                                         view(src, a.hd, (P, ST_), (32, HPG))).then_inc(s["rd_done"], 1)
                    dve.wait_ge(s["rd_done"], k["rd_done"] + i + 1)
                    nc.vector.tensor_tensor(view(ON, 0, (HPG * a.hd, ST_), (a.hd, HPG), (1, a.hd)),
                                            view(src, 0, (P, ST_), (32, HPG), (1, a.hd)),
                                            view(RD, 0, (HPG, ST_), (1, HPG), (0, a.hd)),
                                            ALU.mult).then_inc(s["on_ready"], 1)

                def half(i, par, ahead):
                    if ahead:
                        maxima(i + 1, i, 0)
                    if ahead > 1:
                        copy_q(i, a.q_use)
                        copy_k(i, a.k_use, par)
                    divide(i, a.out_use(ahead))

                copy_q(None, 0)
                copy_k(None, 1, 0)
                maxima(0, None, 2)
                copy_q(None, a.lead - 2)
                copy_k(None, a.lead - 1, 1)
                with dve.Fori(0, a.iters // 2 - 1) as r:
                    i = dve.snap(r * 2)
                    half(i, 0, 2)
                    half(i + 1, 1, 2)
                half(a.iters - 2, 0, 1)
                half(a.iters - 1, 1, 0)

            def mix(k):
                def turned(w, use, dst, rows):
                    return nc.vector.tensor_copy(by_block(dst, 1), by_head(A, rows, 1))

                def a_filled(w, use):
                    dve.wait_ge(s["a_full"], k["a_full"] + w * 8 + 2 * use + 2)

                def turned_q(w, par):
                    a_filled(w, 0)
                    turned(w, 0, QT2[par][:, :], slice(0, P)).then_inc(s["a1_read"], 1)

                def turned_k(w, par):
                    a_filled(w, 1)
                    for u in range(2):
                        rows = slice(64 * u, 64 * u + 64)
                        op = turned(w, 1, KT[par][rows, u * BLOCKS * P:(u + 1) * BLOCKS * P], rows)
                    op.then_inc(s["a1_read"], 1)

                def turned_v(w):
                    a_filled(w, 2)
                    turned(w, 2, QT1[0:64, :], slice(0, 64)).then_inc(s["a1_read"], 1)

                def blocks_v(w, par):
                    a_filled(w, 3)
                    nc.vector.tensor_copy(view(VG[par], 32 * BLOCKS, (32, BLOCKS), (1, HD0)),
                                          view(A, BANK, (HD0, BLOCKS), (1, HD0))).then_inc(s["a1_read"], 1)

                def maximum(w, c):
                    dve.wait_ge(s["b_full"], k["b_full"] + w * (CHUNKS + 1) + c + 1)
                    nc.vector.tensor_reduce(NM[:, c * CHUNK:(c + 1) * CHUNK],
                                            view(B, c % 2 * BANK, (P, CHUNK), (1, P)), AX_X, ALU.max,
                                            negate=True).then_inc(s["maxed"], 1)

                def turned_m(w, par):
                    dve.wait_ge(s["b_full"], k["b_full"] + (w + 1) * (CHUNKS + 1))
                    nc.vector.tensor_copy(MT[par][0:2 * BLOCKS, :], B[0:2 * BLOCKS, 0:P]).then_inc(s["m_ready"], 1)

                def divide(w, u):
                    dve.wait_ge(s["ot_full"], k["ot_full"] + w * 2 + u + 1)
                    nc.vector.reciprocal(RD[:, u * BLOCKS:(u + 1) * BLOCKS], view(C, 3 * BANK + HD0, (32, BLOCKS)))\
                        .then_inc(s["rd_done"], 1)
                    dve.wait_ge(s["rd_done"], k["rd_done"] + w * 2 + u + 1)
                    nc.vector.tensor_tensor(view(ON, u * D, (HD0, BLOCKS), (1, HD0)),
                                            view(C, 3 * BANK, (32, BLOCKS), (1, HD0)),
                                            view(RD, u * BLOCKS, (1, BLOCKS), (0, HD0)),
                                            ALU.mult).then_inc(s["on_ready"], 1)

                def low(w, u):
                    dve.wait_ge(s["oh_ready"], k["oh_ready"] + w * 2 + u + 1)
                    t = w * 2 + u
                    at = (t // ST_) * SEQ + (t % ST_) * NEAR
                    for c in range(DC):
                        op = nc.vector.tensor_tensor(view(AL, at + c * TOK, (SEQ // HEADS0, HEADS0), (1, NEAR)),
                                                     view(C, 3 * BANK + c * P, (NEAR, HEADS0), (1, NEAR)),
                                                     view(AH, at + c * TOK, (SEQ // HEADS0, HEADS0), (1, NEAR)),
                                                     ALU.subtract)
                    op.then_inc(s["ol_ready"], 1)

                def half(w, par, more):
                    n, other = w + 1, 1 - par
                    if more:
                        turned_q(n, other)
                        turned_k(n, other)
                        turned_v(n)
                        maximum(n, 0)
                        maximum(n, 1)
                        blocks_v(n, other)
                        maximum(n, 2)
                    divide(w, 0)
                    if more:
                        maximum(n, 3)
                        maximum(n, 4)
                    low(w, 0)
                    if more:
                        for c in range(5, CHUNKS):
                            maximum(n, c)
                        turned_m(n, other)
                    divide(w, 1)
                    low(w, 1)

                dve.wait_ge(v_pad, 4)
                turned_q(0, 0)
                turned_k(0, 0)
                turned_v(0)
                blocks_v(0, 0)
                for c in range(CHUNKS):
                    maximum(0, c)
                turned_m(0, 0)
                with dve.Fori(0, MIXES // 2 - 1) as r:
                    w = dve.snap(r * 2)
                    half(w, 0, True)
                    half(w + 1, 1, True)
                half(MIXES - 2, 0, True)
                half(MIXES - 1, 1, False)

            def outward(k):
                def group(g):
                    dve.wait_ge(s["y_ready"], k["y_ready"] + g + 1)
                    add_to_x(g, 1 / WSCALE)

                with dve.Fori(0, GROUPS - 1) as g:
                    group(g)
                dve.wait_ge(s["resid"], k["resid"] + 1)
                statistics(k.next, 0)
                normalise(k.next, 0)
                group(GROUPS - 1)
                split_low(k.next, 0)

            def proj(k):
                with dve.Fori(0, GROUPS) as g:
                    dve.wait_ge(s["at_ready"], k["at_ready"] + g * 2 + 2)
                    nc.vector.tensor_copy(XL, A[:, BANK:2 * BANK].bitcast(F16)).then_inc(s["al_copied"], 1)
                    dve.wait_ge(s["y_ready"], k["y_ready"] + g + 1)
                    add_to_x(g, 1 / WSCALE)

            steps = [0]

            def step(op):
                steps[0] += 1
                op.then_inc(setup_step, 1)
                dve.wait_ge(setup_step, steps[0])

            dve.wait_ge(ffn_w_in, 16 * 4)
            for n, (_, src, _) in enumerate(quant):
                op = nc.vector.tensor_reduce(sums[:, n:n + 1], src, AX_X, ALU.add, apply_absolute_value=True)
            op.then_inc(sums_ready, 1)
            dve.wait_ge(tot_ready, 1)
            for k, (floor, cut) in enumerate(((1e-5, 0.7), (1e-8, 0.5))):
                c = slice(2 * k, 2 * k + 2)
                size = float(D * HID[k])
                step(nc.vector.tensor_scalar(means[:, c], C[:, c], 1 / size, floor, ALU.mult, ALU.max))
                nc.vector.tensor_scalar(lim[:, c], means[:, c], cut, None, ALU.mult)
                step(nc.vector.tensor_scalar(lim[:, 4 + 2 * k:6 + 2 * k], means[:, c], -cut, None, ALU.mult))
            step(nc.vector.tensor_tensor(sc[:, 0:1], means[:, 0:1], means[:, 0:1], ALU.mult))
            step(nc.vector.tensor_scalar(sc[:, 1:2], sc[:, 0:1], means[:, 1:2], 0.5 / RSCALE ** 2, ALU.mult, ALU.mult))
            for n, (w, src, dst) in enumerate(quant[:2]):
                step(nc.vector.tensor_scalar(dst[:, :], src, lim[:, 4 + n:5 + n], None, ALU.is_lt))
                step(nc.vector.scalar_tensor_tensor(out=dst[:, :], in0=src, scalar=lim[:, n:n + 1], in1=dst[:, :],
                                                    op0=ALU.is_gt, op1=ALU.subtract))
            for n, (_, src, dst) in enumerate(split):
                dve.wait_ge(high_done, n + 1)
                nc.vector.scalar_tensor_tensor(out=dst[1][:, :], in0=src, scalar=WSCALE, in1=dst[0][:, :],
                                               op0=ALU.mult, op1=ALU.subtract)
            nc.vector.tensor_scalar(b2h[:, :], b2h[:, :], 0.5, None, ALU.mult).then_inc(w_ready, 1)
            dve.wait_ge(x_in, 16 * GROUPS)
            for k in phases:
                {"ffn": ffn, "qkv": qkv, "mix": mix, "out": outward, "att": att, "proj": proj}[k.kind](k)

        @block.gpsimd
        def _(pool):
            def rsqrt(k, g):
                pool.wait_ge(s["var_ready"], k["var_ready"] + g + 1)
                nc.gpsimd.tensor_tensor(var[:, :], view(mv, 1, (2, GT)), eps[:, :], ALU.add).then_inc(s["eps_done"], 1)
                pool.wait_ge(s["eps_done"], k["eps_done"] + g + 1)
                nc.gpsimd.tensor_tensor(rstd[:, :], var[:, :], mhalf[:, :], ALU.pow).then_inc(s["rstd_ready"], 1)

            def ternary(n):
                _, src, dst = quant[n]
                nc.gpsimd.tensor_scalar(dst[:, :], src, lim[:, 4 + n:5 + n], None, ALU.is_lt)\
                    .then_inc(ternary_step, 1)
                pool.wait_ge(ternary_step, 2 * n - 3)
                nc.gpsimd.tensor_scalar(src, src, lim[:, n:n + 1], None, ALU.is_gt).then_inc(ternary_step, 1)
                pool.wait_ge(ternary_step, 2 * n - 2)
                nc.gpsimd.tensor_tensor(dst[:, :], src, dst[:, :], ALU.subtract).then_inc(ternary_1, 1)

            def ffn(k):
                def group(g, last):
                    if k.layer == 1:
                        pool.wait_ge(s["xn_ready"], k["xn_ready"] + g + 1)
                        xs = view(X, g * (GT * D), (D, GT), (1, D))
                        nc.gpsimd.tensor_tensor(xs, xs, view(b2h, 0, (0, GT), (1, D)), ALU.add)\
                            .then_inc(s["bias_added"], 1)
                    if not last:
                        rsqrt(k, g + 1)
                    elif k.next:
                        rsqrt(k.next, 0)

                if not k.primed:
                    rsqrt(k, 0)
                if k.layer == 0:
                    for g in range(GROUPS - 1):
                        rsqrt(k, g + 1)
                        if k is phases[0]:
                            [apart_rows, lambda: ternary(2), lambda: ternary(3)][g]()
                        else:
                            pads_1(g)
                    rsqrt(k.next, 0)
                    return
                with pool.Fori(0, GROUPS - 1) as g:
                    group(g, False)
                group(GROUPS - 1, True)

            def qkv(k):
                a = k.att
                row = a.step * (HPG // a.vh)

                def group(g, last):
                    if not last:
                        rsqrt(k, g + 1)
                    for t in range(GT):
                        pool.wait_ge(s["qkv_free"], k["qkv_free"] + g * GT + t + 1)
                        at = a.at(g, t)
                        nc.gpsimd.tensor_copy(view(QA, at + 2 * a.hd, (a.step, a.heads), (1, a.hd)),
                                              view(QA, at, (a.step, a.heads), (1, a.hd)))
                        op = nc.gpsimd.tensor_copy(view(KA, at + a.hd, (row, a.kv), (1, a.hd)),
                                                   view(KA, at, (row, a.kv), (1, a.hd)))
                        op.then_inc(s["dup_done"], 1)

                if not k.primed:
                    rsqrt(k, 0)
                with pool.Fori(0, GROUPS - 1) as g:
                    group(g, False)
                group(GROUPS - 1, True)

            def att(k):
                a = k.att
                nset = len(a.sets)

                def place(i, of_batch, of_group):
                    b = i // a.groups
                    at = b * of_batch + (i % a.groups) * of_group
                    return at if isinstance(at, int) else pool.snap(at)

                def group_v(i, par):
                    if not (isinstance(i, int) and i == 0):
                        pool.wait_ge(s["pv_done"], k["pv_done"] + (i - 1) * nset)
                    at = place(i, ST_ * a.kvw, a.vh * a.hd)
                    nc.gpsimd.tensor_copy(view(VG[par], 0, (a.vh * 32, ST_), (32, a.vh), (1, a.hd)),
                                          view(VS, at, (a.kvw, ST_), (a.hd, a.vh), (1, a.hd))).then_inc(s["v_ready"], 1)

                def half(i, par, more):
                    if more:
                        group_v(i + 1, 1 - par)
                    pool.wait_ge(s["on_ready"], k["on_ready"] + i + 1)
                    at = place(i, ST_ * D, HPG * a.hd)
                    w = HPG * a.hd
                    nc.gpsimd.tensor_copy(view(AH, at, (D, ST_), (1, w)), view(ON, 0, (w, ST_), (1, w)))\
                        .then_inc(s["ah_done"], 1)
                    pool.wait_ge(s["ah_done"], k["ah_done"] + i + 1)
                    nc.gpsimd.tensor_tensor(view(AL, at, (D, ST_), (1, w)), view(ON, 0, (w, ST_), (1, w)),
                                            view(AH, at, (D, ST_), (1, w)), ALU.subtract).then_inc(s["ao_ready"], 1)

                pool.wait_ge(s["hi_ready"], k["hi_ready"])
                ones_of_v(1)
                group_v(0, 0)
                with pool.Fori(0, a.iters // 2 - 1) as r:
                    i = pool.snap(r * 2)
                    half(i, 0, True)
                    half(i + 1, 1, True)
                half(a.iters - 2, 0, True)
                half(a.iters - 1, 1, False)

            def mix(k):
                ones_of_v(0)

            def outward(k):
                rsqrt(k.next, 0)

            def ones_of_v(layer):
                a = ATTS[layer]
                for n in range(2):
                    nc.gpsimd.memset(VG[n][:, :], 0.0).then_inc(v_pad, 1)
                pool.wait_ge(v_pad, 4 * layer + 2)
                for n in range(2):
                    nc.gpsimd.memset(view(VG[n], a.hd, (32, ST_ * a.vh)), 1.0).then_inc(v_pad, 1)
                pool.wait_ge(v_pad, 4 * layer + 4)

            def zero(tensors, done):
                for t in tensors:
                    nc.gpsimd.memset(t[:, :].bitcast(F32), 0.0).then_inc(done, 1)

            def pads_1(part):
                if part == 0:
                    pool.wait_ge(s["ol_ready"], phases[3]["ol_ready"])
                    zero([QA], pad_zeroed)
                elif part == 1:
                    zero([KA], pad_zeroed)
                    zero(KT, k_zeroed)
                else:
                    pool.wait_ge(pad_zeroed, 4)
                    pool.wait_ge(k_zeroed, 6)
                    nc.gpsimd.memset(view(KA, 3 * ATTS[1].hd, (32, NT * 32), (1, 2)), 1.0).then_inc(pad_ready, 1)

            def apart_rows():
                a = ATTS[0]
                pool.wait_ge(w_in, 16 * 7)
                for n, t in enumerate((QA, KA)):
                    op = nc.gpsimd.tensor_copy(view(t, 3 * a.hd, (a.row, NT * a.heads), (1, NEAR)),
                                               view(aparts, n * NEAR, (0, NT * a.heads), (1, NEAR)))
                op.then_inc(pad_ready, 1)

            def proj(k):
                pass

            for name, counter in s.items():
                pool.sem_inc(counter, CREDIT.get(name, 1))
            for n, t in enumerate((ident, ident16, identb, maskb, maskt)):
                nc.gpsimd.memset(t[:, :], 0.0).then_inc(const_step, 1)
            pool.wait_ge(const_step, 5)
            for t in (ident, ident16, identb):
                nc.gpsimd.affine_select(out=t[:, :], in_=t[:, :], compare_op=ALU.not_equal, fill=1.0, base=0,
                                        pattern=[[-1, P]], channel_multiplier=1).then_inc(const_ready, 1)
            for t, sign in ((maskb, 1), (maskt, -1)):
                nc.gpsimd.affine_select(out=t[:, :], in_=t[:, :], compare_op=ALU.is_ge, fill=NEG, base=0,
                                        pattern=[[-sign, P]], channel_multiplier=sign).then_inc(const_ready, 1)
            nc.gpsimd.memset(ones[:, :], 1.0).then_inc(const_ready, 1)
            nc.gpsimd.memset(two[:, :], 0.0).then_inc(const_step, 1)
            for n in range(4):
                pool.wait_ge(const_step, 6 + n)
                nc.gpsimd.affine_select(out=two[:, :], in_=two[:, :], compare_op=ALU.not_equal, fill=1.0,
                                        base=-n * HD0, pattern=[[-1, HD0]], channel_multiplier=1)\
                    .then_inc(const_step, 1)
            pool.wait_ge(const_step, 10)
            nc.gpsimd.memset(mhalf[:, :], -0.5).then_inc(const_ready, 1)
            nc.gpsimd.memset(eps[:, :], EPS).then_inc(const_ready, 1)
            pool.wait_ge(const_ready, 8)
            nc.gpsimd.memset(VS[:, NT * D:], 0.0).then_inc(pad_ready, 1)
            zero([QA, KA], pad_zeroed)
            zero(KT, k_zeroed)
            for t in MT:
                nc.gpsimd.memset(t[:, :], 0.0).then_inc(k_zeroed, 1)
            pool.wait_ge(pad_zeroed, 2)
            pool.wait_ge(k_zeroed, 4)
            for k in phases:
                {"ffn": ffn, "qkv": qkv, "mix": mix, "out": outward, "att": att, "proj": proj}[k.kind](k)


def kernel(L0_attn_x, L0_attn_w_qkv, L0_attn_w_proj, L0_ffn_w_fc, L0_ffn_w_proj, L1_attn_wq, L1_attn_wk,
           L1_attn_wv, L1_attn_wo, L1_ffn_w1, L1_ffn_b1, L1_ffn_w2, L1_ffn_b2):
    import numpy as np
    import concourse.bacc as bacc
    from concourse.bass_utils import run_bass_kernel_spmd

    shape = L0_attn_x.shape
    near = BIG * (np.arange(P)[:, None] // BLOCKS == np.arange(NEAR)[None, :])
    arrays = {
        "x": np.asarray(L0_attn_x).reshape(TOK, D),
        "fc0": np.asarray(L0_ffn_w_fc).T, "down0": np.asarray(L0_ffn_w_proj).T,
        "fc1": np.asarray(L1_ffn_w1).T, "down1": np.asarray(L1_ffn_w2).T,
        "apart": np.concatenate([near, near - BIG], axis=1).astype(np.float32),
        "b1": np.asarray(L1_ffn_b1).reshape(-1, P).T, "b2": np.asarray(L1_ffn_b2).reshape(1, D),
        "qkv0": np.asarray(L0_attn_w_qkv).T, "wo0": np.asarray(L0_attn_w_proj).T,
        "qkv1": np.concatenate([np.asarray(w) for w in (L1_attn_wq, L1_attn_wk, L1_attn_wv)], axis=1),
        "wo1": np.asarray(L1_attn_wo),
    }
    arrays = {name: np.ascontiguousarray(a) for name, a in arrays.items()}
    nc = bacc.Bacc("TRN2", target_bir_lowering=False, num_devices=1)
    args = [nc.dram_tensor(name, a.shape, F32, kind="ExternalInput").ap() for name, a in arrays.items()]
    out = nc.dram_tensor("out", [TOK, D], F32, kind="ExternalOutput").ap()
    names = list(arrays)
    order = dict(zip(names, args))
    macaron_kernel(nc, out=out, **order)
    r = run_bass_kernel_spmd(nc, [arrays], core_ids=[0])
    return r.results[0]["out"].reshape(shape)
```

```python
from contextlib import ExitStack

import concourse.bass as bass
from concourse import mybir

F32 = mybir.dt.float32
F16 = mybir.dt.float16
BF16 = mybir.dt.bfloat16
ALU = mybir.AluOpType
ACT = mybir.ActivationFunctionType
AX_X = mybir.AxisListType.X

P = 128
D = 256
DC = D // P
TOK = 2048
NT = TOK // P
SEQ = 1024
ST_ = SEQ // P
BATCH = TOK // SEQ
GT = 4
GROUPS = NT // GT
GTOK = GT * P
BANK = 512
HPG = 4
WSCALE = 64.0
RSCALE = 0.25
NEG = -1.0e30
EPS = 1e-5

HID = (640, 1024)
BIG = 60000.0

HD0, HEADS0, NEAR = 16, 16, 8
BLOCKS = P // NEAR
MIXES = NT // 2
CHUNK = 4
HALF = HEADS0 // 2
CHUNKS = 2 * BLOCKS // CHUNK


class Att:

    def __init__(self, heads, kv_heads, causal):
        self.heads, self.kv, self.causal = heads, kv_heads, causal
        self.hd = D // heads
        self.row = 64 if self.hd == 16 else 32
        self.step = self.row if causal else 2 * self.row
        self.qkw = HPG * self.row
        self.groups = heads // HPG
        self.iters = BATCH * self.groups
        self.vh = HPG if kv_heads == heads else 1
        self.scale = float(self.hd) ** -0.5
        self.kvw = kv_heads * self.hd
        self.cols = D + 2 * self.kvw
        self.sets = [(h, k) for h in range(2) for k in range(GT * (h + 1) if causal else ST_)]
        self.maxes = []
        for qt in range(ST_):
            n = min(HPG, 2 * BANK // self.width(qt))
            self.maxes += [(qt, list(range(h, h + n))) for h in range(0, HPG, n)]
        n = len(self.maxes)
        self.lead = n + 5
        self.m_use, self.q_use, self.k_use, self.o_use = n, n + 1, n + 2, n + 3
        self.uses = n + 4
        assert self.uses % 2 == 0

    def out_use(self, ahead):
        return [0, self.q_use, self.o_use][ahead]

    def full(self, i, n):
        if i is None:
            return n + 1
        if isinstance(i, int) and i == self.iters - 1:
            return self.full(i - 1, self.out_use(1)) + n + 1
        return self.lead + i * self.uses + n + 1

    def at(self, g, t):
        if self.causal:
            return g * (GT * 1024) + t * 1024
        return g * (GT * 1024) + (t // 2 * 2048 + t % 2 * self.row)

    def v_at(self, g, t):
        if self.causal:
            return g * (GT * self.kvw) + t * self.kvw
        return g * (GT * 2 * D) + (t // 2 * 4 * D + t % 2 * 2 * self.hd)

    def keys(self, qt):
        return P * (qt + 1) if self.causal else SEQ

    def width(self, qt):
        w = self.keys(qt)
        return w if BANK % w == 0 else -(-w // BANK) * BANK

    def first(self, s):
        h, k = self.sets[s]
        return max(0, (k - GT * h) * P) if self.causal else 0

    def diagonal(self, s):
        h, k = self.sets[s]
        return self.causal and k >= GT * h

    def work(self, s, h):
        cols = [HPG * (BANK - self.first(x)) for x in range(len(self.sets))]
        return sum(cols[:s]) + cols[s] * (h + 1) // HPG

    def quota(self, s, h):
        part = self.work(s, h) / self.work(len(self.sets) - 4, HPG - 1)
        done = [sum(self.keys(q) * len(hs) for q, hs in self.maxes[:n + 1]) for n in range(len(self.maxes))]
        return sum(d <= part * done[-1] for d in done)

    def half_ends(self, s):
        return s + 1 == len(self.sets) or self.sets[s + 1][0] != self.sets[s][0]


ATTS = (Att(HEADS0, HEADS0, False), Att(32, 8, True))


def before(j, used):
    steps = [n for n, b in enumerate(used * 2) if b == used[j] and n < j + len(used)]
    return j + len(used) - steps[-1]


class Phase:

    def __init__(self, kind, layer, at):
        self.kind, self.layer, self.at = kind, layer, at
        self.next, self.primed = None, False
        self.att = ATTS[layer]
        self.nb = HID[layer] // P
        self.banks = [j % 4 if j % 4 or j + 1 < self.nb else 1 for j in range(self.nb)]
        self.rings = [j % 3 for j in range(self.nb)]
        n, a = {}, self.att
        if kind in ("ffn", "qkv"):
            n.update(stats_done=GROUPS, var_ready=GROUPS, eps_done=GROUPS, rstd_ready=GROUPS, xn_ready=GROUPS,
                     xt_ready=DC * GROUPS, xh_ready=DC * GROUPS, xl_ready=DC * GROUPS)
        if kind == "ffn":
            for name in ("h_ready", "t_ready", "uh_ready", "ul_ready", "down_done"):
                n[name] = self.nb * GROUPS
            n["resid"] = GROUPS
            n["u_done" if layer == 0 else "bias_added"] = self.nb * GROUPS if layer == 0 else GROUPS
        if kind == "qkv":
            n.update(qkv_ready=NT, hi_ready=NT, qkv_free=NT, dup_done=NT)
        if kind == "mix":
            w = MIXES
            n.update(a_full=8 * w, a0_read=4 * w, a1_read=4 * w, b_full=(CHUNKS + 1) * w, maxed=CHUNKS * w,
                     m_ready=w, st_ready=CHUNKS * w, p_ready=CHUNKS * w, pv_done=CHUNKS * w, o_out=2 * w, ot_full=2 * w,
                     rd_done=2 * w, on_ready=2 * w, on_turned=2 * w, oh_ready=2 * w, ol_ready=2 * w)
        if kind == "out":
            n.update(y_ready=GROUPS, resid=GROUPS)
        if kind == "att":
            i, s = a.iters, len(a.sets)
            n.update(slot_full=a.full(i - 1, 0), maxed=len(a.maxes) * i, q_copied=i, k_copied=i, qm_copied=i,
                     mh_done=i, m_written=i, st_ready=HPG * s * i, p_ready=HPG * s * i, pv_done=s * i,
                     o_out=2 * i, v_ready=i, rd_done=i, on_ready=i, ah_done=i, ao_ready=i)
        if kind == "proj":
            n.update(at_ready=2 * GROUPS, ah_copied=GROUPS, al_copied=GROUPS, y_ready=GROUPS, resid=GROUPS)
        self.n = n
        self.after = {**at, **{k: at.get(k, 1) + v for k, v in n.items()}}

    def __getitem__(self, name):
        return self.at.get(name, 1)


CREDIT = {"down_done": 8, "t_ready": 8, "qkv_free": 2, "pv_done": 8, "p_ready": 4}


def plan():
    phases, at = [], dict(CREDIT)
    for kind, layer in [("ffn", 0), ("qkv", 0), ("mix", 0), ("out", 0), ("ffn", 0),
                        ("ffn", 1), ("qkv", 1), ("att", 1), ("proj", 1), ("ffn", 1)]:
        phases.append(Phase(kind, layer, at))
        at = phases[-1].after
    for k, n in zip(phases, phases[1:]):
        if k.kind in ("ffn", "out", "proj") and n.kind in ("ffn", "qkv"):
            k.next, n.primed = n, True
    phases[0].primed = True
    return phases


def macaron_kernel(nc, x, apart, fc0, down0, fc1, down1, b1, b2, qkv0, wo0, qkv1, wo1, out):
    phases = plan()

    with ExitStack() as ctx:
        def sb(name, cols, dt):
            return ctx.enter_context(nc.sbuf_tensor(name, [P, cols], dt))

        def ps(name, cols):
            return ctx.enter_context(nc.psum_tensor(name, [P, cols], F32))

        def sem(name):
            return ctx.enter_context(nc.semaphore(name))

        def view(t, at, *dims):
            return bass.AP(t, at, [[t.shape[1], P], *[list(d) for d in dims]])

        def view16(t, at, *dims):
            full = t[:, :].bitcast(F16)
            return bass.AP(full.tensor, at, [[t.shape[1] * 2, P], *[list(d) for d in dims]])

        X = sb("X", NT * D, F32)
        QA = sb("QA", NT * 1024, F16)
        KA = sb("KA", NT * 1024, F16)
        VS = sb("VS", NT * D + P // 4, F32)
        VG = [sb(f"VG{k}", ST_ * HPG * 32, F32) for k in range(2)]
        QT1 = sb("QT1", 2 * SEQ, F16)
        QT2 = [sb(f"QT2{k}", 2 * SEQ, F16) for k in range(2)]
        KT = [sb(f"KT{k}", HPG * SEQ, F16) for k in range(2)]
        AH = sb("AH", NT * D, F16)
        AL = sb("AL", NT * D, F16)
        OT = sb("OT", 2 * BANK, F32)
        ON = sb("ON", ST_ * HPG * 16, F32)
        RD = sb("RD", ST_ * HPG, F32)
        NM = sb("NM", ST_ * HPG, F32)
        work = sb("work", 5120, F32)
        PR = [work[:, k * HPG * BANK:(k + 1) * HPG * BANK] for k in range(2)]
        XN = work[:, 0:GT * D]
        XH = work[:, 1024:1536].bitcast(F16)
        XL = work[:, 1536:2048].bitcast(F16)
        XHL = [(XH, XL), (work[:, 2048:2560].bitcast(F16), work[:, 2560:3072].bitcast(F16))]
        T = [work[:, 2048 + k * BANK:2048 + (k + 1) * BANK] for k in range(2)] + [OT[:, 0:BANK]]
        U = [work[:, 3072 + k * BANK:3072 + (k + 1) * BANK] for k in range(2)] + [OT[:, BANK:2 * BANK]]
        UH = [t.bitcast(F16) for t in (work[:, 4096:4352], work[:, 4352:4608], ON[:, 0:256])]
        UL = [t.bitcast(F16) for t in (work[:, 4608:4864], work[:, 4864:5120], ON[:, 256:512])]
        up = [sb(f"up_w{k}", DC * HID[k], F16) for k in range(2)]
        down = [sb(f"down_w{k}", HID[k] // P * D, F16) for k in range(2)]
        wqkv = [[sb(f"qkv_w{k}{p}", DC * ATTS[k].cols, F16) for p in "hl"] for k in range(2)]
        wo = [[sb(f"wo_w{k}{p}", DC * D, F16) for p in "hl"] for k in range(2)]
        b1s = sb("b1s", HID[1] // P, F32)
        b2h = sb("b2h", D, F32)
        ident = sb("ident", P, F32)
        ident16 = sb("ident16", P, F16)
        identb = sb("identb", P, BF16)
        maskb = sb("maskb", P, BF16)
        maskt = sb("maskt", P, BF16)
        ones = sb("ones", P, F32)
        sums = sb("sums", 4, F32)
        means = sb("means", 4, F32)
        lim = sb("lim", 8, F32)
        sc = sb("sc", 2, F32)
        bn = sb("bn", GT * 6, F32)
        mv = sb("mv", GT * 2, F32)
        var = sb("var", GT, F32)
        rstd = sb("rstd", GT, F32)
        mhalf = sb("mhalf", GT, F32)
        eps = sb("eps", GT, F32)
        aparts = sb("aparts", 2 * NEAR, F32)
        MT = [sb(f"MT{k}", P, BF16) for k in range(2)]
        two = sb("two", HD0, F16)

        A = ps("A", 2 * BANK)
        B = ps("B", 2 * BANK)
        C = ps("C", 4 * BANK)
        slots = [A, B]
        outs = [C[:, 0:2 * BANK], B]

        def by_block(t, b):
            return t.rearrange("p (r h n) -> p r h n", r=BLOCKS, h=HEADS0)[:, :, b * HALF:(b + 1) * HALF, :]

        def by_head(t, rows, b):
            return t[rows, b * BANK:(b + 1) * BANK].bitcast(F16).rearrange("p (h n r) -> p r h n", r=BLOCKS, h=HALF)

        def slot(i, n):
            return slots[(n if i is None else ATTS[1].lead + n) % 2]

        s = {k: sem(k) for k in sorted({k for ph in phases for k in ph.n})}
        gate, x0_in, x_in, ffn_w_in, ffn1_w_in, w_in, ternary_step, ternary_1, up_down_ready, const_ready, const_step, sums_ready, tot_ready = (sem(k) for k in (
            "gate", "x0_in", "x_in", "ffn_w_in", "ffn1_w_in", "w_in", "ternary_step", "ternary_1", "up_down_ready", "const_ready", "const_step", "sums_ready", "tot_ready"))
        setup_step, high_done, w_ready, pad_zeroed, pad_ready, v_pad, k_zeroed, out_done = (sem(k) for k in (
            "setup_step", "high_done", "w_ready", "pad_zeroed", "pad_ready", "v_pad", "k_zeroed", "out_done"))

        landing = {id(fc0): VS[:, 0:1280], id(down0): VS[:, 1280:2560], id(qkv0): VS[:, 2560:4096],
                   id(fc1): AH[:, :].bitcast(F32), id(down1): AL[:, :].bitcast(F32), id(wo0): QT1[:, :].bitcast(F32)[:, DC * D:],
                   id(qkv1): QT2[0][:, :].bitcast(F32)[:, 0:DC * ATTS[1].cols],
                   id(wo1): QT1[:, :].bitcast(F32)[:, 0:DC * D]}
        quant = [(w, landing[id(w)], dst) for w, dst in ((fc0, up[0]), (down0, down[0]), (fc1, up[1]), (down1, down[1]))]
        split = [(w, landing[id(w)], dst) for w, dst in ((qkv0, wqkv[0]), (wo0, wo[0]), (qkv1, wqkv[1]), (wo1, wo[1]))]

        block = ctx.enter_context(nc.Block())

        @block.sync
        def _(sp):
            def tiles(dram, g):
                return dram.rearrange("(t p) d -> p t d", p=P)[:, g * GT:(g + 1) * GT, :]

            def load(w, dst, done):
                sp.dma_start(dst.rearrange("p (c n) -> p c n", c=w.shape[0] // P),
                             w.rearrange("(c p) n -> p c n", p=P)).then_inc(done, 16)

            def load_x(g, done):
                sp.dma_start(view(X, g * GT * D, (D, GT), (1, D)), tiles(x, g)).then_inc(done, 16)

            load_x(0, x0_in)
            for n, (w, dst, _) in enumerate(quant):
                load(w, dst, (ffn_w_in if n < 2 else ffn1_w_in))
            for g in range(1, GROUPS):
                load_x(g, x_in)
            for w, dst, _ in split:
                load(w, dst, w_in)
            sp.dma_start(aparts[:, :], apart).then_inc(w_in, 16)
            sp.dma_start(b1s[:, :], b1).then_inc(w_in, 16)
            sp.dma_start(b2h[:, :], b2.broadcast_to([P, D])).then_inc(w_in, 16)
            for g in range(GROUPS):
                sp.wait_ge(s["resid"], phases[-1]["resid"] + g + 1)
                sp.dma_start(tiles(out, g), view(X, g * GT * D, (D, GT), (1, D))).then_inc(out_done, 16)
            sp.wait_ge(out_done, 16 * GROUPS)

        @block.tensor
        def _(pe):
            def transposes(k, g):
                pe.wait_ge(s["xn_ready"], k["xn_ready"] + g + 1)
                for c in range(DC):
                    for t in range(GT):
                        mm = pe.transpose(A[:, c * BANK + t * P:c * BANK + (t + 1) * P],
                                          XN[:, t * D + c * P:t * D + (c + 1) * P], ident[:, :])
                    mm.then_inc(s["xt_ready"], 1)

            def ffn(k):
                W, V, nb, hid = up[k.layer], down[k.layer], k.nb, HID[k.layer]

                def hidden(g, j):
                    b = k.banks[j]
                    pe.wait_ge(s["t_ready"], k["t_ready"] + g * nb + j - before(j, k.banks) + 1)
                    for c in range(DC):
                        if j == 0:
                            pe.wait_ge(s["xl_ready"], k["xl_ready"] + g * DC + c + 1)
                        for n, part in enumerate((XH, XL)):
                            mm = pe.matmul(C[:, b * BANK:(b + 1) * BANK],
                                           W[:, c * hid + j * P:c * hid + (j + 1) * P],
                                           part[:, c * GTOK:(c + 1) * GTOK],
                                           start=(c == 0 and n == 0), stop=(c == DC - 1 and n == 1))
                    mm.then_inc(s["h_ready"], 1)

                def to_model(g, j):
                    if j == 0:
                        pe.wait_ge(s["resid"], k["resid"] + g)
                    pe.wait_ge(s["ul_ready"], k["ul_ready"] + g * nb + j + 1)
                    for t in range(GT):
                        for n, part in enumerate((UH[k.rings[j]], UL[k.rings[j]])):
                            mm = pe.matmul(B[:, t * D:(t + 1) * D], part[:, t * P:(t + 1) * P],
                                           V[:, j * D:(j + 1) * D],
                                           start=(j == 0 and n == 0 and t % 2 == 0),
                                           stop=(j == nb - 1 and n == 1), skip_group_check=True)
                    mm.then_inc(s["down_done"], 1)

                def group(g, last):
                    for j in range(nb):
                        if j + 2 < nb:
                            hidden(g, j + 2)
                        elif not last:
                            hidden(g + 1, j + 2 - nb)
                        if j + 3 == nb and not last:
                            transposes(k, g + 1)
                        elif j + 3 == nb and k.next:
                            transposes(k.next, 0)
                        to_model(g, j)

                if not k.primed:
                    transposes(k, 0)
                if k is not phases[0]:
                    pe.wait_ge(s["resid"], k["resid"] - 1)
                hidden(0, 0)
                hidden(0, 1)
                with pe.Fori(0, GROUPS - 1) as g:
                    group(g, False)
                group(GROUPS - 1, True)

            def qkv(k):
                a = k.att
                Wh, Wl = wqkv[k.layer]

                def group(g, par, last):
                    XH, XL = XHL[par]
                    for t in range(GT):
                        pe.wait_ge(s["qkv_free"], k["qkv_free"] + g * GT + t - 1)
                        if t == 0:
                            pe.wait_ge(s["xl_ready"], k["xl_ready"] + g * DC + DC)
                        for lo in range(0, a.cols, BANK):
                            w, o = min(BANK, a.cols - lo), t % 2 * 2 * BANK + lo
                            for c in range(DC):
                                for n, (p, q) in enumerate(((XH, Wh), (XH, Wl), (XL, Wh))):
                                    mm = pe.matmul(C[:, o:o + w], p[:, c * GTOK + t * P:c * GTOK + (t + 1) * P],
                                                   q[:, c * a.cols + lo:c * a.cols + lo + w],
                                                   start=(c == 0 and n == 0), stop=(c == DC - 1 and n == 2))
                        mm.then_inc(s["qkv_ready"], 1)
                        if t == 1 and not last:
                            transposes(k, g + 1)

                if not k.primed:
                    transposes(k, 0)
                with pe.Fori(0, GROUPS // 2 - 1) as n:
                    g = pe.snap(n * 2)
                    group(g, 0, False)
                    group(g + 1, 1, False)
                group(GROUPS - 2, 0, False)
                group(GROUPS - 1, 1, True)

            def att(k):
                a = k.att
                nset, nmax = len(a.sets), len(a.maxes)

                def turn(src, i, dst):
                    b = i // a.groups
                    at = b * (ST_ * 1024) + (i % a.groups) * a.qkw
                    at = at if isinstance(at, int) else pe.snap(at)
                    for t in range(ST_):
                        mm = pe.transpose(dst[:, :].bitcast(F16)[:, t * P:(t + 1) * P],
                                          view(src, at + t * 1024, (1, P)), ident16[:, :])
                    mm.then_inc(s["slot_full"], 1)

                def maximum(i, par, m, dst):
                    qt, heads = a.maxes[m]
                    if m == 0:
                        pe.wait_ge(s["q_copied"], k["q_copied"] + i + 1)
                        pe.wait_ge(s["k_copied"], k["k_copied"] + i + 1)
                    elif m == 1:
                        pe.wait_ge(s["on_ready"], k["on_ready"] + i - 1)
                    else:
                        pe.wait_ge(s["maxed"], k["maxed"] + i * nmax + m - 1)
                    keys, begun = a.keys(qt), []
                    for w in range(len(heads)):
                        o = w * a.width(qt) + keys - P
                        pe.matmul(dst[:, o:o + P], identb[:, :], maskb[:, :], start=o // BANK not in begun,
                                  stop=False, skip_group_check=True)
                        begun.append(o // BANK)
                    for w, h in enumerate(heads):
                        for lo in range(0, keys, BANK):
                            o, c = w * a.width(qt) + lo, min(BANK, keys - lo)
                            mm = pe.matmul(dst[:, o:o + c], QT1[:, qt * P:(qt + 1) * P],
                                           KT[par][:, h * SEQ + lo:h * SEQ + lo + c], start=o // BANK not in begun,
                                           stop=True, skip_group_check=True)
                            begun.append(o // BANK)
                    mm.then_inc(s["slot_full"], 1)

                def score(i, par, x, h):
                    st = x * HPG + h
                    pe.wait_ge(s["p_ready"], k["p_ready"] + i * (HPG * nset) + st - before(st, [n % 3 for n in range(HPG * nset)]) + 1)
                    if st == 0:
                        pe.wait_ge(s["qm_copied"], k["qm_copied"] + i + 1)
                    qh, kt = a.sets[x]
                    lo, b = a.first(x), st % 3
                    diagonal = a.diagonal(x)
                    if diagonal:
                        pe.matmul(C[:, b * BANK + lo:b * BANK + lo + P], identb[:, :], maskt[:, :],
                                  start=True, stop=False, skip_group_check=True)
                    pe.matmul(C[:, b * BANK + lo:(b + 1) * BANK], KT[par][:, h * SEQ + kt * P:h * SEQ + (kt + 1) * P],
                              QT2[par][:, qh * BANK + lo:(qh + 1) * BANK],
                              start=not diagonal, stop=True, skip_group_check=True).then_inc(s["st_ready"], 1)

                def values(i, par, x):
                    qh, kt = a.sets[x]
                    lo = a.first(x)
                    if x == 0:
                        pe.wait_ge(s["v_ready"], k["v_ready"] + i + 1)
                    if kt == 0:
                        pe.wait_ge(s["o_out"], k["o_out"] + i * 2 + qh)
                    pe.wait_ge(s["p_ready"], k["p_ready"] + i * (HPG * nset) + HPG * (x + 1))
                    for h in range(HPG):
                        v = (kt * a.vh + h % a.vh) * 32
                        mm = pe.matmul(C[32 * h:32 * h + 32, 3 * BANK + lo:4 * BANK], VG[par][:, v:v + 32],
                                       PR[x % 2][:, h * BANK + lo:(h + 1) * BANK],
                                       start=(kt == 0), stop=a.half_ends(x), skip_group_check=True,
                                       tile_position=(0, 32 * h))
                    mm.then_inc(s["pv_done"], 1)

                def turned_qm(i, dst):
                    pe.wait_ge(s["m_written"], k["m_written"] + i + 1)
                    pe.sem_inc(gate, 1)
                    turn(QA, i, dst)

                def turned_k(i, dst):
                    pe.wait_ge(s["qm_copied"], k["qm_copied"] + i)
                    pe.sem_inc(gate, 1)
                    turn(KA, i, dst)

                def half(i, par, ahead):
                    m = 0
                    for x in range(nset):
                        for h in range(HPG):
                            if x or h > 2:
                                score(i, par, x, h)
                            if x == nset - 2 and h == HPG - 1 and ahead:
                                turned_qm(i + 1, slot(i, a.m_use))
                            if x == nset - 1 and h == 1 and ahead > 1:
                                turn(QA, i + 2, slot(i, a.q_use))
                            while ahead and m < a.quota(x, h):
                                maximum(i + 1, 1 - par, m, slot(i, m))
                                m += 1
                        if x:
                            values(i, par, x - 1)
                    if ahead > 1:
                        turned_k(i + 2, slot(i, a.k_use))
                    values(i, par, nset - 1)
                    if ahead:
                        for h in range(3):
                            score(i + 1, 1 - par, 0, h)
                    if ahead > 1:
                        pe.wait_ge(s["q_copied"], k["q_copied"] + i + 3)
                    elif not ahead:
                        pe.wait_ge(s["qm_copied"], k["qm_copied"] + a.iters)
                    pe.wait_ge(s["o_out"], k["o_out"] + i * 2 + 2)
                    dst = slot(i, a.out_use(ahead))
                    for t in range(ST_):
                        mm = pe.transpose(dst[:, t * P:(t + 1) * P], OT[:, t * P:(t + 1) * P], ident[:, :])
                    mm.then_inc(s["slot_full"], 1)

                pe.wait_ge(s["qkv_free"], k["qkv_free"])
                pe.wait_ge(s["dup_done"], k["dup_done"])
                turn(QA, 0, slot(None, 0))
                turn(KA, 0, slot(None, 1))
                for m in range(nmax):
                    maximum(0, 0, m, slot(None, 2 + m))
                turned_qm(0, slot(None, nmax + 2))
                turn(QA, 1, slot(None, nmax + 3))
                turned_k(1, slot(None, nmax + 4))
                for h in range(3):
                    score(0, 0, 0, h)
                with pe.Fori(0, a.iters // 2 - 1) as r:
                    i = pe.snap(r * 2)
                    half(i, 0, 2)
                    half(i + 1, 1, 2)
                half(a.iters - 2, 0, 1)
                half(a.iters - 1, 1, 0)

            def mix(k):
                def bank_free(w, use, b):
                    pe.wait_ge(s[f"a{b}_read"], k[f"a{b}_read"] + w * 4 + use)

                def turn(seen, src, w, use, step):
                    at = w * (step * HEADS0)
                    for b in range(2):
                        bank_free(w, use, b)
                        pe.sem_inc(gate, 1)
                        for h in range(b * HALF, (b + 1) * HALF):
                            mm = pe.transpose(A[:, :].bitcast(F16)[:, h * P:(h + 1) * P],
                                              seen(src, at + h * step, (1, P)), ident16[:, :])
                        mm.then_inc(s["a_full"], 1)

                def turn_q(w):
                    turn(view, QA, w, 0, P)

                def turn_k(w):
                    turn(view, KA, w, 1, P)

                def turn_v(w):
                    turn(view16, VS, w, 2, P // 2)

                def blocks_v(w):
                    for u in range(2):
                        bank_free(w, 3, u)
                    for u in range(2):
                        for r in range(BLOCKS):
                            mm = pe.matmul(A[:, u * BANK + r * HD0:u * BANK + (r + 1) * HD0],
                                           QT1[32 * u:32 * u + 32, r * P:(r + 1) * P], two[32 * u:32 * u + 32, :],
                                           start=(r == 0), stop=True, skip_group_check=True)
                        mm.then_inc(s["a_full"], 1)

                def maximum(w, par, c):
                    if c == 0:
                        for b in range(2):
                            bank_free(w, 2, b)
                        pe.wait_ge(s["m_ready"], k["m_ready"] + w)
                    if c > 1:
                        pe.wait_ge(s["maxed"], k["maxed"] + w * CHUNKS + c - 1)
                    for n in range(CHUNK):
                        x = c * CHUNK + n
                        o, r = (c % 2 * CHUNK + n) * P, x % BLOCKS * P
                        mm = pe.matmul(B[:, o:o + P], QT2[par][:, r:r + P], KT[par][:, x * P:(x + 1) * P],
                                       start=(n == 0), stop=True, skip_group_check=True)
                    mm.then_inc(s["b_full"], 1)

                def turn_m(w):
                    pe.wait_ge(s["maxed"], k["maxed"] + (w + 1) * CHUNKS)
                    pe.transpose(B[0:2 * BLOCKS, 0:P], NM[:, :], ident[:, :]).then_inc(s["b_full"], 1)

                def score(w, par, c):
                    if c == 0:
                        pe.wait_ge(s["m_ready"], k["m_ready"] + w + 1)
                    pe.wait_ge(s["p_ready"], k["p_ready"] + w * CHUNKS + c - 1)
                    for n in range(CHUNK):
                        o = (c % 2 * CHUNK + n) * P
                        pe.matmul(C[:, o:o + P], view(identb, c * CHUNK + n, (0, P)), MT[par][:, :],
                                  start=(n == 0), stop=False, skip_group_check=True)
                    for n in range(CHUNK):
                        x = c * CHUNK + n
                        o, r = (c % 2 * CHUNK + n) * P, x % BLOCKS * P
                        mm = pe.matmul(C[:, o:o + P], KT[par][:, x * P:(x + 1) * P], QT2[par][:, r:r + P],
                                       start=False, stop=True, skip_group_check=True)
                    mm.then_inc(s["st_ready"], 1)

                def values(w, par, c):
                    if c == 0:
                        for b in range(2):
                            bank_free(w, 4, b)
                    if c % CHUNK == 0:
                        pe.wait_ge(s["o_out"], k["o_out"] + w * 2 + c // CHUNK)
                    pe.wait_ge(s["p_ready"], k["p_ready"] + w * CHUNKS + c + 1)
                    for n in range(CHUNK):
                        o, v = 2 * BANK + c % CHUNK * P, (c * CHUNK + n) * 32
                        mm = pe.matmul(C[32 * n:32 * n + 32, o:o + P], VG[par][:, v:v + 32],
                                       PR[c // CHUNK][:, (c % CHUNK * CHUNK + n) * P:(c % CHUNK * CHUNK + n + 1) * P],
                                       start=(c % CHUNK == 0), stop=True, skip_group_check=True,
                                       tile_position=(0, 32 * n))
                    mm.then_inc(s["pv_done"], 1)

                def turn_sums(w, u):
                    pe.wait_ge(s["o_out"], k["o_out"] + w * 2 + u + 1)
                    pe.wait_ge(s["ol_ready"], k["ol_ready"] + w * 2 + u)
                    for n in range(4):
                        mm = pe.transpose(C[:, 3 * BANK + n * P:3 * BANK + (n + 1) * P],
                                          OT[:, u * BANK + n * P:u * BANK + (n + 1) * P], ident[:, :])
                    mm.then_inc(s["ot_full"], 1)

                def turn_out(w, u):
                    pe.wait_ge(s["on_ready"], k["on_ready"] + w * 2 + u + 1)
                    for c in range(DC):
                        mm = pe.transpose(C[:, 3 * BANK + c * P:3 * BANK + (c + 1) * P],
                                          ON[:, u * D + c * P:u * D + (c + 1) * P], ident[:, :])
                    mm.then_inc(s["on_turned"], 1)

                def half(w, par, ahead):
                    def maxima(*cs):
                        for c in cs:
                            if ahead:
                                maximum(w + 1, 1 - par, c)

                    score(w, par, 0)
                    score(w, par, 1)
                    if ahead:
                        turn_v(w + 1)
                    values(w, par, 0)
                    score(w, par, 2)
                    maxima(0)
                    values(w, par, 1)
                    score(w, par, 3)
                    maxima(1)
                    values(w, par, 2)
                    score(w, par, 4)
                    if ahead:
                        blocks_v(w + 1)
                    maxima(2)
                    values(w, par, 3)
                    score(w, par, 5)
                    maxima(3)
                    turn_sums(w, 0)
                    values(w, par, 4)
                    score(w, par, 6)
                    maxima(4)
                    turn_out(w, 0)
                    values(w, par, 5)
                    score(w, par, 7)
                    if ahead > 1:
                        turn_q(w + 2)
                    maxima(5)
                    values(w, par, 6)
                    maxima(6)
                    values(w, par, 7)
                    maxima(7)
                    if ahead:
                        turn_m(w + 1)
                    turn_sums(w, 1)
                    if ahead > 1:
                        turn_k(w + 2)
                    turn_out(w, 1)

                pe.wait_ge(s["qkv_free"], k["qkv_free"])
                pe.wait_ge(s["dup_done"], k["dup_done"])
                turn_q(0)
                turn_k(0)
                for c in range(CHUNKS):
                    maximum(0, 0, c)
                    if c in (1, 3, 5, 6):
                        {1: turn_v, 3: blocks_v, 5: turn_q, 6: turn_k}[c](c // 5)
                turn_m(0)
                with pe.Fori(0, MIXES // 2 - 1) as r:
                    w = pe.snap(r * 2)
                    half(w, 0, 2)
                    half(w + 1, 1, 2)
                half(MIXES - 2, 0, 1)
                half(MIXES - 1, 1, 0)

            def outward(k):
                Wh, Wl = wo[k.layer]
                pe.wait_ge(s["ol_ready"], k["ol_ready"])
                pe.wait_ge(s["oh_ready"], k["oh_ready"])

                def group(g, par):
                    pe.wait_ge(s["resid"], k["resid"] + g - 1)
                    for t in range(GT):
                        for c in range(DC):
                            for n, (p, q) in enumerate(((AH, Wh), (AH, Wl), (AL, Wh))):
                                mm = pe.matmul(outs[par][:, t * D:(t + 1) * D], view(p, g * GTOK + (c * TOK + t * P), (1, P)),
                                               q[:, c * D:(c + 1) * D], start=(c == 0 and n == 0 and t % 2 == 0),
                                               stop=(c == DC - 1 and n == 2), skip_group_check=True)
                    mm.then_inc(s["y_ready"], 1)

                with pe.Fori(0, GROUPS // 2 - 1) as n:
                    g = pe.snap(n * 2)
                    group(g, 0)
                    group(g + 1, 1)
                group(GROUPS - 2, 0)
                transposes(k.next, 0)
                group(GROUPS - 1, 1)

            def proj(k):
                Wh, Wl = wo[k.layer]

                def turned(g):
                    pe.wait_ge(s["ah_copied"], k["ah_copied"] + g)
                    pe.wait_ge(s["al_copied"], k["al_copied"] + g)
                    pe.sem_inc(gate, 1)
                    for part, src in enumerate((AH, AL)):
                        for c in range(DC):
                            for t in range(GT):
                                o = part * 2 * BANK + c * GTOK + t * P
                                mm = pe.transpose(A[:, :].bitcast(F16)[:, o:o + P],
                                                  view(src, g * (GT * D) + (t * D + c * P), (1, P)), ident16[:, :])
                        mm.then_inc(s["at_ready"], 1)

                def group(g, par, last):
                    if last:
                        pe.wait_ge(s["ah_copied"], k["ah_copied"] + GROUPS)
                        pe.wait_ge(s["al_copied"], k["al_copied"] + GROUPS)
                        transposes(k.next, 0)
                    else:
                        turned(g + 1)
                    XH, XL = XHL[par]
                    pe.wait_ge(s["ah_copied"], k["ah_copied"] + g + 1)
                    pe.wait_ge(s["al_copied"], k["al_copied"] + g + 1)
                    pe.wait_ge(s["resid"], k["resid"] + g - 1)
                    for t in range(GT):
                        for c in range(DC):
                            for n, (p, q) in enumerate(((XH, Wh), (XH, Wl), (XL, Wh))):
                                mm = pe.matmul(outs[par][:, t * D:(t + 1) * D],
                                               p[:, c * GTOK + t * P:c * GTOK + (t + 1) * P],
                                               q[:, c * D:(c + 1) * D], start=(c == 0 and n == 0 and t % 2 == 0),
                                               stop=(c == DC - 1 and n == 2), skip_group_check=True)
                    mm.then_inc(s["y_ready"], 1)

                pe.wait_ge(s["ao_ready"], k["ao_ready"])
                turned(0)
                with pe.Fori(0, GROUPS // 2 - 1) as n:
                    g = pe.snap(n * 2)
                    group(g, 0, False)
                    group(g + 1, 1, False)
                group(GROUPS - 2, 0, False)
                group(GROUPS - 1, 1, True)

            pe.wait_ge(const_ready, 8)
            transposes(phases[0], 0)
            pe.wait_ge(sums_ready, 1)
            pe.matmul(C[:, 0:4], ones[:, :], sums[:, :], start=True, stop=True).then_inc(tot_ready, 1)
            pe.wait_ge(w_ready, 1)
            for k in phases:
                if k is phases[1]:
                    pe.wait_ge(w_ready, 2)
                if k.layer == 1:
                    pe.wait_ge(ternary_1, 2)
                {"ffn": ffn, "qkv": qkv, "mix": mix, "out": outward, "att": att, "proj": proj}[k.kind](k)

        @block.scalar
        def _(act):
            def split_high(k, g, par=0):
                XH = XHL[par][0]
                for c in range(DC):
                    act.wait_ge(s["xt_ready"], k["xt_ready"] + g * DC + c + 1)
                    nc.scalar.activation(XH[:, c * GTOK:(c + 1) * GTOK], A[:, c * BANK:(c + 1) * BANK],
                                         ACT.Copy).then_inc(s["xh_ready"], 1)

            def ffn(k):
                def group(g, last):
                    for j in range(k.nb):
                        n, b, t = g * k.nb + j, k.banks[j], k.rings[j]
                        act.wait_ge(s["h_ready"], k["h_ready"] + n + 1)
                        act.wait_ge(s["down_done"], k["down_done"] + n - before(j, k.rings) + 1)
                        src = C[:, b * BANK:(b + 1) * BANK]
                        if k.layer == 0:
                            nc.scalar.activation(T[t], src, ACT.Relu, scale=RSCALE).then_inc(s["t_ready"], 1)
                            act.wait_ge(s["t_ready"], k["t_ready"] + n + 1)
                            nc.scalar.activation(U[t], T[t], ACT.Square).then_inc(s["u_done"], 1)
                            act.wait_ge(s["u_done"], k["u_done"] + n + 1)
                        else:
                            nc.scalar.activation(T[t], src, ACT.Gelu, bias=b1s[:, j:j + 1]).then_inc(s["t_ready"], 1)
                            act.wait_ge(s["t_ready"], k["t_ready"] + n + 1)
                        nc.scalar.activation(UH[t], (U if k.layer == 0 else T)[t], ACT.Copy).then_inc(s["uh_ready"], 1)
                        if j + 2 == k.nb and not last:
                            split_high(k, g + 1)
                        elif j + 2 == k.nb and k.next:
                            split_high(k.next, 0)

                nc.scalar.preload_act_table(ACT.Exp if k.layer == 0 else ACT.Gelu)
                if not k.primed:
                    split_high(k, 0)
                with act.Fori(0, GROUPS - 1) as g:
                    group(g, False)
                group(GROUPS - 1, True)

            def qkv(k):
                a = k.att

                def group(g, par, last):
                    for t in range(GT):
                        act.wait_ge(s["qkv_ready"], k["qkv_ready"] + g * GT + t + 1)
                        o = t % 2 * 2 * BANK
                        at, row = a.at(g, t), a.step * (HPG // a.vh)
                        nc.scalar.activation(view(QA, at, (a.step, a.heads), (1, a.hd)),
                                             view(C, o, (a.hd, a.heads), (1, a.hd)), ACT.Copy, scale=1 / WSCALE)
                        nc.scalar.activation(view(KA, at, (row, a.kv), (1, a.hd)),
                                             view(C, o + D, (a.hd, a.kv), (1, a.hd)), ACT.Copy, scale=1 / WSCALE)
                        if k.layer == 0:
                            dst = view16(VS, a.v_at(g, t), (4 * a.hd, a.kv), (1, a.hd))
                        else:
                            dst = view(VS, a.v_at(g, t), (a.hd, a.kv), (1, a.hd))
                        nc.scalar.activation(dst, view(C, o + D + a.kvw, (a.hd, a.kv), (1, a.hd)), ACT.Copy,
                                             scale=1 / WSCALE).then_inc(s["hi_ready"], 1)
                        if t == 2 and not last:
                            split_high(k, g + 1, 1 - par)

                if not k.primed:
                    split_high(k, 0)
                act.wait_ge(pad_ready, 2 + k.layer)
                with act.Fori(0, GROUPS // 2 - 1) as n:
                    g = act.snap(n * 2)
                    group(g, 0, False)
                    group(g + 1, 1, False)
                group(GROUPS - 2, 0, False)
                group(GROUPS - 1, 1, True)

            def att(k):
                a = k.att
                nset = len(a.sets)

                def await_slot(i, n):
                    act.wait_ge(s["slot_full"], k["slot_full"] + a.full(i, n))

                def copy_qm(i, n, dst):
                    await_slot(i, n)
                    nc.scalar.activation(dst[:, 0:SEQ], slot(i, n)[:, :].bitcast(F16)[:, 0:SEQ],
                                         ACT.Copy).then_inc(s["qm_copied"], 1)

                def drain(i, x):
                    qh = a.sets[x][0]
                    act.wait_ge(s["pv_done"], k["pv_done"] + i * nset + x + 1)
                    if qh == 0:
                        act.wait_ge(s["slot_full"], k["slot_full"] + a.full(i, -1))
                    nc.scalar.activation(OT[:, qh * BANK:(qh + 1) * BANK], C[:, 3 * BANK:4 * BANK],
                                         ACT.Copy).then_inc(s["o_out"], 1)

                def half(i, par, ahead):
                    for x in range(nset):
                        lo = a.first(x)
                        act.wait_ge(s["pv_done"], k["pv_done"] + i * nset + x - 1)
                        for h in range(HPG):
                            st = x * HPG + h
                            b = st % 3
                            act.wait_ge(s["st_ready"], k["st_ready"] + i * (HPG * nset) + st + 1)
                            nc.scalar.activation(PR[x % 2][:, h * BANK + lo:(h + 1) * BANK],
                                                 C[:, b * BANK + lo:(b + 1) * BANK], ACT.Exp,
                                                 scale=a.scale).then_inc(s["p_ready"], 1)
                        if x and a.half_ends(x - 1):
                            drain(i, x - 1)
                        if x == nset - 2 and ahead:
                            copy_qm(i, a.m_use, QT2[1 - par])
                    drain(i, nset - 1)

                nc.scalar.preload_act_table(ACT.Exp)
                copy_qm(None, a.lead - 3, QT2[0])
                with act.Fori(0, a.iters // 2 - 1) as r:
                    i = act.snap(r * 2)
                    half(i, 0, 2)
                    half(i + 1, 1, 2)
                half(a.iters - 2, 0, 1)
                half(a.iters - 1, 1, 0)

            def mix(k):
                def turned(dst, rows):
                    return nc.scalar.activation(by_block(dst, 0), by_head(A, rows, 0), ACT.Copy)

                def a_filled(w, use):
                    act.wait_ge(s["a_full"], k["a_full"] + w * 8 + 2 * use + 1)

                def turned_q(w, par):
                    a_filled(w, 0)
                    turned(QT2[par][:, :], slice(0, P)).then_inc(s["a0_read"], 1)

                def turned_k(w, par):
                    a_filled(w, 1)
                    for u in range(2):
                        rows = slice(64 * u, 64 * u + 64)
                        op = turned(KT[par][rows, u * BLOCKS * P:(u + 1) * BLOCKS * P], rows)
                    op.then_inc(s["a0_read"], 1)

                def turned_v(w):
                    a_filled(w, 2)
                    turned(QT1[0:64, :], slice(0, 64)).then_inc(s["a0_read"], 1)

                def blocks_v(w, par):
                    a_filled(w, 3)
                    nc.scalar.activation(view(VG[par], 0, (32, BLOCKS), (1, HD0)),
                                         view(A, 0, (HD0, BLOCKS), (1, HD0)), ACT.Copy).then_inc(s["a0_read"], 1)

                def exps(w, c):
                    act.wait_ge(s["pv_done"], k["pv_done"] + w * CHUNKS + c - CHUNKS + 1)
                    act.wait_ge(s["st_ready"], k["st_ready"] + w * CHUNKS + c + 1)
                    o = c % CHUNK * BANK
                    nc.scalar.activation(PR[c // CHUNK][:, o:o + BANK], C[:, c % 2 * BANK:(c % 2 + 1) * BANK],
                                         ACT.Exp, scale=k.att.scale).then_inc(s["p_ready"], 1)

                def sums_out(w, u):
                    act.wait_ge(s["pv_done"], k["pv_done"] + w * CHUNKS + (u + 1) * CHUNK)
                    act.wait_ge(s["ot_full"], k["ot_full"] + w * 2 + u - 1 + 1)
                    nc.scalar.activation(OT[:, u * BANK:(u + 1) * BANK], C[:, 2 * BANK:3 * BANK],
                                         ACT.Copy).then_inc(s["o_out"], 1)

                def high(w, u):
                    act.wait_ge(s["on_turned"], k["on_turned"] + w * 2 + u + 1)
                    t = w * 2 + u
                    at = (t // ST_) * SEQ + (t % ST_) * NEAR
                    for c in range(DC):
                        op = nc.scalar.activation(view(AH, at + c * TOK, (SEQ // HEADS0, HEADS0), (1, NEAR)),
                                                  view(C, 3 * BANK + c * P, (NEAR, HEADS0), (1, NEAR)), ACT.Copy)
                    op.then_inc(s["oh_ready"], 1)

                def half(w, par, ahead):
                    exps(w, 0)
                    exps(w, 1)
                    if ahead:
                        turned_v(w + 1)
                    exps(w, 2)
                    exps(w, 3)
                    if ahead:
                        blocks_v(w + 1, 1 - par)
                    exps(w, 4)
                    sums_out(w, 0)
                    exps(w, 5)
                    exps(w, 6)
                    high(w, 0)
                    exps(w, 7)
                    if ahead > 1:
                        turned_q(w + 2, par)
                    sums_out(w, 1)
                    if ahead > 1:
                        turned_k(w + 2, par)
                    high(w, 1)

                nc.scalar.preload_act_table(ACT.Exp)
                turned_q(0, 0)
                turned_k(0, 0)
                turned_v(0)
                blocks_v(0, 0)
                turned_q(1, 1)
                turned_k(1, 1)
                with act.Fori(0, MIXES // 2 - 1) as r:
                    w = act.snap(r * 2)
                    half(w, 0, 2)
                    half(w + 1, 1, 2)
                half(MIXES - 2, 0, 1)
                half(MIXES - 1, 1, 0)

            def outward(k):
                split_high(k.next, 0)

            def proj(k):
                def copy_high(g, par):
                    act.wait_ge(s["at_ready"], k["at_ready"] + g * 2 + 1)
                    nc.scalar.activation(XHL[par][0], A[:, 0:BANK].bitcast(F16), ACT.Copy).then_inc(s["ah_copied"], 1)

                with act.Fori(0, GROUPS // 2) as n:
                    g = act.snap(n * 2)
                    copy_high(g, 0)
                    copy_high(g + 1, 1)
                split_high(k.next, 0)

            split_high(phases[0], 0)
            act.wait_ge(w_in, 16 * 7)
            for n, (_, src, dst) in enumerate(split):
                nc.scalar.activation(dst[0][:, :], src, ACT.Copy, scale=WSCALE).then_inc(high_done, 1)
            for k in phases:
                {"ffn": ffn, "qkv": qkv, "mix": mix, "out": outward, "att": att, "proj": proj}[k.kind](k)

        @block.vector
        def _(dve):
            def statistics(k, g):
                for t in range(GT):
                    st = nc.vector.bn_stats(bn[:, t * 6:(t + 1) * 6], view(X, g * (GT * D) + t * D, (1, D)))
                st.then_inc(s["stats_done"], 1)
                dve.wait_ge(s["stats_done"], k["stats_done"] + g + 1)
                dve.sem_inc(gate, 1)
                for t in range(GT):
                    ag = nc.vector.bn_aggr(mv[:, t * 2:(t + 1) * 2], bn[:, t * 6:(t + 1) * 6])
                ag.then_inc(s["var_ready"], 1)

            def normalise(k, g):
                dve.wait_ge(s["rstd_ready"], k["rstd_ready"] + g + 1)
                for t in range(GT):
                    op = nc.vector.tensor_scalar(XN[:, t * D:(t + 1) * D], view(X, g * (GT * D) + t * D, (1, D)),
                                                 mv[:, t * 2:t * 2 + 1], rstd[:, t:t + 1], ALU.subtract, ALU.mult)
                op.then_inc(s["xn_ready"], 1)

            def split_low(k, g, par=0):
                XH, XL = XHL[par]
                for c in range(DC):
                    dve.wait_ge(s["xh_ready"], k["xh_ready"] + g * DC + c + 1)
                    nc.vector.tensor_tensor(XL[:, c * GTOK:(c + 1) * GTOK], A[:, c * BANK:(c + 1) * BANK],
                                            XH[:, c * GTOK:(c + 1) * GTOK], ALU.subtract).then_inc(s["xl_ready"], 1)

            def first_group(k):
                if not k.primed:
                    statistics(k, 0)
                    normalise(k, 0)
                    split_low(k, 0)

            def add_to_x(g, scale, src=B):
                for n in range(2):
                    xs = view(X, g * (GT * D) + n * BANK, (1, BANK))
                    op = nc.vector.scalar_tensor_tensor(out=xs, in0=src[:, n * BANK:(n + 1) * BANK], scalar=scale,
                                                        in1=xs, op0=ALU.mult, op1=ALU.add)
                op.then_inc(s["resid"], 1)

            def ffn(k):
                def group(g, left):
                    follow = [(k, g + n) if n <= left else (k.next, 0) if n == left + 1 and k.next else None
                              for n in (1, 2)]
                    for j in range(k.nb):
                        n, t = g * k.nb + j, k.rings[j]
                        dve.wait_ge(s["uh_ready"], k["uh_ready"] + n + 1)
                        nc.vector.tensor_tensor(UL[t], (U if k.layer == 0 else T)[t], UH[t], ALU.subtract)\
                            .then_inc(s["ul_ready"], 1)
                        if j == 1 and follow[0]:
                            normalise(*follow[0])
                        if j + 2 == k.nb and follow[0]:
                            split_low(*follow[0])
                        if j + 2 == k.nb and follow[1]:
                            if left == 1:
                                dve.wait_ge(s["resid"], k["resid"] + 1)
                            statistics(*follow[1])
                    dve.wait_ge(s["down_done"], k["down_done"] + (g + 1) * k.nb)
                    if k.layer == 1:
                        dve.wait_ge(s["bias_added"], k["bias_added"] + g + 1)
                    add_to_x(g, sc[:, 1:2] if k.layer == 0 else 0.5)

                dve.wait_ge(s["resid"], k["resid"])
                first_group(k)
                statistics(k, 1)
                with dve.Fori(0, GROUPS - 2) as g:
                    group(g, 2)
                group(GROUPS - 2, 1)
                group(GROUPS - 1, 0)

            def qkv(k):
                a = k.att

                def low(dst, o, at, row, heads, part):
                    return nc.vector.scalar_tensor_tensor(
                        out=view(dst, at + part * a.hd, (row, heads), (1, a.hd)),
                        in0=view(C, o, (a.hd, heads), (1, a.hd)), scalar=1 / WSCALE,
                        in1=view(dst, at, (row, heads), (1, a.hd)), op0=ALU.mult, op1=ALU.subtract)

                def group(g, par, left):
                    for t in range(GT):
                        dve.wait_ge(s["hi_ready"], k["hi_ready"] + g * GT + t + 1)
                        o, at = t % 2 * 2 * BANK, a.at(g, t)
                        low(QA, o, at, a.step, a.heads, 1)
                        op = low(KA, o + D, at, a.step * (HPG // a.vh), a.kv, 2)
                        if k.layer == 0:
                            v_at = a.v_at(g, t)
                            op = nc.vector.scalar_tensor_tensor(
                                out=view16(VS, v_at + a.hd, (4 * a.hd, a.kv), (1, a.hd)),
                                in0=view(C, o + 2 * D, (a.hd, a.kv), (1, a.hd)), scalar=1 / WSCALE,
                                in1=view16(VS, v_at, (4 * a.hd, a.kv), (1, a.hd)), op0=ALU.mult, op1=ALU.subtract)
                        op.then_inc(s["qkv_free"], 1)
                        if t == 0 and left:
                            normalise(k, g + 1)
                        if t == 2 and left:
                            split_low(k, g + 1, 1 - par)
                        if t == 2 and left > 1:
                            statistics(k, g + 2)

                dve.wait_ge(s["resid"], k["resid"])
                first_group(k)
                statistics(k, 1)
                with dve.Fori(0, GROUPS // 2 - 1) as n:
                    g = dve.snap(n * 2)
                    group(g, 0, 2)
                    group(g + 1, 1, 2)
                group(GROUPS - 2, 0, 1)
                group(GROUPS - 1, 1, 0)

            def att(k):
                a = k.att
                nmax = len(a.maxes)

                def place(i, of_batch, of_group):
                    b = i // a.groups
                    at = b * of_batch + (i % a.groups) * of_group
                    return at if isinstance(at, int) else dve.snap(at)

                def maximum(i, m, full, dst):
                    qt, heads = a.maxes[m]
                    dve.wait_ge(s["slot_full"], full)
                    src = view(dst, 0, (a.width(qt), len(heads)), (1, a.keys(qt)))
                    c = qt * HPG + heads[0]
                    nc.vector.tensor_reduce(NM[:, c:c + len(heads)], src, AX_X, ALU.max,
                                            negate=True).then_inc(s["maxed"], 1)

                def copy_q(i, n):
                    dve.wait_ge(s["slot_full"], k["slot_full"] + a.full(i, n))
                    nc.vector.tensor_copy(QT1[:, 0:SEQ], slot(i, n)[:, :].bitcast(F16)[:, 0:SEQ])\
                        .then_inc(s["q_copied"], 1)

                def copy_k(i, n, par):
                    dve.wait_ge(s["slot_full"], k["slot_full"] + a.full(i, n))
                    for h in range(HPG):
                        op = nc.vector.tensor_copy(KT[par][h * a.row:(h + 1) * a.row, h * SEQ:(h + 1) * SEQ],
                                                   slot(i, n)[0:a.row, :].bitcast(F16)[:, 0:SEQ])
                    op.then_inc(s["k_copied"], 1)

                def maxima(i, at, n0):
                    dve.wait_ge(s["m_written"], k["m_written"] + i)
                    for m in range(nmax):
                        maximum(i, m, k["slot_full"] + a.full(at, n0 + m), slot(at, n0 + m))
                    at = place(i, ST_ * 1024, a.qkw)
                    dve.wait_ge(s["maxed"], k["maxed"] + (i + 1) * nmax)
                    nm = view(NM, 0, (HPG, ST_), (1, HPG))
                    mh = view(QA, at + 3 * a.hd, (1024, ST_), (a.row, HPG))
                    nc.vector.tensor_copy(mh, nm).then_inc(s["mh_done"], 1)
                    dve.wait_ge(s["mh_done"], k["mh_done"] + i + 1)
                    nc.vector.tensor_tensor(view(QA, at + (3 * a.hd + 1), (1024, ST_), (a.row, HPG)), nm, mh,
                                            ALU.subtract).then_inc(s["m_written"], 1)

                def divide(i, n):
                    dve.wait_ge(s["slot_full"], k["slot_full"] + a.full(i, n))
                    dve.wait_ge(s["ao_ready"], k["ao_ready"] + i)
                    src = slot(i, n)
                    nc.vector.reciprocal(view(RD, 0, (HPG, ST_), (1, HPG)),
                                         view(src, a.hd, (P, ST_), (32, HPG))).then_inc(s["rd_done"], 1)
                    dve.wait_ge(s["rd_done"], k["rd_done"] + i + 1)
                    nc.vector.tensor_tensor(view(ON, 0, (HPG * a.hd, ST_), (a.hd, HPG), (1, a.hd)),
                                            view(src, 0, (P, ST_), (32, HPG), (1, a.hd)),
                                            view(RD, 0, (HPG, ST_), (1, HPG), (0, a.hd)),
                                            ALU.mult).then_inc(s["on_ready"], 1)

                def half(i, par, ahead):
                    if ahead:
                        maxima(i + 1, i, 0)
                    if ahead > 1:
                        copy_q(i, a.q_use)
                        copy_k(i, a.k_use, par)
                    divide(i, a.out_use(ahead))

                copy_q(None, 0)
                copy_k(None, 1, 0)
                maxima(0, None, 2)
                copy_q(None, a.lead - 2)
                copy_k(None, a.lead - 1, 1)
                with dve.Fori(0, a.iters // 2 - 1) as r:
                    i = dve.snap(r * 2)
                    half(i, 0, 2)
                    half(i + 1, 1, 2)
                half(a.iters - 2, 0, 1)
                half(a.iters - 1, 1, 0)

            def mix(k):
                def turned(dst, rows):
                    return nc.vector.tensor_copy(by_block(dst, 1), by_head(A, rows, 1))

                def a_filled(w, use):
                    dve.wait_ge(s["a_full"], k["a_full"] + w * 8 + 2 * use + 2)

                def turned_q(w, par):
                    a_filled(w, 0)
                    turned(QT2[par][:, :], slice(0, P)).then_inc(s["a1_read"], 1)

                def turned_k(w, par):
                    a_filled(w, 1)
                    for u in range(2):
                        rows = slice(64 * u, 64 * u + 64)
                        op = turned(KT[par][rows, u * BLOCKS * P:(u + 1) * BLOCKS * P], rows)
                    op.then_inc(s["a1_read"], 1)

                def turned_v(w):
                    a_filled(w, 2)
                    turned(QT1[0:64, :], slice(0, 64)).then_inc(s["a1_read"], 1)

                def blocks_v(w, par):
                    a_filled(w, 3)
                    nc.vector.tensor_copy(view(VG[par], 32 * BLOCKS, (32, BLOCKS), (1, HD0)),
                                          view(A, BANK, (HD0, BLOCKS), (1, HD0))).then_inc(s["a1_read"], 1)

                def maximum(w, c):
                    dve.wait_ge(s["b_full"], k["b_full"] + w * (CHUNKS + 1) + c + 1)
                    nc.vector.tensor_reduce(NM[:, c * CHUNK:(c + 1) * CHUNK],
                                            view(B, c % 2 * BANK, (P, CHUNK), (1, P)), AX_X, ALU.max,
                                            negate=True).then_inc(s["maxed"], 1)

                def turned_m(w, par):
                    dve.wait_ge(s["b_full"], k["b_full"] + (w + 1) * (CHUNKS + 1))
                    nc.vector.tensor_copy(MT[par][0:2 * BLOCKS, :], B[0:2 * BLOCKS, 0:P]).then_inc(s["m_ready"], 1)

                def divide(w, u):
                    dve.wait_ge(s["ot_full"], k["ot_full"] + w * 2 + u + 1)
                    nc.vector.reciprocal(RD[:, u * BLOCKS:(u + 1) * BLOCKS], view(C, 3 * BANK + HD0, (32, BLOCKS)))\
                        .then_inc(s["rd_done"], 1)
                    dve.wait_ge(s["rd_done"], k["rd_done"] + w * 2 + u + 1)
                    nc.vector.tensor_tensor(view(ON, u * D, (HD0, BLOCKS), (1, HD0)),
                                            view(C, 3 * BANK, (32, BLOCKS), (1, HD0)),
                                            view(RD, u * BLOCKS, (1, BLOCKS), (0, HD0)),
                                            ALU.mult).then_inc(s["on_ready"], 1)

                def low(w, u):
                    dve.wait_ge(s["oh_ready"], k["oh_ready"] + w * 2 + u + 1)
                    t = w * 2 + u
                    at = (t // ST_) * SEQ + (t % ST_) * NEAR
                    for c in range(DC):
                        op = nc.vector.tensor_tensor(view(AL, at + c * TOK, (SEQ // HEADS0, HEADS0), (1, NEAR)),
                                                     view(C, 3 * BANK + c * P, (NEAR, HEADS0), (1, NEAR)),
                                                     view(AH, at + c * TOK, (SEQ // HEADS0, HEADS0), (1, NEAR)),
                                                     ALU.subtract)
                    op.then_inc(s["ol_ready"], 1)

                def half(w, par, ahead):
                    def maxima(*cs):
                        for c in cs:
                            if ahead:
                                maximum(w + 1, c)

                    if ahead:
                        turned_v(w + 1)
                    maxima(0, 1)
                    if ahead:
                        blocks_v(w + 1, 1 - par)
                    maxima(2, 3)
                    divide(w, 0)
                    maxima(4)
                    low(w, 0)
                    if ahead > 1:
                        turned_q(w + 2, par)
                    maxima(5, 6, 7)
                    if ahead:
                        turned_m(w + 1, 1 - par)
                    divide(w, 1)
                    if ahead > 1:
                        turned_k(w + 2, par)
                    low(w, 1)

                dve.wait_ge(v_pad, 4)
                turned_q(0, 0)
                turned_k(0, 0)
                for c in range(CHUNKS):
                    maximum(0, c)
                    if c == 1:
                        turned_v(0)
                    if c == 3:
                        blocks_v(0, 0)
                    if c == 5:
                        turned_q(1, 1)
                    if c == 6:
                        turned_k(1, 1)
                turned_m(0, 0)
                with dve.Fori(0, MIXES // 2 - 1) as r:
                    w = dve.snap(r * 2)
                    half(w, 0, 2)
                    half(w + 1, 1, 2)
                half(MIXES - 2, 0, 1)
                half(MIXES - 1, 1, 0)

            def outward(k):
                def group(g, par):
                    dve.wait_ge(s["y_ready"], k["y_ready"] + g + 1)
                    add_to_x(g, 1 / WSCALE, outs[par])

                with dve.Fori(0, GROUPS // 2 - 1) as n:
                    g = dve.snap(n * 2)
                    group(g, 0)
                    group(g + 1, 1)
                dve.wait_ge(s["resid"], k["resid"] + 1)
                statistics(k.next, 0)
                group(GROUPS - 2, 0)
                normalise(k.next, 0)
                split_low(k.next, 0)
                group(GROUPS - 1, 1)

            def proj(k):
                def copy_low(g, par):
                    dve.wait_ge(s["at_ready"], k["at_ready"] + g * 2 + 2)
                    nc.vector.tensor_copy(XHL[par][1], A[:, BANK:2 * BANK].bitcast(F16)).then_inc(s["al_copied"], 1)

                def group(g, par, left):
                    if left:
                        copy_low(g + 1, 1 - par)
                    else:
                        split_low(k.next, 0)
                    dve.wait_ge(s["y_ready"], k["y_ready"] + g + 1)
                    add_to_x(g, 1 / WSCALE, outs[par])

                copy_low(0, 0)
                with dve.Fori(0, GROUPS // 2 - 1) as n:
                    g = dve.snap(n * 2)
                    group(g, 0, 2)
                    group(g + 1, 1, 2)
                dve.wait_ge(s["resid"], k["resid"] + 1)
                statistics(k.next, 0)
                group(GROUPS - 2, 0, 1)
                normalise(k.next, 0)
                group(GROUPS - 1, 1, 0)

            steps = [0]

            def step(op):
                steps[0] += 1
                op.then_inc(setup_step, 1)
                dve.wait_ge(setup_step, steps[0])

            dve.wait_ge(x0_in, 16)
            statistics(phases[0], 0)
            normalise(phases[0], 0)
            dve.wait_ge(ffn_w_in, 16 * 2)
            for n, (_, src, _) in enumerate(quant):
                if n == 2:
                    split_low(phases[0], 0)
                    dve.wait_ge(ffn1_w_in, 16 * 2)
                op = nc.vector.tensor_reduce(sums[:, n:n + 1], src, AX_X, ALU.add, apply_absolute_value=True)
            op.then_inc(sums_ready, 1)
            dve.wait_ge(tot_ready, 1)
            for k, (floor, cut) in enumerate(((1e-5, 0.7), (1e-8, 0.5))):
                c = slice(2 * k, 2 * k + 2)
                size = float(D * HID[k])
                step(nc.vector.tensor_scalar(means[:, c], C[:, c], 1 / size, floor, ALU.mult, ALU.max))
                nc.vector.tensor_scalar(lim[:, c], means[:, c], cut, None, ALU.mult)
                step(nc.vector.tensor_scalar(lim[:, 4 + 2 * k:6 + 2 * k], means[:, c], -cut, None, ALU.mult))
            step(nc.vector.tensor_tensor(sc[:, 0:1], means[:, 0:1], means[:, 0:1], ALU.mult))
            step(nc.vector.tensor_scalar(sc[:, 1:2], sc[:, 0:1], means[:, 1:2], 0.5 / RSCALE ** 2, ALU.mult, ALU.mult))
            for n, (w, src, dst) in enumerate(quant[:2]):
                step(nc.vector.tensor_scalar(dst[:, :], src, lim[:, 4 + n:5 + n], None, ALU.is_lt))
                nc.vector.scalar_tensor_tensor(out=dst[:, :], in0=src, scalar=lim[:, n:n + 1], in1=dst[:, :],
                                               op0=ALU.is_gt, op1=ALU.subtract).then_inc(up_down_ready, 1)
            dve.wait_ge(up_down_ready, 2)
            dve.sem_inc(w_ready, 1)
            for n, (_, src, dst) in enumerate(split):
                dve.wait_ge(high_done, n + 1)
                nc.vector.scalar_tensor_tensor(out=dst[1][:, :], in0=src, scalar=WSCALE, in1=dst[0][:, :],
                                               op0=ALU.mult, op1=ALU.subtract)
            nc.vector.tensor_scalar(b2h[:, :], b2h[:, :], 0.5, None, ALU.mult).then_inc(w_ready, 1)
            dve.wait_ge(x_in, 16 * (GROUPS - 1))
            for k in phases:
                {"ffn": ffn, "qkv": qkv, "mix": mix, "out": outward, "att": att, "proj": proj}[k.kind](k)

        @block.gpsimd
        def _(pool):
            def rsqrt(k, g):
                pool.wait_ge(s["var_ready"], k["var_ready"] + g + 1)
                nc.gpsimd.tensor_tensor(var[:, :], view(mv, 1, (2, GT)), eps[:, :], ALU.add).then_inc(s["eps_done"], 1)
                pool.wait_ge(s["eps_done"], k["eps_done"] + g + 1)
                nc.gpsimd.tensor_tensor(rstd[:, :], var[:, :], mhalf[:, :], ALU.pow).then_inc(s["rstd_ready"], 1)

            def ternary(n):
                _, src, dst = quant[n]
                nc.gpsimd.tensor_scalar(dst[:, :], src, lim[:, 4 + n:5 + n], None, ALU.is_lt)\
                    .then_inc(ternary_step, 1)
                pool.wait_ge(ternary_step, 2 * n - 3)
                nc.gpsimd.tensor_scalar(src, src, lim[:, n:n + 1], None, ALU.is_gt).then_inc(ternary_step, 1)
                pool.wait_ge(ternary_step, 2 * n - 2)
                nc.gpsimd.tensor_tensor(dst[:, :], src, dst[:, :], ALU.subtract).then_inc(ternary_1, 1)

            def ffn(k):
                def group(g, last):
                    if k.layer == 1:
                        pool.wait_ge(s["xn_ready"], k["xn_ready"] + g + 1)
                        xs = view(X, g * (GT * D), (D, GT), (1, D))
                        nc.gpsimd.tensor_tensor(xs, xs, view(b2h, 0, (0, GT), (1, D)), ALU.add)\
                            .then_inc(s["bias_added"], 1)
                    if not last:
                        rsqrt(k, g + 1)
                    elif k.next:
                        rsqrt(k.next, 0)

                if not k.primed:
                    rsqrt(k, 0)
                if k.layer == 0:
                    for g in range(GROUPS - 1):
                        rsqrt(k, g + 1)
                        if k is phases[0]:
                            [apart_rows, lambda: ternary(2), lambda: ternary(3)][g]()
                        else:
                            pads_1(g)
                    rsqrt(k.next, 0)
                    return
                with pool.Fori(0, GROUPS - 1) as g:
                    group(g, False)
                group(GROUPS - 1, True)

            def qkv(k):
                a = k.att
                row = a.step * (HPG // a.vh)

                def group(g, left):
                    for t in range(GT):
                        if t == GT - 1 and left > 1:
                            rsqrt(k, g + 2)
                        pool.wait_ge(s["qkv_free"], k["qkv_free"] + g * GT + t + 1)
                        at = a.at(g, t)
                        nc.gpsimd.tensor_copy(view(QA, at + 2 * a.hd, (a.step, a.heads), (1, a.hd)),
                                              view(QA, at, (a.step, a.heads), (1, a.hd)))
                        op = nc.gpsimd.tensor_copy(view(KA, at + a.hd, (row, a.kv), (1, a.hd)),
                                                   view(KA, at, (row, a.kv), (1, a.hd)))
                        op.then_inc(s["dup_done"], 1)

                if not k.primed:
                    rsqrt(k, 0)
                rsqrt(k, 1)
                with pool.Fori(0, GROUPS - 2) as g:
                    group(g, 2)
                group(GROUPS - 2, 1)
                group(GROUPS - 1, 0)

            def att(k):
                a = k.att
                nset = len(a.sets)

                def place(i, of_batch, of_group):
                    b = i // a.groups
                    at = b * of_batch + (i % a.groups) * of_group
                    return at if isinstance(at, int) else pool.snap(at)

                def group_v(i, par):
                    if not (isinstance(i, int) and i == 0):
                        pool.wait_ge(s["pv_done"], k["pv_done"] + (i - 1) * nset)
                    at = place(i, ST_ * a.kvw, a.vh * a.hd)
                    nc.gpsimd.tensor_copy(view(VG[par], 0, (a.vh * 32, ST_), (32, a.vh), (1, a.hd)),
                                          view(VS, at, (a.kvw, ST_), (a.hd, a.vh), (1, a.hd))).then_inc(s["v_ready"], 1)

                def half(i, par, more):
                    if more:
                        group_v(i + 1, 1 - par)
                    pool.wait_ge(s["on_ready"], k["on_ready"] + i + 1)
                    at = place(i, ST_ * D, HPG * a.hd)
                    w = HPG * a.hd
                    nc.gpsimd.tensor_copy(view(AH, at, (D, ST_), (1, w)), view(ON, 0, (w, ST_), (1, w)))\
                        .then_inc(s["ah_done"], 1)
                    pool.wait_ge(s["ah_done"], k["ah_done"] + i + 1)
                    nc.gpsimd.tensor_tensor(view(AL, at, (D, ST_), (1, w)), view(ON, 0, (w, ST_), (1, w)),
                                            view(AH, at, (D, ST_), (1, w)), ALU.subtract).then_inc(s["ao_ready"], 1)

                pool.wait_ge(s["hi_ready"], k["hi_ready"])
                ones_of_v(1)
                group_v(0, 0)
                with pool.Fori(0, a.iters // 2 - 1) as r:
                    i = pool.snap(r * 2)
                    half(i, 0, True)
                    half(i + 1, 1, True)
                half(a.iters - 2, 0, True)
                half(a.iters - 1, 1, False)

            def mix(k):
                ones_of_v(0)

            def outward(k):
                rsqrt(k.next, 0)

            def ones_of_v(layer):
                a = ATTS[layer]
                for n in range(2):
                    nc.gpsimd.memset(VG[n][:, :], 0.0).then_inc(v_pad, 1)
                pool.wait_ge(v_pad, 4 * layer + 2)
                for n in range(2):
                    nc.gpsimd.memset(view(VG[n], a.hd, (32, ST_ * a.vh)), 1.0).then_inc(v_pad, 1)
                pool.wait_ge(v_pad, 4 * layer + 4)

            def zero(tensors, done):
                for t in tensors:
                    nc.gpsimd.memset(t[:, :].bitcast(F32), 0.0).then_inc(done, 1)

            def pads_1(part):
                if part == 0:
                    pool.wait_ge(s["ol_ready"], phases[3]["ol_ready"])
                    zero([QA], pad_zeroed)
                elif part == 1:
                    zero([KA], pad_zeroed)
                    zero(KT, k_zeroed)
                else:
                    pool.wait_ge(pad_zeroed, 4)
                    pool.wait_ge(k_zeroed, 6)
                    nc.gpsimd.memset(view(KA, 3 * ATTS[1].hd, (32, NT * 32), (1, 2)), 1.0).then_inc(pad_ready, 1)

            def apart_rows():
                a = ATTS[0]
                pool.wait_ge(w_in, 16 * 7)
                for n, t in enumerate((QA, KA)):
                    op = nc.gpsimd.tensor_copy(view(t, 3 * a.hd, (a.row, NT * a.heads), (1, NEAR)),
                                               view(aparts, n * NEAR, (0, NT * a.heads), (1, NEAR)))
                op.then_inc(pad_ready, 1)

            def proj(k):
                rsqrt(k.next, 0)

            for name, counter in s.items():
                pool.sem_inc(counter, CREDIT.get(name, 1))
            for n, t in enumerate((ident, ident16, identb, maskb, maskt)):
                nc.gpsimd.memset(t[:, :], 0.0).then_inc(const_step, 1)
            pool.wait_ge(const_step, 5)
            for t in (ident, ident16, identb):
                nc.gpsimd.affine_select(out=t[:, :], in_=t[:, :], compare_op=ALU.not_equal, fill=1.0, base=0,
                                        pattern=[[-1, P]], channel_multiplier=1).then_inc(const_ready, 1)
            for t, sign in ((maskb, 1), (maskt, -1)):
                nc.gpsimd.affine_select(out=t[:, :], in_=t[:, :], compare_op=ALU.is_ge, fill=NEG, base=0,
                                        pattern=[[-sign, P]], channel_multiplier=sign).then_inc(const_ready, 1)
            nc.gpsimd.memset(ones[:, :], 1.0).then_inc(const_ready, 1)
            nc.gpsimd.memset(two[:, :], 0.0).then_inc(const_step, 1)
            for n in range(4):
                pool.wait_ge(const_step, 6 + n)
                nc.gpsimd.affine_select(out=two[:, :], in_=two[:, :], compare_op=ALU.not_equal, fill=1.0,
                                        base=-n * HD0, pattern=[[-1, HD0]], channel_multiplier=1)\
                    .then_inc(const_step, 1)
            pool.wait_ge(const_step, 10)
            nc.gpsimd.memset(mhalf[:, :], -0.5).then_inc(const_ready, 1)
            nc.gpsimd.memset(eps[:, :], EPS).then_inc(const_ready, 1)
            pool.wait_ge(const_ready, 8)
            nc.gpsimd.memset(VS[:, NT * D:], 0.0).then_inc(pad_ready, 1)
            rsqrt(phases[0], 0)
            zero([QA, KA], pad_zeroed)
            zero(KT, k_zeroed)
            for t in MT:
                nc.gpsimd.memset(t[:, :], 0.0).then_inc(k_zeroed, 1)
            pool.wait_ge(pad_zeroed, 2)
            pool.wait_ge(k_zeroed, 4)
            for k in phases:
                {"ffn": ffn, "qkv": qkv, "mix": mix, "out": outward, "att": att, "proj": proj}[k.kind](k)


def kernel(L0_attn_x, L0_attn_w_qkv, L0_attn_w_proj, L0_ffn_w_fc, L0_ffn_w_proj, L1_attn_wq, L1_attn_wk,
           L1_attn_wv, L1_attn_wo, L1_ffn_w1, L1_ffn_b1, L1_ffn_w2, L1_ffn_b2):
    import numpy as np
    import concourse.bacc as bacc
    from concourse.bass_utils import run_bass_kernel_spmd

    shape = L0_attn_x.shape
    near = BIG * (np.arange(P)[:, None] // BLOCKS == np.arange(NEAR)[None, :])
    arrays = {
        "x": np.asarray(L0_attn_x).reshape(TOK, D),
        "fc0": np.asarray(L0_ffn_w_fc).T, "down0": np.asarray(L0_ffn_w_proj).T,
        "fc1": np.asarray(L1_ffn_w1).T, "down1": np.asarray(L1_ffn_w2).T,
        "apart": np.concatenate([near, near - BIG], axis=1).astype(np.float32),
        "b1": np.asarray(L1_ffn_b1).reshape(-1, P).T, "b2": np.asarray(L1_ffn_b2).reshape(1, D),
        "qkv0": np.asarray(L0_attn_w_qkv).T, "wo0": np.asarray(L0_attn_w_proj).T,
        "qkv1": np.concatenate([np.asarray(w) for w in (L1_attn_wq, L1_attn_wk, L1_attn_wv)], axis=1),
        "wo1": np.asarray(L1_attn_wo),
    }
    arrays = {name: np.ascontiguousarray(a) for name, a in arrays.items()}
    nc = bacc.Bacc("TRN2", target_bir_lowering=False, num_devices=1)
    args = [nc.dram_tensor(name, a.shape, F32, kind="ExternalInput").ap() for name, a in arrays.items()]
    out = nc.dram_tensor("out", [TOK, D], F32, kind="ExternalOutput").ap()
    macaron_kernel(nc, out=out, **dict(zip(arrays, args)))
    r = run_bass_kernel_spmd(nc, [arrays], core_ids=[0])
    return r.results[0]["out"].reshape(shape)
```
